# Optimizing a Trainium2 kernel written in Bass

```python
import numpy as np
import jax
import jax.numpy as jnp

def _softmax(x, axis=-1):
    return jax.nn.softmax(x, axis=axis)

def _gelu(x):
    return jax.nn.gelu(x, approximate=True)

def _silu(x):
    return jax.nn.silu(x)

def _sigmoid(x):
    return jax.nn.sigmoid(x)

def _layernorm(x, axis=-1, eps=1e-05):
    m = jnp.mean(x, axis=axis, keepdims=True)
    v = jnp.var(x, axis=axis, keepdims=True)
    return (x - m) / jnp.sqrt(v + eps)

def _scatter_add(tgt, idx, src, axis=0):
    return tgt.at[idx].add(src)

def _segment_sum(src, seg, n):
    return jax.ops.segment_sum(src, seg, n)
kernel_name = 'mk_pixart_resid_d2_seqx_r8_91965e'

def setup_inputs(seed: int=0):
    np.random.seed(seed)
    _w = jnp.asarray

    def _rec_inputs():
        import jax
        import jax.numpy as jnp
        _rk = jax.random.key(seed)
        x = -0.0002928 + 1 * jax.random.normal(jax.random.fold_in(_rk, 1), (4, 512, 128), jnp.float32)
        _lenS = 512 - jax.random.randint(jax.random.fold_in(_rk, 7), (4,), 0, max(1, 512 // 4) + 1, jnp.int32)
        _lenS2 = 77 - jax.random.randint(jax.random.fold_in(_rk, 8), (4,), 0, max(1, 77 // 4) + 1, jnp.int32)
        cond_1024 = 0.000887014 + 1.03683 * jax.random.normal(jax.random.fold_in(_rk, 11), (4, 128), jnp.float32)
        _ctx_1024P = jax.random.normal(jax.random.fold_in(_rk, 12), (4, 16, 128), jnp.float32)
        _ctx_1024c = jax.random.dirichlet(jax.random.fold_in(_rk, 512), 0.3 * jnp.ones((16,), jnp.float32), (4, 77))
        _ctx_1024t = jnp.einsum('bsk,bkd->bsd', _ctx_1024c, _ctx_1024P)
        _ctx_1024t = _ctx_1024t * jax.lax.rsqrt(jnp.mean(jnp.square(_ctx_1024t)) + 1e-12) * 0.953939
        ctx_1024 = -0.000761806 + 0.999296 * (_ctx_1024t + 0.3 * jax.random.normal(jax.random.fold_in(_rk, 612), (4, 77, 128), jnp.float32))
        return (x, cond_1024, ctx_1024)
    x, cond_1024, ctx_1024 = _rec_inputs()

    def _L0_xcond_setup():
        import jax, jax.numpy as jnp
        import numpy as np
        import math
        B, S, CTX, D, H, DH = (2, 256, 32, 128, 16, 64)
        INNER = H * DH
        DFF = 4 * D

        def layernorm(x, eps=1e-05):
            m = jnp.mean(x, axis=-1, keepdims=True)
            v = jnp.var(x, axis=-1, keepdims=True)
            return (x - m) * jax.lax.rsqrt(v + eps)

        def adaln(x, t, w, b):
            emb = t @ w + b
            scale, shift = jnp.split(emb, 2, axis=-1)
            return layernorm(x) * (1.0 + scale) + shift

        def mha(xq, ctx, wq, wk, wv, wo, bo):
            b, sq, _ = xq.shape
            sk = ctx.shape[1]
            q = (xq @ wq).reshape(b, sq, H, DH).transpose(0, 2, 1, 3)
            k = (ctx @ wk).reshape(b, sk, H, DH).transpose(0, 2, 1, 3)
            v = (ctx @ wv).reshape(b, sk, H, DH).transpose(0, 2, 1, 3)
            scores = jnp.einsum('bhqd,bhkd->bhqk', q, k) / math.sqrt(DH)
            attn = jax.nn.softmax(scores, axis=-1)
            out = jnp.einsum('bhqk,bhkd->bhqd', attn, v)
            out = out.transpose(0, 2, 1, 3).reshape(b, sq, INNER)
            return out @ wo + bo

        def glu_ff(x, w1, b1, w2, b2):
            u = x @ w1 + b1
            a, gate = jnp.split(u, 2, axis=-1)
            return a * jax.nn.gelu(gate, approximate=False) @ w2 + b2
        key = jax.random.key(seed)
        ks = jax.random.split(key, 24)
        s = 1.0 / math.sqrt(D)

        def n(k, shape, scale=1.0):
            return jax.random.normal(k, shape, dtype=jnp.float32) * scale
        return {'x': n(ks[0], (B, S, D)), 't': n(ks[1], (B, 1, D)), 'context': n(ks[2], (B, CTX, D)), 'attn1_wq': n(ks[3], (D, INNER), s), 'attn1_wk': n(ks[4], (D, INNER), s), 'attn1_wv': n(ks[5], (D, INNER), s), 'attn1_wo': n(ks[6], (INNER, D), s), 'attn1_bo': n(ks[7], (D,), 0.01), 'attn2_wq': n(ks[8], (D, INNER), s), 'attn2_wk': n(ks[9], (D, INNER), s), 'attn2_wv': n(ks[10], (D, INNER), s), 'attn2_wo': n(ks[11], (INNER, D), s), 'attn2_bo': n(ks[12], (D,), 0.01), 'ff_w1': n(ks[13], (D, 2 * DFF), s), 'ff_b1': n(ks[14], (2 * DFF,), 0.01), 'ff_w2': n(ks[15], (DFF, D), 1.0 / math.sqrt(DFF)), 'ff_b2': n(ks[16], (D,), 0.01), 'norm1_w': n(ks[17], (D, 2 * D), s), 'norm1_b': n(ks[18], (2 * D,), 0.01), 'norm2_w': n(ks[19], (D, 2 * D), s), 'norm2_b': n(ks[20], (2 * D,), 0.01), 'norm3_w': n(ks[21], (D, 2 * D), s), 'norm3_b': n(ks[22], (2 * D,), 0.01)}
    _L0_xcond_all = _L0_xcond_setup()
    _L0_xcond_in = {k: v for k, v in _L0_xcond_all.items() if k in ('attn1_wq', 'attn1_wk', 'attn1_wv', 'attn1_wo', 'attn1_bo', 'attn2_wq', 'attn2_wk', 'attn2_wv', 'attn2_wo', 'attn2_bo', 'ff_w1', 'ff_b1', 'ff_w2', 'ff_b2', 'norm1_w', 'norm1_b', 'norm2_w', 'norm2_b', 'norm3_w', 'norm3_b')}
    del _L0_xcond_all

    def _L0_ffn_setup():
        import jax, jax.numpy as jnp
        import numpy as np
        QK_SCALE = 10.0
        NEG_INF = -1000000000.0

        def layernorm(x, g, b, eps=1e-05):
            mu = jnp.mean(x, axis=-1, keepdims=True)
            var = jnp.var(x, axis=-1, keepdims=True)
            return (x - mu) * jax.lax.rsqrt(var + eps) * g + b

        def l2norm(x, eps=1e-12):
            return x / jnp.sqrt(jnp.sum(x * x, axis=-1, keepdims=True) + eps)
        key = jax.random.key(seed)
        ks = jax.random.split(key, 10)
        B, S, D, H, DH, E, FF = (2, 128, 128, 16, 64, 8, 512)
        sd = lambda fan: 1.0 / np.sqrt(fan)
        return {'x': jax.random.normal(ks[0], (B, S, D), jnp.float32), 'ln_g': jnp.ones((D,), jnp.float32), 'ln_b': jnp.zeros((D,), jnp.float32), 'Wq': jax.random.normal(ks[1], (D, H * DH), jnp.float32) * sd(D), 'Wk': jax.random.normal(ks[2], (D, H * DH), jnp.float32) * sd(D), 'Wv': jax.random.normal(ks[3], (D, H * DH), jnp.float32) * sd(D), 'q_scale': jnp.ones((H, 1, DH), jnp.float32), 'k_scale': jnp.ones((H, 1, DH), jnp.float32), 'Wo': jax.random.normal(ks[4], (H * DH, D), jnp.float32) * sd(H * DH), 'gate_w': jax.random.normal(ks[5], (D, E), jnp.float32) * sd(D), 'gate_b': jnp.zeros((E,), jnp.float32), 'w1': jax.random.normal(ks[6], (E, D, FF), jnp.float32) * sd(D), 'b1': jnp.zeros((E, FF), jnp.float32), 'w2': jax.random.normal(ks[7], (E, FF, D), jnp.float32) * sd(FF), 'b2': jnp.zeros((E, D), jnp.float32)}
    _L0_ffn_all = _L0_ffn_setup()
    _L0_ffn_in = {k: v for k, v in _L0_ffn_all.items() if k in ('ln_g', 'ln_b', 'Wq', 'Wk', 'Wv', 'q_scale', 'k_scale', 'Wo', 'gate_w', 'gate_b', 'w1', 'b1', 'w2', 'b2')}
    del _L0_ffn_all

    def _L1_xcond_setup():
        import jax, jax.numpy as jnp
        import numpy as np
        B, T, S, H, E = (32, 64, 64, 128, 128)
        key = jax.random.key(seed)
        ks = jax.random.split(key, 7)
        sc = 0.02
        return {'dec_seq': jax.random.normal(ks[0], (B, T, E), jnp.float32), 'enc_hiddens': jax.random.normal(ks[1], (B, S, H), jnp.float32), 'last_hidden': jax.random.normal(ks[2], (B, H), jnp.float32), 'W': jax.random.normal(ks[3], (H, H), jnp.float32) * sc, 'kernel': jax.random.normal(ks[4], (E + H, 3 * H), jnp.float32) * sc, 'recurrent_kernel': jax.random.normal(ks[5], (H, 3 * H), jnp.float32) * sc, 'bias': jnp.zeros((3 * H,), jnp.float32)}
    _L1_xcond_all = _L1_xcond_setup()
    _L1_xcond_in = {k: v for k, v in _L1_xcond_all.items() if k in ('W', 'kernel', 'recurrent_kernel', 'bias')}
    del _L1_xcond_all

    def _L1_ffn_setup():
        import jax, jax.numpy as jnp
        import numpy as np
        NUM_EXPERTS = 8
        EXPERT_CAPACITY = 2.0
        DIM = 128
        HIDDEN_DIM = 512
        key = jax.random.key(seed)
        k_x, k_g, k_w1, k_w2 = jax.random.split(key, 4)
        n, t, d, f, e = (8, 128, DIM, HIDDEN_DIM, NUM_EXPERTS)
        x = jax.random.normal(k_x, (n, t, d), dtype=jnp.float32)
        gate_w = jax.random.normal(k_g, (e, d), dtype=jnp.float32) * 0.02
        w1 = jax.random.normal(k_w1, (e, d, f), dtype=jnp.float32) * 0.02
        w2 = jax.random.normal(k_w2, (e, f, d), dtype=jnp.float32) * 0.02
        return {'x': x, 'gate_w': gate_w, 'w1': w1, 'w2': w2}
    _L1_ffn_all = _L1_ffn_setup()
    _L1_ffn_in = {k: v for k, v in _L1_ffn_all.items() if k in ('gate_w', 'w1', 'w2')}
    del _L1_ffn_all
    return {'x': x, 'cond_1024': cond_1024, 'ctx_1024': ctx_1024, 'L0_xcond_attn1_wq': _L0_xcond_in['attn1_wq'], 'L0_xcond_attn1_wk': _L0_xcond_in['attn1_wk'], 'L0_xcond_attn1_wv': _L0_xcond_in['attn1_wv'], 'L0_xcond_attn1_wo': _L0_xcond_in['attn1_wo'], 'L0_xcond_attn1_bo': _L0_xcond_in['attn1_bo'], 'L0_xcond_attn2_wq': _L0_xcond_in['attn2_wq'], 'L0_xcond_attn2_wk': _L0_xcond_in['attn2_wk'], 'L0_xcond_attn2_wv': _L0_xcond_in['attn2_wv'], 'L0_xcond_attn2_wo': _L0_xcond_in['attn2_wo'], 'L0_xcond_attn2_bo': _L0_xcond_in['attn2_bo'], 'L0_xcond_ff_w1': _L0_xcond_in['ff_w1'], 'L0_xcond_ff_b1': _L0_xcond_in['ff_b1'], 'L0_xcond_ff_w2': _L0_xcond_in['ff_w2'], 'L0_xcond_ff_b2': _L0_xcond_in['ff_b2'], 'L0_xcond_norm1_w': _L0_xcond_in['norm1_w'], 'L0_xcond_norm1_b': _L0_xcond_in['norm1_b'], 'L0_xcond_norm2_w': _L0_xcond_in['norm2_w'], 'L0_xcond_norm2_b': _L0_xcond_in['norm2_b'], 'L0_xcond_norm3_w': _L0_xcond_in['norm3_w'], 'L0_xcond_norm3_b': _L0_xcond_in['norm3_b'], 'L0_ffn_ln_g': _L0_ffn_in['ln_g'], 'L0_ffn_ln_b': _L0_ffn_in['ln_b'], 'L0_ffn_Wq': _L0_ffn_in['Wq'], 'L0_ffn_Wk': _L0_ffn_in['Wk'], 'L0_ffn_Wv': _L0_ffn_in['Wv'], 'L0_ffn_q_scale': _L0_ffn_in['q_scale'], 'L0_ffn_k_scale': _L0_ffn_in['k_scale'], 'L0_ffn_Wo': _L0_ffn_in['Wo'], 'L0_ffn_gate_w': _L0_ffn_in['gate_w'], 'L0_ffn_gate_b': _L0_ffn_in['gate_b'], 'L0_ffn_w1': _L0_ffn_in['w1'], 'L0_ffn_b1': _L0_ffn_in['b1'], 'L0_ffn_w2': _L0_ffn_in['w2'], 'L0_ffn_b2': _L0_ffn_in['b2'], 'L1_xcond_W': _L1_xcond_in['W'], 'L1_xcond_kernel': _L1_xcond_in['kernel'], 'L1_xcond_recurrent_kernel': _L1_xcond_in['recurrent_kernel'], 'L1_xcond_bias': _L1_xcond_in['bias'], 'L1_ffn_gate_w': _L1_ffn_in['gate_w'], 'L1_ffn_w1': _L1_ffn_in['w1'], 'L1_ffn_w2': _L1_ffn_in['w2']}

def reference(x, cond_1024, ctx_1024, L0_xcond_attn1_wq, L0_xcond_attn1_wk, L0_xcond_attn1_wv, L0_xcond_attn1_wo, L0_xcond_attn1_bo, L0_xcond_attn2_wq, L0_xcond_attn2_wk, L0_xcond_attn2_wv, L0_xcond_attn2_wo, L0_xcond_attn2_bo, L0_xcond_ff_w1, L0_xcond_ff_b1, L0_xcond_ff_w2, L0_xcond_ff_b2, L0_xcond_norm1_w, L0_xcond_norm1_b, L0_xcond_norm2_w, L0_xcond_norm2_b, L0_xcond_norm3_w, L0_xcond_norm3_b, L0_ffn_ln_g, L0_ffn_ln_b, L0_ffn_Wq, L0_ffn_Wk, L0_ffn_Wv, L0_ffn_q_scale, L0_ffn_k_scale, L0_ffn_Wo, L0_ffn_gate_w, L0_ffn_gate_b, L0_ffn_w1, L0_ffn_b1, L0_ffn_w2, L0_ffn_b2, L1_xcond_W, L1_xcond_kernel, L1_xcond_recurrent_kernel, L1_xcond_bias, L1_ffn_gate_w, L1_ffn_w1, L1_ffn_w2):
    import jax
    import jax.numpy as jnp

    def _L0_xcond_ref(x, t, context, attn1_wq, attn1_wk, attn1_wv, attn1_wo, attn1_bo, attn2_wq, attn2_wk, attn2_wv, attn2_wo, attn2_bo, ff_w1, ff_b1, ff_w2, ff_b2, norm1_w, norm1_b, norm2_w, norm2_b, norm3_w, norm3_b):
        import jax, jax.numpy as jnp
        import numpy as np
        import math
        B, S, CTX, D, H, DH = (2, 256, 32, 128, 16, 64)
        INNER = H * DH
        DFF = 4 * D

        def layernorm(x, eps=1e-05):
            m = jnp.mean(x, axis=-1, keepdims=True)
            v = jnp.var(x, axis=-1, keepdims=True)
            return (x - m) * jax.lax.rsqrt(v + eps)

        def adaln(x, t, w, b):
            emb = t @ w + b
            scale, shift = jnp.split(emb, 2, axis=-1)
            return layernorm(x) * (1.0 + scale) + shift

        def mha(xq, ctx, wq, wk, wv, wo, bo):
            b, sq, _ = xq.shape
            sk = ctx.shape[1]
            q = (xq @ wq).reshape(b, sq, H, DH).transpose(0, 2, 1, 3)
            k = (ctx @ wk).reshape(b, sk, H, DH).transpose(0, 2, 1, 3)
            v = (ctx @ wv).reshape(b, sk, H, DH).transpose(0, 2, 1, 3)
            scores = jnp.einsum('bhqd,bhkd->bhqk', q, k) / math.sqrt(DH)
            attn = jax.nn.softmax(scores, axis=-1)
            out = jnp.einsum('bhqk,bhkd->bhqd', attn, v)
            out = out.transpose(0, 2, 1, 3).reshape(b, sq, INNER)
            return out @ wo + bo

        def glu_ff(x, w1, b1, w2, b2):
            u = x @ w1 + b1
            a, gate = jnp.split(u, 2, axis=-1)
            return a * jax.nn.gelu(gate, approximate=False) @ w2 + b2
        h1 = adaln(x, t, norm1_w, norm1_b)
        x = mha(h1, h1, attn1_wq, attn1_wk, attn1_wv, attn1_wo, attn1_bo) + x
        h2 = adaln(x, t, norm2_w, norm2_b)
        x = mha(h2, context, attn2_wq, attn2_wk, attn2_wv, attn2_wo, attn2_bo) + x
        h3 = adaln(x, t, norm3_w, norm3_b)
        x = glu_ff(h3, ff_w1, ff_b1, ff_w2, ff_b2) + x
        return x

    def _L0_ffn_ref(x, ln_g, ln_b, Wq, Wk, Wv, q_scale, k_scale, Wo, gate_w, gate_b, w1, b1, w2, b2):
        import jax, jax.numpy as jnp
        import numpy as np
        QK_SCALE = 10.0
        NEG_INF = -1000000000.0

        def layernorm(x, g, b, eps=1e-05):
            mu = jnp.mean(x, axis=-1, keepdims=True)
            var = jnp.var(x, axis=-1, keepdims=True)
            return (x - mu) * jax.lax.rsqrt(var + eps) * g + b

        def l2norm(x, eps=1e-12):
            return x / jnp.sqrt(jnp.sum(x * x, axis=-1, keepdims=True) + eps)
        B, S, D = x.shape
        H = q_scale.shape[0]
        DH = q_scale.shape[-1]
        h = layernorm(x, ln_g, ln_b)
        q = (h @ Wq).reshape(B, S, H, DH).transpose(0, 2, 1, 3)
        k = (h @ Wk).reshape(B, S, H, DH).transpose(0, 2, 1, 3)
        v = (h @ Wv).reshape(B, S, H, DH).transpose(0, 2, 1, 3)
        q = l2norm(q) * q_scale
        k = l2norm(k) * k_scale
        logits = jnp.einsum('bhid,bhjd->bhij', q, k) * QK_SCALE
        causal = jnp.tril(jnp.ones((S, S), bool))
        logits = jnp.where(causal, logits, NEG_INF)
        attn = jax.nn.softmax(logits, axis=-1)
        out = jnp.einsum('bhij,bhjd->bhid', attn, v)
        out = out.transpose(0, 2, 1, 3).reshape(B, S, H * DH) @ Wo
        h = layernorm(out, ln_g, ln_b)
        gate = jax.nn.softmax(h @ gate_w + gate_b, axis=-1)
        hid = jax.nn.gelu(jnp.einsum('bsd,edf->bsef', h, w1) + b1)
        exp_out = jnp.einsum('bsef,efd->bsed', hid, w2) + b2
        moe = jnp.einsum('bse,bsed->bsd', gate, exp_out)
        return layernorm(moe, ln_g, ln_b)

    def _L1_xcond_ref(dec_seq, enc_hiddens, last_hidden, W, kernel, recurrent_kernel, bias):
        import jax, jax.numpy as jnp
        import numpy as np
        B, T, S, H, E = (32, 64, 64, 128, 128)
        Hd = last_hidden.shape[-1]

        def step(h, x_t):
            proj = h @ W
            score = jnp.einsum('bsh,bh->bs', enc_hiddens, proj)
            attn = jax.nn.softmax(score, axis=-1)
            context = jnp.einsum('bs,bsh->bh', attn, enc_hiddens)
            inp = jnp.concatenate([x_t, context], axis=-1)
            gx = inp @ kernel + bias
            gh = h @ recurrent_kernel
            xz, xr, xh = (gx[:, :Hd], gx[:, Hd:2 * Hd], gx[:, 2 * Hd:])
            hz, hr, hh = (gh[:, :Hd], gh[:, Hd:2 * Hd], gh[:, 2 * Hd:])
            z = jax.nn.sigmoid(xz + hz)
            r = jax.nn.sigmoid(xr + hr)
            cand = jnp.tanh(xh + r * hh)
            h_new = z * h + (1.0 - z) * cand
            return (h_new, h_new)
        xs = jnp.swapaxes(dec_seq, 0, 1)
        _, outs = jax.lax.scan(step, last_hidden, xs)
        return jnp.swapaxes(outs, 0, 1)

    def _L1_ffn_ref(x, gate_w, w1, w2):
        import jax, jax.numpy as jnp
        import numpy as np
        NUM_EXPERTS = 8
        EXPERT_CAPACITY = 2.0
        DIM = 128
        HIDDEN_DIM = 512
        n, t, d = x.shape
        e = gate_w.shape[0]
        k = int(EXPERT_CAPACITY * t / e)
        scores = jnp.einsum('ntd,ed->nte', x, gate_w)
        probs = jax.nn.softmax(scores, axis=-1)
        g, m = jax.lax.top_k(probs.transpose(0, 2, 1), k)
        batch_idx = jnp.arange(n)[:, None, None]
        xin = x[batch_idx, m]
        h = jnp.einsum('nekd,edf->nekf', xin, w1)
        h = jax.nn.gelu(h, approximate=False)
        h = jnp.einsum('nekf,efd->nekd', h, w2)
        out_tok = g[..., None] * h
        out = jnp.zeros((n, t, d), dtype=x.dtype).at[batch_idx, m].add(out_tok)
        return out
    x = x + _L0_xcond_ref(_layernorm(x, axis=-1), cond_1024[:, None, :], ctx_1024, L0_xcond_attn1_wq, L0_xcond_attn1_wk, L0_xcond_attn1_wv, L0_xcond_attn1_wo, L0_xcond_attn1_bo, L0_xcond_attn2_wq, L0_xcond_attn2_wk, L0_xcond_attn2_wv, L0_xcond_attn2_wo, L0_xcond_attn2_bo, L0_xcond_ff_w1, L0_xcond_ff_b1, L0_xcond_ff_w2, L0_xcond_ff_b2, L0_xcond_norm1_w, L0_xcond_norm1_b, L0_xcond_norm2_w, L0_xcond_norm2_b, L0_xcond_norm3_w, L0_xcond_norm3_b)
    x = x + _L0_ffn_ref(_layernorm(x, axis=-1), L0_ffn_ln_g, L0_ffn_ln_b, L0_ffn_Wq, L0_ffn_Wk, L0_ffn_Wv, L0_ffn_q_scale, L0_ffn_k_scale, L0_ffn_Wo, L0_ffn_gate_w, L0_ffn_gate_b, L0_ffn_w1, L0_ffn_b1, L0_ffn_w2, L0_ffn_b2)
    x = x + _L1_xcond_ref(_layernorm(x, axis=-1), ctx_1024, cond_1024, L1_xcond_W, L1_xcond_kernel, L1_xcond_recurrent_kernel, L1_xcond_bias)
    x = x + _L1_ffn_ref(_layernorm(x, axis=-1), L1_ffn_gate_w, L1_ffn_w1, L1_ffn_w2)
    return x

_drawn_inputs = setup_inputs


def setup_inputs(seed=0):
    import zlib

    import numpy as np

    out = dict(_drawn_inputs(seed))
    spreads = {'L0_ffn_ln_g': (1.0, 0.2),
     'L0_ffn_ln_b': (0.0, 0.1),
     'L0_ffn_q_scale': (1.0, 0.6),
     'L0_ffn_k_scale': (1.0, 0.6),
     'L0_ffn_gate_b': (0.0, 0.563),
     'L0_ffn_b1': (0.0, 0.381),
     'L0_ffn_b2': (0.0, 0.1),
     'L1_xcond_bias': (0.0, 0.4)}
    factors = {'L0_xcond_attn1_bo': 8.0,
     'L0_xcond_attn2_bo': 8.0,
     'L0_xcond_ff_b1': 8.0,
     'L0_xcond_ff_b2': 8.0,
     'L0_xcond_norm1_b': 5.601,
     'L0_xcond_norm2_b': 8.0,
     'L0_xcond_norm3_b': 8.0,
     'L1_xcond_W': 8.0,
     'L1_xcond_recurrent_kernel': 8.0,
     'L1_ffn_gate_w': 8.0,
     'L1_ffn_w1': 8.0,
     'L1_ffn_w2': 8.0}
    for name, (base, spread) in spreads.items():
        noise = np.random.default_rng([zlib.crc32(name.encode()), seed]).standard_normal(out[name].shape)
        drawn = base * np.exp(spread * noise) if base else spread * noise
        out[name] = jnp.asarray(drawn.astype(out[name].dtype))
    for name, factor in factors.items():
        out[name] = (out[name] * factor).astype(out[name].dtype)
    return out
```

```python
from contextlib import ExitStack

import concourse.bass as bass
from concourse import mybir

F32 = mybir.dt.float32
BF16 = mybir.dt.bfloat16
ALU = mybir.AluOpType
ACT = mybir.ActivationFunctionType
AX = mybir.AxisListType


P = 128
B = 4
S = 512
NT = S // P
CTX = 77
CPAD = 96
NP = 8
HD = 64
E = 8
FC = 4
TOPK = 2 * S // E
EPS = 1e-5
BANK = 512
STEPS_PER_TURN = 4


class Counted:

    def __init__(self, sem):
        self.sem, self.base = sem, 0


def layer_norm(nc, ln, name, src, eps_sb, ident, rows_out=None, cols_out=None, scale=None, shift=None,
               add_to=None, gain_rows=None, bias_rows=None):
    with ExitStack() as ctx:
        def sb(n, shape):
            return ctx.enter_context(nc.sbuf_tensor(f"{name}_{n}", shape, F32))

        stats, mv, std, rstd = sb("stats", [P, NT, 6]), sb("mv", [P, NT, 2]), sb("std", [P, NT]), sb("rstd", [P, NT])
        landed = sb("landed", [P, 1])
        xn, xg, xb = sb("xn", [P, NT, P]), sb("xg", [P, NT, P]), sb("xb", [P, NT, P])
        tp = ctx.enter_context(nc.psum_tensor(f"{name}_tp", [P, S], F32))
        block = ctx.enter_context(nc.Block())

        def wait(eng, what, n):
            eng.wait_ge(ln[what].sem, n + ln[what].base)

        @block.vector
        def _(dve):
            with dve.Fori(0, B) as b:
                for j in range(NT):
                    last = dve.bn_stats(stats[:, j, :], src[:, bass.ds(b * NT + j, 1), :])
                last.then_inc(ln["stats"].sem, 1)
                wait(dve, "stats", b + 1)
                dve.tensor_copy(landed[:], stats[:, NT - 1, 0:1])
                for j in range(NT):
                    last = dve.bn_aggr(mv[:, j, :], stats[:, j, :])
                last.then_inc(ln["aggr"].sem, 1)
                wait(dve, "sqrt", b + 1)
                dve.reciprocal(rstd[:], std[:]).then_inc(ln["rstd"].sem, 1)
                wait(dve, "rstd", b + 1)
                if cols_out is not None:
                    wait(dve, "turned", b + 1)
                for j in range(NT):
                    dst = xn[:, j, :] if gain_rows is not None or cols_out is not None else \
                        rows_out[:, bass.ds(b * NT + j, 1), :]
                    last = dve.tensor_scalar(dst, src[:, bass.ds(b * NT + j, 1), :], mv[:, j, 0:1],
                                             rstd[:, j:j + 1], ALU.subtract, ALU.mult)
                last.then_inc(ln["xn"].sem, 1)
                if gain_rows is not None:
                    wait(dve, "xn", b + 1)
                    dve.tensor_tensor(xg[:], xn[:], gain_rows, ALU.mult).then_inc(ln["gained"].sem, 1)
                    wait(dve, "gained", b + 1)
                    dve.tensor_tensor(xb[:], xg[:], bias_rows, ALU.add).then_inc(ln["biased"].sem, 1)
                    wait(dve, "biased", b + 1)
                    dve.tensor_tensor(rows_out[:, bass.ds(b * NT, NT), :], xb[:], add_to[:, bass.ds(b * NT, NT), :],
                                      ALU.add)

        @block.scalar
        def _(act):
            with act.Fori(0, B) as b:
                wait(act, "aggr", b + 1)
                act.activation(std[:], mv[:, :, 1], ACT.Sqrt, bias=eps_sb).then_inc(ln["sqrt"].sem, 1)
                if cols_out is not None:
                    wait(act, "turned", b + 2)
                    act.activation(cols_out(b), tp[:], ACT.Identity, bias=shift(b), scale=scale(b))\
                       .then_inc(ln["cols"].sem, 1)

        if cols_out is not None:
            @block.tensor
            def _(pe):
                with pe.Fori(0, B) as b:
                    wait(pe, "xn", b + 1)
                    wait(pe, "cols", b + 1)
                    for j in range(NT):
                        last = pe.transpose(tp[:, j * P:(j + 1) * P], xn[:, j, :], ident)
                    last.then_inc(ln["turned"].sem, 1)

    for what in ["stats", "aggr", "sqrt", "rstd", "xn"] + ["turned", "cols"] * (cols_out is not None) \
            + ["gained", "biased"] * (gain_rows is not None):
        ln[what].base += B


def attention(nc, name, h_cols, y, wqkv, wo, ident, ctx_cols=None, out_bias=None, causal=False, masks=None, norm=None,
              q_scale=1.0, accumulate=True):
    NK = S if ctx_cols is None else CTX
    KT = NT if ctx_cols is None else 1
    kw = min(NK, P)
    U = 2 * NT

    def keys(qt):
        return (qt + 1) * P if causal else NK

    def ktiles(qt):
        return qt + 1 if causal else KT

    with ExitStack() as ctx:
        def sb(n, shape, dt=F32):
            return ctx.enter_context(nc.sbuf_tensor(f"{name}_{n}", shape, dt))

        def pb(n, shape):
            return ctx.enter_context(nc.psum_tensor(f"{name}_{n}", shape, F32))

        def sem(n):
            return ctx.enter_context(nc.semaphore(f"{name}_{n}"))

        h_b = sb("h_b", [P, S])
        c_b = h_b if ctx_cols is None else sb("c_b", [P, CTX])
        w_sb = sb("w_sb", [P, 3, P])
        wo_sb = sb("wo_sb", [P, P])
        q_sb = sb("q_sb", [P, S])
        k_sb = sb("k_sb", [P, NK])
        v_sb = sb("v_sb", [P, KT, P])
        probs = sb("probs", [P, 4, NK])
        probs_t = sb("probs_t", [P, 4, KT, P])
        o_sb = sb("o_sb", [P, S])
        negmax = sb("negmax", [P, U])
        total = sb("total", [P, U])
        rtotal = sb("rtotal", [P, U])
        sc = [pb(f"sc{i}", [P, S]) for i in range(4)]
        pt = [pb(f"pt{i}", [P, S]) for i in range(2)]
        ot = pb("ot", [P, S])
        wob = pb("wob", [P, S])
        s_hb = sem("hb")
        s_w, s_wo = sem("w"), sem("wo")
        s_pq, s_pk, s_pv = sem("pq"), sem("pk"), sem("pv")
        s_qe, s_ke, s_ve = sem("qe"), sem("ke"), sem("ve")
        s_sc, s_max, s_exp, s_rt, s_pn = sem("sc"), sem("max"), sem("exp"), sem("rt"), sem("pn")
        s_pt, s_pte, s_ot, s_oe, s_wd, s_y = sem("pt"), sem("pte"), sem("ot"), sem("oe"), sem("wd"), sem("y")
        s_y0 = sem("y0")
        if norm is not None:
            ones_half, qk_gain, eps_l2 = norm
            q_raw, k_raw, q_sq, k_sq = sb("q_raw", [P, S]), sb("k_raw", [P, S]), sb("q_sq", [P, S]), sb("k_sq", [P, S])
            s_sq, s_raw, s_ss, s_rms, s_rrms = sem("sq"), sem("raw"), sem("ss"), sem("rms"), sem("rrms")
        block = ctx.enter_context(nc.Block())

        @block.sync
        def _(sp):
            with sp.Fori(0, B) as b:
                with sp.Fori(0, NP) as hp:
                    it = b * NP + hp
                    sp.wait_ge(s_pv, it + 1)
                    sp.dma_start(w_sb[:], wqkv[bass.ds(hp, 1), :, :, :].rearrange("a p t n -> (a p) t n")).then_inc(s_w, 16)
                    sp.wait_ge(s_wd, it + 1)
                    sp.dma_start(wo_sb[:], wo[bass.ds(hp, 1), :, :].rearrange("a p n -> (a p) n")).then_inc(s_wo, 16)

        @block.gpsimd
        def _(pool):
            with pool.Fori(0, B) as b:
                pool.wait_ge(s_pv, b * NP + 1)
                last = pool.tensor_copy(h_b[:], h_cols[:, bass.ds(b * S, S)])
                if ctx_cols is not None:
                    last = pool.tensor_copy(c_b[:], ctx_cols[:, bass.ds(b * CPAD, CTX)])
                last.then_inc(s_hb, 1)

        @block.tensor
        def _(pe):
            pe.sem_inc(s_pv, 1)
            pe.sem_inc(s_wd, 1)
            with pe.Fori(0, B) as b:
                with pe.Fori(0, NP) as hp:
                    it = b * NP + hp
                    pe.wait_ge(s_hb, b + 1)
                    pe.wait_ge(s_w, 16 * it + 16)
                    pe.wait_ge(s_pte, U * it + 1)
                    pe.matmul(pt[0][:], w_sb[:, 0, :], h_b[:], start=True, stop=True).then_inc(s_pq, 1)
                    pe.matmul(pt[1][:, 0:NK], w_sb[:, 1, :], c_b[:], start=True, stop=True).then_inc(s_pk, 1)
                    pe.wait_ge(s_oe, it + 1)
                    for kt in range(KT):
                        last = pe.matmul(ot[0:kw, kt * P:(kt + 1) * P], c_b[:, kt * P:kt * P + kw], w_sb[:, 2, :],
                                         start=True, stop=True)
                    last.then_inc(s_pv, 1)
                    if norm is not None:
                        pe.wait_ge(s_sq, 2 * it + 1)
                        pe.matmul(sc[0][:], ones_half, q_sq[:], start=True, stop=True).then_inc(s_ss, 1)
                        pe.wait_ge(s_sq, 2 * it + 2)
                        pe.matmul(sc[1][:], ones_half, k_sq[:], start=True, stop=True).then_inc(s_ss, 1)
                    pe.wait_ge(s_qe, it + 1)
                    pe.wait_ge(s_ke, it + 1)

                    def scores(qt):
                        for j in range(2):
                            u = 2 * qt + j
                            if qt >= 2:
                                pe.wait_ge(s_exp, U * it + u - 2)
                            bank = sc[u % 4]
                            last = pe.matmul(bank[:, 0:keys(qt)], q_sb[HD * j:HD * j + HD, qt * P:(qt + 1) * P],
                                             k_sb[HD * j:HD * j + HD, 0:keys(qt)], start=True, stop=not causal)
                            if causal:
                                last = pe.matmul(bank[:, qt * P:(qt + 1) * P], masks[0], masks[1], start=False, stop=True)
                            last.then_inc(s_sc, 1)

                    def turn_probs(qt):
                        for j in range(2):
                            u = 2 * qt + j
                            pe.wait_ge(s_pn, U * it + u + 1)
                            if u >= 2:
                                pe.wait_ge(s_pte, U * it + u)
                            for kt in range(ktiles(qt)):
                                last = pe.transpose(pt[j][0:kw, kt * P:(kt + 1) * P],
                                                    probs[:, u % 4, kt * P:kt * P + kw], ident)
                            last.then_inc(s_pt, 1)

                    def values(qt):
                        pe.wait_ge(s_pte, U * it + 2 * qt + 3)
                        if qt == 0:
                            pe.wait_ge(s_ve, it + 1)
                        for kt in range(ktiles(qt)):
                            for j in range(2):
                                last = pe.matmul(ot[HD * j:HD * j + HD, qt * P:(qt + 1) * P],
                                                 v_sb[0:kw, kt, HD * j:HD * j + HD],
                                                 probs_t[0:kw, (2 * qt + j) % 4, kt, :],
                                                 start=kt == 0, stop=kt == ktiles(qt) - 1, tile_position=(0, HD * j))
                        if qt == NT - 1:
                            last.then_inc(s_ot, 1)

                    scores(0)
                    scores(1)
                    turn_probs(0)
                    scores(2)
                    values(0)
                    turn_probs(1)
                    scores(3)
                    values(1)
                    turn_probs(2)
                    values(2)
                    turn_probs(3)
                    values(3)
                    pe.wait_ge(s_oe, it + 2)
                    pe.wait_ge(s_wo, 16 * it + 16)
                    pe.wait_ge(s_y, it + 1)
                    for j in range(NT):
                        last = pe.matmul(wob[:, j * P:(j + 1) * P], o_sb[:, j * P:(j + 1) * P], wo_sb[:], start=True,
                                         stop=True)
                    last.then_inc(s_wd, 1)

        @block.scalar
        def _(act):
            act.sem_inc(s_pte, 1)
            act.sem_inc(s_exp, 1)
            with act.Fori(0, B) as b:
                with act.Fori(0, NP) as hp:
                    it = b * NP + hp
                    if norm is None:
                        act.wait_ge(s_pq, it + 1)
                        act.activation(q_sb[:], pt[0][:], ACT.Copy, scale=q_scale).then_inc(s_qe, 1)
                        act.wait_ge(s_pk, it + 1)
                        act.activation(k_sb[:], pt[1][:, 0:NK], ACT.Copy).then_inc(s_ke, 1)
                    else:
                        act.wait_ge(s_pq, it + 1)
                        act.activation(q_sq[:], pt[0][:], ACT.Square).then_inc(s_sq, 1)
                        act.activation(q_raw[:], pt[0][:], ACT.Copy, scale=q_scale).then_inc(s_raw, 1)
                        act.wait_ge(s_pk, it + 1)
                        act.activation(k_sq[:], pt[1][:], ACT.Square).then_inc(s_sq, 1)
                        act.activation(k_raw[:], pt[1][:], ACT.Copy).then_inc(s_raw, 1)
                        act.wait_ge(s_ss, 2 * it + 1)
                        act.wait_ge(s_sq, 2 * it + 1)
                        act.activation(q_sq[:], sc[0][:], ACT.Sqrt, bias=eps_l2).then_inc(s_rms, 1)
                        act.wait_ge(s_ss, 2 * it + 2)
                        act.wait_ge(s_sq, 2 * it + 2)
                        act.activation(k_sq[:], sc[1][:], ACT.Sqrt, bias=eps_l2).then_inc(s_rms, 1)

                    def exps(qt):
                        for j in range(2):
                            u = 2 * qt + j
                            act.wait_ge(s_max, U * it + u + 1)
                            act.activation(probs[:, u % 4, 0:keys(qt)], sc[u % 4][:, 0:keys(qt)], ACT.Exp,
                                           bias=negmax[:, u:u + 1], accum_out=total[:, u:u + 1]).then_inc(s_exp, 1)

                    def evacuate(qt):
                        for j in range(2):
                            u = 2 * qt + j
                            act.wait_ge(s_pt, U * it + u + 1)
                            act.activation(probs_t[0:kw, u % 4, 0:ktiles(qt), :],
                                           pt[j][0:kw, 0:ktiles(qt) * P].rearrange("p (t q) -> p t q", q=P),
                                           ACT.Copy).then_inc(s_pte, 1)

                    exps(0)
                    exps(1)
                    evacuate(0)
                    exps(2)
                    evacuate(1)
                    exps(3)
                    evacuate(2)
                    evacuate(3)

        @block.vector
        def _(dve):
            dve.sem_inc(s_oe, 1)
            dve.sem_inc(s_y, 1)
            n_tiles = B * NT
            if not accumulate:
                dve.memset(y[:], 0.0).then_inc(s_y0, 1)
                dve.wait_ge(s_y0, 1)
            elif out_bias is not None:
                dve.tensor_tensor(y[:], y[:], out_bias.rearrange("p (a d) -> p a d", a=1).broadcast_to([P, n_tiles, P]),
                                  ALU.add).then_inc(s_y0, 1)
                dve.wait_ge(s_y0, 1)
            with dve.Fori(0, B) as b:
                with dve.Fori(0, NP) as hp:
                    it = b * NP + hp
                    dve.wait_ge(s_pv, it + 2)
                    dve.tensor_copy(v_sb[0:kw, :, :], ot[0:kw, 0:KT * P].rearrange("p (t d) -> p t d", d=P)).then_inc(s_ve, 1)
                    if norm is not None:
                        dve.wait_ge(s_rms, 2 * it + 1)
                        dve.reciprocal(q_sq[:], q_sq[:]).then_inc(s_rrms, 1)
                        dve.wait_ge(s_rrms, 2 * it + 1)
                        dve.wait_ge(s_raw, 2 * it + 1)
                        dve.scalar_tensor_tensor(out=q_sb[:], in0=q_raw[:], scalar=qk_gain[0][:, bass.ds(hp, 1)],
                                                 in1=q_sq[:], op0=ALU.mult, op1=ALU.mult).then_inc(s_qe, 1)
                        dve.wait_ge(s_rms, 2 * it + 2)
                        dve.reciprocal(k_sq[:], k_sq[:]).then_inc(s_rrms, 1)
                        dve.wait_ge(s_rrms, 2 * it + 2)
                        dve.wait_ge(s_raw, 2 * it + 2)
                        dve.scalar_tensor_tensor(out=k_sb[:], in0=k_raw[:], scalar=qk_gain[1][:, bass.ds(hp, 1)],
                                                 in1=k_sq[:], op0=ALU.mult, op1=ALU.mult).then_inc(s_ke, 1)

                    def maxima(qt):
                        for j in range(2):
                            u = 2 * qt + j
                            dve.wait_ge(s_sc, U * it + u + 1)
                            dve.tensor_reduce(negmax[:, u:u + 1], sc[u % 4][:, 0:keys(qt)], axis=AX.X, op=ALU.max,
                                              negate=True).then_inc(s_max, 1)

                    def normalise(qt):
                        u = 2 * qt
                        dve.wait_ge(s_exp, U * it + u + 3)
                        dve.reciprocal(rtotal[:, u:u + 2], total[:, u:u + 2]).then_inc(s_rt, 1)
                        dve.wait_ge(s_rt, NT * it + qt + 1)
                        for j in range(2):
                            dve.tensor_scalar(probs[:, (u + j) % 4, 0:keys(qt)], probs[:, (u + j) % 4, 0:keys(qt)],
                                              rtotal[:, u + j:u + j + 1], None, ALU.mult).then_inc(s_pn, 1)

                    maxima(0)
                    maxima(1)
                    normalise(0)
                    maxima(2)
                    normalise(1)
                    maxima(3)
                    normalise(2)
                    normalise(3)
                    dve.wait_ge(s_ot, it + 1)
                    dve.tensor_copy(o_sb[:], ot[:]).then_inc(s_oe, 1)
                    dve.wait_ge(s_wd, it + 2)
                    dve.wait_ge(s_y, it + 1)
                    out = y[:, bass.ds(b * NT, NT), :]
                    dve.tensor_tensor(out, out, wob[:].rearrange("p (t d) -> p t d", d=P), ALU.add).then_inc(s_y, 1)


def feed_forward(nc, h_cols, y, w1, b1, w2, b2_rows):
    with ExitStack() as ctx:
        def sb(n, shape):
            return ctx.enter_context(nc.sbuf_tensor(f"ff_{n}", shape, F32))

        def pb(n):
            return ctx.enter_context(nc.psum_tensor(f"ff_{n}", [P, S], F32))

        def sem(n):
            return ctx.enter_context(nc.semaphore(f"ff_{n}"))

        w1_sb, b1_sb, w2_sb = sb("w1_sb", [P, 2 * FC * P]), sb("b1_sb", [P, 2 * FC]), sb("w2_sb", [P, FC, P])
        gate, hidden = sb("gate", [P, 2, S]), sb("hidden", [P, FC, S])
        up, gt, down = [pb("up0"), pb("up1")], [pb("gt0"), pb("gt1")], pb("down")
        s_w, s_up, s_gelu, s_hid, s_down, s_y, s_y0 = (sem(n) for n in ("w", "up", "gelu", "hid", "down", "y", "y0"))
        block = ctx.enter_context(nc.Block())

        @block.sync
        def _(sp):
            sp.dma_start(w1_sb[:], w1).then_inc(s_w, 16)
            sp.dma_start(b1_sb[:], b1).then_inc(s_w, 16)
            sp.dma_start(w2_sb[:], w2).then_inc(s_w, 16)

        @block.tensor
        def _(pe):
            pe.sem_inc(s_down, 1)
            pe.wait_ge(s_w, 48)
            with pe.Fori(0, B) as b:
                for f in range(FC):
                    pe.wait_ge(s_hid, b * FC + max(f - 1, 0) + 1)
                    pe.matmul(up[f % 2][:], w1_sb[:, f * P:(f + 1) * P], h_cols[:, bass.ds(b * S, S)],
                              start=True, stop=True)
                    pe.matmul(gt[f % 2][:], w1_sb[:, (FC + f) * P:(FC + f + 1) * P], h_cols[:, bass.ds(b * S, S)],
                              start=True, stop=True).then_inc(s_up, 1)
                pe.wait_ge(s_y, b + 1)
                for f in range(FC):
                    pe.wait_ge(s_hid, b * FC + f + 2)
                    for j in range(NT):
                        last = pe.matmul(down[:, j * P:(j + 1) * P], hidden[:, f, j * P:(j + 1) * P], w2_sb[:, f, :],
                                         start=f == 0 and j == 0, stop=f == FC - 1, skip_group_check=True)
                last.then_inc(s_down, 1)

        @block.scalar
        def _(act):
            act.wait_ge(s_w, 48)
            with act.Fori(0, B) as b:
                for f in range(FC):
                    act.wait_ge(s_up, b * FC + f + 1)
                    if f >= 2:
                        act.wait_ge(s_hid, b * FC + f)
                    act.activation(gate[:, f % 2, :], gt[f % 2][:], ACT.Gelu, bias=b1_sb[:, FC + f:FC + f + 1])\
                       .then_inc(s_gelu, 1)

        @block.vector
        def _(dve):
            dve.sem_inc(s_hid, 1)
            dve.sem_inc(s_y, 1)
            dve.tensor_tensor(y[:], y[:], b2_rows.rearrange("p (a d) -> p a d", a=1).broadcast_to([P, B * NT, P]), ALU.add)\
               .then_inc(s_y0, 1)
            dve.wait_ge(s_y0, 1)
            dve.wait_ge(s_w, 48)
            with dve.Fori(0, B) as b:
                for f in range(FC):
                    dve.wait_ge(s_gelu, b * FC + f + 1)
                    if f == 0:
                        dve.wait_ge(s_down, b + 1)
                    dve.scalar_tensor_tensor(out=hidden[:, f, :], in0=up[f % 2][:], scalar=b1_sb[:, f:f + 1],
                                             in1=gate[:, f % 2, :], op0=ALU.add, op1=ALU.mult).then_inc(s_hid, 1)
                dve.wait_ge(s_down, b + 2)
                out = y[:, bass.ds(b * NT, NT), :]
                dve.tensor_tensor(out, out, down[:].rearrange("p (t d) -> p t d", d=P), ALU.add).then_inc(s_y, 1)


def experts(nc, name, h_cols, acc, gates, w1, b1, w2, gelu):
    with ExitStack() as ctx:
        def sb(n, shape):
            return ctx.enter_context(nc.sbuf_tensor(f"{name}_{n}", shape, F32))

        def pb(n):
            return ctx.enter_context(nc.psum_tensor(f"{name}_{n}", [P, S], F32))

        def sem(n):
            return ctx.enter_context(nc.semaphore(f"{name}_{n}"))

        w1_sb, w2_sb, b1_sb = sb("w1_sb", [P, 2, FC * P]), sb("w2_sb", [P, 2, FC, P]), sb("b1_sb", [P, 2, FC])
        hidden = sb("hidden", [P, FC, S])
        up, down = [pb("up0"), pb("up1")], pb("down")
        s_w, s_down = [sem("w0"), sem("w1")], [sem("done0"), sem("done1")]
        s_up, s_gelu, s_acc = sem("up"), sem("gelu"), sem("acc")
        loads = 2 + (b1 is not None)
        block = ctx.enter_context(nc.Block())

        @block.sync
        def _(sp):
            with sp.Fori(0, E // 2) as turn:
                for k in range(2):
                    e = turn * 2 + k
                    sp.wait_ge(s_down[k], turn * B + 1)
                    sp.dma_start(w1_sb[:, k, :], w1[bass.ds(e, 1), :, :].rearrange("a p n -> (a p) n")).then_inc(s_w[k], 16)
                    sp.dma_start(w2_sb[:, k, :, :], w2[bass.ds(e, 1), :, :, :].rearrange("a p f n -> (a p) f n"))\
                      .then_inc(s_w[k], 16)
                    if b1 is not None:
                        sp.dma_start(b1_sb[:, k, :], b1[bass.ds(e, 1), :, :].rearrange("a p n -> (a p) n"))\
                          .then_inc(s_w[k], 16)

        @block.tensor
        def _(pe):
            pe.sem_inc(s_down[0], 1)
            pe.sem_inc(s_down[1], 1)
            with pe.Fori(0, E // 2) as turn:
                for k in range(2):
                    with pe.Fori(0, B) as b:
                        pe.wait_ge(s_w[k], 16 * loads * turn + 16 * loads)
                        n = (turn * 2 + k) * B + b
                        for f in range(FC):
                            pe.wait_ge(s_gelu, n * FC + max(f - 1, 0) + 1)
                            pe.matmul(up[f % 2][:], w1_sb[:, k, f * P:(f + 1) * P], h_cols[:, bass.ds(b * S, S)],
                                      start=True, stop=True).then_inc(s_up, 1)
                        pe.wait_ge(s_acc, n + 1)
                        for f in range(FC):
                            pe.wait_ge(s_gelu, n * FC + f + 2)
                            for j in range(NT):
                                last = pe.matmul(down[:, j * P:(j + 1) * P], hidden[:, f, j * P:(j + 1) * P],
                                                 w2_sb[:, k, f, :], start=f == 0 and j == 0, stop=f == FC - 1,
                                                 skip_group_check=True)
                        last.then_inc(s_down[k], 1)

        @block.scalar
        def _(act):
            act.sem_inc(s_gelu, 1)
            with act.Fori(0, E // 2) as turn:
                for k in range(2):
                    with act.Fori(0, B) as b:
                        act.wait_ge(s_w[k], 16 * loads * turn + 16 * loads)
                        n = (turn * 2 + k) * B + b
                        for f in range(FC):
                            act.wait_ge(s_up, n * FC + f + 1)
                            act.activation(hidden[:, f, :], up[f % 2][:], gelu,
                                           bias=b1_sb[:, k, f:f + 1] if b1 is not None else 0.0).then_inc(s_gelu, 1)

        @block.vector
        def _(dve):
            dve.sem_inc(s_acc, 1)
            with dve.Fori(0, E // 2) as turn:
                for k in range(2):
                    with dve.Fori(0, B) as b:
                        dve.wait_ge(s_down[k], turn * B + b + 2)
                        dve.wait_ge(s_acc, (turn * 2 + k) * B + b + 1)
                        for j in range(NT):
                            out = acc[:, bass.ds(b * NT + j, 1), :].rearrange("p a d -> p (a d)")
                            last = dve.scalar_tensor_tensor(out=out, in0=down[:, j * P:(j + 1) * P],
                                                            scalar=gates[:, bass.ds((b * NT + j) * E + turn * 2 + k, 1)],
                                                            in1=out, op0=ALU.mult, op1=ALU.add)
                        last.then_inc(s_acc, 1)


def gating(nc, name, h_cols, gates, gw, gb_rows, ident, acc=None, b2=None):
    NTT = B * NT
    with ExitStack() as ctx:
        def sb(n, shape):
            return ctx.enter_context(nc.sbuf_tensor(f"{name}_{n}", shape, F32))

        def pb(n):
            return ctx.enter_context(nc.psum_tensor(f"{name}_{n}", [P, S], F32))

        def sem(n):
            return ctx.enter_context(nc.semaphore(f"{name}_{n}"))

        logits, shifted = sb("logits", [P, NTT, E]), sb("shifted", [P, NTT, E])
        expd = sb("expd", [P, NTT, E])
        top, total, rtotal = sb("top", [P, NTT]), sb("total", [P, NTT]), sb("rtotal", [P, NTT])
        lg = pb("lg")
        tp = [pb(f"tp{i}") for i in range(4)]
        s_lg, s_step, s_exp, s_g, s_tp, s_ev, s_mm = (sem(n) for n in ("lg", "step", "exp", "g", "tp", "ev", "mm"))
        g3 = gates.rearrange("p (t e) -> p t e", e=E)
        if b2 is not None:
            gates_t = sb("gates_t", [E, NTT * P])
        else:
            ranked = [sb(f"ranked{i}", [B * E, S]) for i in range(2)]
            kept, top8 = sb("kept", [B * E, S]), sb("top8", [B * E, 8])
            probs = sb("probs", [P, NTT, E])
        block = ctx.enter_context(nc.Block())

        @block.tensor
        def _(pe):
            for i in range(NTT):
                last = pe.matmul(lg[:, i * E:(i + 1) * E], h_cols[:, i * P:(i + 1) * P], gw, start=True, stop=True)
            last.then_inc(s_lg, 1)
            pe.wait_ge(s_g, 1)
            if b2 is not None:
                for i in range(NTT):
                    last = pe.transpose(tp[i // NT][0:E, i % NT * P:(i % NT + 1) * P], gates[:, i * E:(i + 1) * E],
                                        ident)
                last.then_inc(s_tp, 1)
                pe.wait_ge(s_ev, 1)
                for i in range(NTT):
                    last = pe.matmul(tp[i // NT][:, i % NT * P:(i % NT + 1) * P], gates_t[:, i * P:(i + 1) * P], b2,
                                     start=True, stop=True)
                last.then_inc(s_mm, 1)
            else:
                for j in range(NT):
                    last = pe.transpose(tp[0][0:B * E, j * P:(j + 1) * P], shifted[:, j * B:(j + 1) * B, :]
                                        .rearrange("p t e -> p (t e)"), ident)
                last.then_inc(s_tp, 1)
                pe.wait_ge(s_ev, 1)
                for j in range(NT):
                    last = pe.transpose(tp[1][:, j * B * E:(j + 1) * B * E], kept[:, j * P:(j + 1) * P],
                                        ident[0:B * E, 0:B * E])
                last.then_inc(s_mm, 1)

        @block.scalar
        def _(act):
            act.wait_ge(s_step, 3)
            act.activation(expd[:], shifted[:], ACT.Exp).then_inc(s_exp, 1)

        @block.vector
        def _(dve):
            done = 0

            def mine(instruction):
                nonlocal done
                done += 1
                instruction.then_inc(s_step, 1)
                dve.wait_ge(s_step, done)

            dve.wait_ge(s_lg, 1)
            raw = lg[:, 0:NTT * E].rearrange("p (t e) -> p t e", e=E)
            if gb_rows is not None:
                bias = gb_rows.rearrange("p (a e) -> p a e", a=1).broadcast_to([P, NTT, E])
                mine(dve.tensor_tensor(logits[:], raw, bias, ALU.add))
            else:
                mine(dve.tensor_copy(logits[:], raw))
            mine(dve.tensor_reduce(top[:], logits[:], axis=AX.X, op=ALU.max))

            def spread(x):
                return x.rearrange("p (t a) -> p t a", a=1).broadcast_to([P, NTT, E])

            mine(dve.tensor_tensor(shifted[:], logits[:], spread(top[:]), ALU.subtract))
            dve.wait_ge(s_exp, 1)
            mine(dve.tensor_reduce(total[:], expd[:], axis=AX.X, op=ALU.add))
            mine(dve.reciprocal(rtotal[:], total[:]))
            if b2 is not None:
                dve.tensor_tensor(g3, expd[:], spread(rtotal[:]), ALU.mult).then_inc(s_g, 1)
                dve.wait_ge(s_tp, 1)
                for b in range(B):
                    last = dve.tensor_copy(gates_t[:, b * S:(b + 1) * S], tp[b][0:E, :])
                last.then_inc(s_ev, 1)
                dve.wait_ge(s_mm, 1)
                for b in range(B):
                    dve.tensor_copy(acc[:, b * NT:(b + 1) * NT, :], tp[b][:].rearrange("p (t d) -> p t d", d=P))
            else:
                mine(dve.tensor_tensor(probs[:], expd[:], spread(rtotal[:]), ALU.mult))
                dve.tensor_copy(shifted[:].rearrange("p (j b) e -> p b j e", b=B),
                                probs[:].rearrange("p (b j) e -> p b j e", b=B)).then_inc(s_g, 1)
                dve.wait_ge(s_tp, 1)
                mine(dve.tensor_copy(ranked[0][:], tp[0][0:B * E, :]))
                for r in range(TOPK // 8):
                    mine(dve.max(top8[:], ranked[r % 2][:]))
                    mine(dve.match_replace(ranked[(r + 1) % 2][:], top8[:], ranked[r % 2][:], -1.0))
                dve.tensor_scalar(kept[:], ranked[TOPK // 8 % 2][:], 0.0, None, ALU.is_lt).then_inc(s_ev, 1)
                dve.wait_ge(s_mm, 1)
                dve.tensor_tensor(g3.rearrange("p (b j) e -> p b j e", b=B), probs[:].rearrange("p (b j) e -> p b j e", b=B),
                                  tp[1][:, 0:NTT * E].rearrange("p (j b e) -> p b j e", b=B, e=E), ALU.mult)


def recurrence_tables(nc, name, ctx_t, ctx_k, w_t, k_ctx, score_w, gate_w):
    with ExitStack() as ctx:
        s_mm, = (ctx.enter_context(nc.semaphore(f"{name}_{n}")) for n in ("mm",))
        ps = [ctx.enter_context(nc.psum_tensor(f"{name}_ps{i}", [P, BANK], F32)) for i in range(4)]
        block = ctx.enter_context(nc.Block())

        @block.tensor
        def _(pe):
            pe.matmul(ps[0][:, 0:B * CPAD], w_t, ctx_t, start=True, stop=True).then_inc(s_mm, 1)
            for k in range(3):
                pe.matmul(ps[1 + k][:, 0:3 * P], ctx_k[:, k * P:(k + 1) * P], k_ctx, start=True, stop=True)\
                  .then_inc(s_mm, 1)

        @block.vector
        def _(dve):
            dve.wait_ge(s_mm, 1)
            dve.tensor_copy(score_w, ps[0][:, 0:B * CPAD])
            for k in range(3):
                dve.wait_ge(s_mm, 2 + k)
                dve.tensor_copy(gate_w[:, k, :], ps[1 + k][:, 0:3 * P])


def recurrence(nc, x_t, score_w, gate_w, r_w, x_w, bias_row, mask_l, mask_r, ones_s, h0_t, h0_c, history):
    with ExitStack() as ctx:
        def sb(n, w, rows=P):
            return ctx.enter_context(nc.sbuf_tensor(f"gru_{n}", [rows, w], F32))

        def pb(n):
            return ctx.enter_context(nc.psum_tensor(f"gru_{n}", [P, BANK], F32))

        def sem(n):
            return ctx.enter_context(nc.semaphore(f"gru_{n}"))

        new_t, old_t = sb("new_t", 32), sb("old_t", 32)
        h, h_half, ones = sb("h", 32), sb("h_half", 32), sb("ones", B, 1)
        xs = sb("xs", B)
        p, p_t = sb("p", CPAD), sb("p_t", CPAD)
        negmax, rtotal = sb("negmax", 1), sb("rtotal", 1)
        own, pre, th = sb("own", 4 * 32), sb("pre", 2 * 32), sb("th", 2 * 32)
        own_h, c_half, rh, c_in, cand = sb("own_h", 32), sb("c_half", 32), sb("rh", 32), sb("c_in", 32), sb("cand", 32)
        one_z, z_h, new = sb("one_z", 32), sb("z_h", 32), sb("new", 32)
        ps_s, ps_own, ps_g, ps_c, ps_t = (pb(n) for n in ("ps_s", "ps_own", "ps_g", "ps_c", "ps_t"))
        (s_init, s_load, s_table, s_score, s_x, s_ownmm, s_total, s_gate, s_max, s_exp, s_pt, s_rt, s_own, s_xs, s_pre,
         s_th, s_ownh, s_chalf, s_rh, s_cin, s_cand, s_onez, s_zh, s_old, s_new, s_newt, s_h, s_hhalf, s_hist) = (
            sem(n) for n in ("init", "load", "table", "score", "x", "ownmm", "total", "gate", "max", "exp", "pt", "rt",
                             "own", "xs", "pre", "th", "ownh", "chalf", "rh", "cin", "cand", "onez", "zh", "old", "new",
                             "newt", "h", "hhalf", "hist"))
        block = ctx.enter_context(nc.Block())
        U = STEPS_PER_TURN

        @block.sync
        def _(sp):
            sp.dma_start(new_t[:, 0:B], h0_t).then_inc(s_load, 16)
            sp.dma_start(h[:], h0_c).then_inc(s_load, 16)

        @block.gpsimd
        def _(pool):
            pool.sem_inc(s_hist, 1)
            pool.tensor_copy(xs[:], x_t[:, 0:B]).then_inc(s_xs, 1)
            with pool.Fori(0, S // U) as turn:
                for k in range(U):
                    t = turn * U + k
                    pool.wait_ge(s_x, t + 1)
                    pool.tensor_copy(xs[:], x_t[:, bass.ds((t + 1) * B, B)]).then_inc(s_xs, 1)
                    pool.wait_ge(s_newt, t + 2)
                    pool.tensor_tensor(history[:, bass.ds(t * B, B)], new_t[:, 0:B], old_t[:, 0:B], ALU.add)\
                        .then_inc(s_hist, 1)

        @block.tensor
        def _(pe):
            pe.wait_ge(s_init, 6)
            pe.wait_ge(s_load, 32)
            with pe.Fori(0, S // U) as turn:
                for k in range(U):
                    t = turn * U + k
                    pe.wait_ge(s_own, t + 1)
                    pe.wait_ge(s_exp, t + 1)
                    pe.matmul(ps_s[:, 0:CPAD], mask_l, mask_r, start=True, stop=False)
                    for c in range(4):
                        pe.matmul(ps_own[32 * c:32 * c + B, 0:P], ones[:], bias_row[:, c, :], start=True, stop=False,
                                  tile_position=(0, 32 * c))
                    pe.wait_ge(s_xs, t + 1)
                    for c in range(4):
                        last = pe.matmul(ps_own[32 * c:32 * c + B, 32:P], xs[:], x_w[:, c, :], start=False, stop=False,
                                         tile_position=(0, 32 * c))
                    last.then_inc(s_x, 1)
                    def state_scores(half, final):
                        for b in range(B):
                            last = pe.matmul(ps_s[32 * b:32 * b + B, 0:80], half[:, 0:B], score_w[:, b, 0:80],
                                             start=False, stop=final, tile_position=(0, 32 * b))
                        return last

                    def state_gates(half, final):
                        for c in range(4):
                            last = pe.matmul(ps_own[32 * c:32 * c + B, 0:96], half[:, 0:B], r_w[:, c, :], start=False,
                                             stop=final, tile_position=(0, 32 * c))
                        return last

                    pe.wait_ge(s_old, t + 1)
                    state_scores(old_t, False)
                    pe.wait_ge(s_newt, t + 1)
                    state_scores(new_t, True).then_inc(s_score, 1)
                    state_gates(old_t, False)
                    state_gates(new_t, True).then_inc(s_ownmm, 1)
                    pe.wait_ge(s_pt, t + 1)
                    for k3 in range(3):
                        for c in range(4):
                            last = pe.matmul(ps_t[32 * c:32 * c + B, 0:2], p_t[:, 32 * k3:32 * k3 + B],
                                             ones_s[:, k3, :], start=k3 == 0, stop=k3 == 2, tile_position=(0, 32 * c))
                    last.then_inc(s_total, 1)
                    for lo, hi, bank in ((0, 64, ps_g), (64, 96, ps_c)):
                        for k3 in range(3):
                            for c in range(4):
                                last = pe.matmul(bank[32 * c:32 * c + B, 0:hi - lo], p_t[:, 32 * k3:32 * k3 + B],
                                                 gate_w[:, k3, 96 * c + lo:96 * c + hi], start=k3 == 0, stop=k3 == 2,
                                                 tile_position=(0, 32 * c))
                        last.then_inc(s_gate, 1)

        @block.scalar
        def _(act):
            act.sem_inc(s_exp, 1)
            act.wait_ge(s_load, 32)
            act.activation(cand[:], h[:], ACT.Exp).then_inc(s_table, 1)
            act.wait_ge(s_table, 1)
            with act.Fori(0, S // U) as turn:
                for k in range(U):
                    t = turn * U + k
                    act.wait_ge(s_max, t + 1)
                    act.activation(p[:], ps_s[:, 0:CPAD], ACT.Exp, bias=negmax[:, 0:1]).then_inc(s_exp, 1)
                    act.wait_ge(s_pre, t + 1)
                    act.activation(th[:], pre[:], ACT.Tanh, scale=0.5).then_inc(s_th, 1)
                    act.wait_ge(s_cin, t + 1)
                    act.activation(cand[:], c_in[:], ACT.Tanh).then_inc(s_cand, 1)

        @block.vector
        def _(dve):
            dve.sem_inc(s_own, 1)
            dve.sem_inc(s_old, 1)
            dve.sem_inc(s_newt, 1)
            dve.memset(ps_g[:], 0.0).then_inc(s_init, 1)
            dve.memset(ps_c[:], 0.0).then_inc(s_init, 1)
            dve.memset(ps_t[:], 1.0).then_inc(s_init, 1)
            dve.memset(ps_own[:], 0.0).then_inc(s_init, 1)
            dve.memset(ones[:], 1.0).then_inc(s_init, 1)
            dve.memset(old_t[:], 0.0).then_inc(s_init, 1)
            dve.wait_ge(s_load, 32)
            dve.tensor_scalar(h_half[:], h[:], 0.5, None, ALU.mult).then_inc(s_hhalf, 1)
            with dve.Fori(0, S // U) as turn:
                for k in range(U):
                    t = turn * U + k
                    dve.wait_ge(s_score, t + 1)
                    dve.tensor_reduce(negmax[:], ps_s[:, 0:78], axis=AX.X, op=ALU.max, negate=True).then_inc(s_max, 1)
                    dve.wait_ge(s_exp, t + 2)
                    dve.transpose(p_t[:], p[:]).then_inc(s_pt, 1)
                    dve.wait_ge(s_ownmm, t + 1)
                    dve.tensor_copy(own[:], ps_own[:, 0:P]).then_inc(s_own, 1)
                    dve.wait_ge(s_total, t + 1)
                    dve.reciprocal(rtotal[:], ps_t[:, 0:1]).then_inc(s_rt, 1)
                    dve.wait_ge(s_rt, t + 1)
                    dve.wait_ge(s_gate, 2 * t + 1)
                    dve.scalar_tensor_tensor(out=pre[:], in0=ps_g[:, 0:64], scalar=rtotal[:, 0:1], in1=own[:, 32:96],
                                             op0=ALU.mult, op1=ALU.add).then_inc(s_pre, 1)
                    dve.scalar_tensor_tensor(out=own_h[:], in0=own[:, 0:32], scalar=0.5, in1=own[:, 96:P],
                                             op0=ALU.mult, op1=ALU.add).then_inc(s_ownh, 1)
                    dve.wait_ge(s_ownh, t + 1)
                    dve.wait_ge(s_gate, 2 * t + 2)
                    dve.scalar_tensor_tensor(out=c_half[:], in0=ps_c[:, 0:32], scalar=rtotal[:, 0:1], in1=own_h[:],
                                             op0=ALU.mult, op1=ALU.add).then_inc(s_chalf, 1)
                    dve.wait_ge(s_th, t + 1)
                    dve.scalar_tensor_tensor(out=rh[:], in0=th[:, 0:32], scalar=0.5, in1=own[:, 0:32], op0=ALU.mult,
                                             op1=ALU.mult).then_inc(s_rh, 1)
                    dve.wait_ge(s_rh, t + 1)
                    dve.tensor_tensor(c_in[:], rh[:], c_half[:], ALU.add).then_inc(s_cin, 1)
                    dve.tensor_scalar(one_z[:], th[:, 32:64], -0.5, 0.5, ALU.mult, ALU.add).then_inc(s_onez, 1)
                    dve.wait_ge(s_hhalf, t + 1)
                    dve.scalar_tensor_tensor(out=z_h[:], in0=th[:, 32:64], scalar=1.0, in1=h_half[:], op0=ALU.add,
                                             op1=ALU.mult).then_inc(s_zh, 1)
                    dve.wait_ge(s_zh, t + 1)
                    dve.wait_ge(s_hist, t + 1)
                    dve.transpose(old_t[:], z_h[:]).then_inc(s_old, 1)
                    dve.wait_ge(s_cand, t + 1)
                    dve.tensor_tensor(new[:], cand[:], one_z[:], ALU.mult).then_inc(s_new, 1)
                    dve.wait_ge(s_new, t + 1)
                    dve.transpose(new_t[:], new[:]).then_inc(s_newt, 1)
                    dve.tensor_tensor(h[:], new[:], z_h[:], ALU.add).then_inc(s_h, 1)
                    dve.wait_ge(s_h, t + 1)
                    dve.tensor_scalar(h_half[:], h[:], 0.5, None, ALU.mult).then_inc(s_hhalf, 1)


def add_history(nc, x, history, ident):
    with ExitStack() as ctx:
        s_tp = ctx.enter_context(nc.semaphore("hist_tp"))
        tp = [ctx.enter_context(nc.psum_tensor(f"hist_tp{b}", [P, S], F32)) for b in range(B)]
        block = ctx.enter_context(nc.Block())
        by_batch = history.rearrange("p (t b) -> p b t", b=B)

        @block.tensor
        def _(pe):
            for b in range(B):
                for j in range(NT):
                    last = pe.transpose(tp[b][:, j * P:(j + 1) * P], by_batch[:, b, j * P:(j + 1) * P], ident)
                last.then_inc(s_tp, 1)

        @block.vector
        def _(dve):
            for b in range(B):
                dve.wait_ge(s_tp, b + 1)
                rows = x[:, b * NT:(b + 1) * NT, :]
                dve.tensor_tensor(rows, rows, tp[b][:].rearrange("p (t d) -> p t d", d=P), ALU.add)


def condition_columns(nc, cond_t, norm_w, norm_b, columns):
    with ExitStack() as ctx:
        s_mm = ctx.enter_context(nc.semaphore("cond_mm"))
        ps = ctx.enter_context(nc.psum_tensor("cond_ps", [P, S], F32))
        block = ctx.enter_context(nc.Block())

        @block.tensor
        def _(pe):
            for i in range(6):
                last = pe.matmul(ps[:, i * B:(i + 1) * B], norm_w[:, i * P:(i + 1) * P], cond_t, start=True, stop=True)
            last.then_inc(s_mm, 1)

        @block.vector
        def _(dve):
            dve.wait_ge(s_mm, 1)
            for i in range(6):
                dve.tensor_scalar(columns[:, i * B:(i + 1) * B], ps[:, i * B:(i + 1) * B], norm_b[:, i:i + 1],
                                  1.0 if i % 2 == 0 else 0.0, ALU.add, ALU.add)


def program(nc, a, out, probe=None):
    with ExitStack() as ctx:
        def sb(n, shape, dt=F32):
            return ctx.enter_context(nc.sbuf_tensor(n, shape, dt))

        ln = {n: Counted(ctx.enter_context(nc.semaphore(f"ln_{n}")))
              for n in ("stats", "aggr", "sqrt", "rstd", "xn", "turned", "cols", "gained", "biased")}
        s_in = ctx.enter_context(nc.semaphore("in"))
        s_out = ctx.enter_context(nc.semaphore("out"))
        x, y = sb("x", [P, B * NT, P]), sb("y", [P, B * NT, P])
        h_cols = sb("h_cols", [P, B * S])
        columns = sb("columns", [P, 6 * B])
        gates = sb("gates", [P, B * NT * E])
        resident = {}
        for n in ("ident", "masks", "eps", "ones_half", "cond_t", "norm_w", "norm_b", "ctx_t", "ctx_k", "bo1_rows", "bo2_rows",
                  "ffb2_rows", "ln_cols", "g_rows", "b_rows", "qk_gain", "gate_w", "gate_b_rows", "b2", "gw2",
                  "w_t", "k_ctx", "r_w", "x_w", "bias_row", "mask_l", "mask_r", "ones_s"):
            resident[n] = sb(f"c_{n}", list(a[n].shape))
        c = {n: t[:] for n, t in resident.items()}
        narrow = {n: sb(f"b_{n}", list(a[n].shape), BF16) for n in ("masks", "mask_l", "mask_r")}
        x_dram = a["x"].rearrange("(n p) d -> p n d", p=P)
        with nc.Block() as block:
            @block.scalar
            def _(act):
                act.sem_inc(ln["cols"].sem, 1)

            @block.tensor
            def _(pe):
                pe.sem_inc(ln["turned"].sem, 1)

            @block.sync
            def _(sp):
                sp.dma_start(x[:], x_dram).then_inc(s_in, 16)
                for n in resident:
                    sp.dma_start(c[n], a[n]).then_inc(s_in, 16)
                sp.wait_ge(s_in, 16 * (1 + len(resident)))

            @block.vector
            def _(dve):
                dve.wait_ge(s_in, 16 * (1 + len(resident)))
                for n, t in narrow.items():
                    dve.tensor_copy(t[:], c[n])
        c.update({n: t[:] for n, t in narrow.items()})
        ident, eps = c["ident"], c["eps"][:, 0:1]
        g_rows = c["g_rows"].rearrange("p (a d) -> p a d", a=1).broadcast_to([P, NT, P])
        b_rows = c["b_rows"].rearrange("p (a d) -> p a d", a=1).broadcast_to([P, NT, P])
        masks = (c["masks"][:, 0:P], c["masks"][:, P:2 * P])

        def columns_of(layer):
            return (lambda b: columns[:, bass.ds(b + (2 * layer) * B, 1)],
                    lambda b: columns[:, bass.ds(b + (2 * layer + 1) * B, 1)])

        def by_batch(b):
            return h_cols[:, bass.ds(b * S, S)]

        gain, bias = (lambda b: c["ln_cols"][:, 0:1]), (lambda b: c["ln_cols"][:, 1:2])
        one, zero = (lambda b: c["eps"][:, 2:3]), (lambda b: c["eps"][:, 3:4])

        condition_columns(nc, c["cond_t"], c["norm_w"], c["norm_b"], columns)
        layer_norm(nc, ln, "ln_a", x, eps, ident, rows_out=y)
        scale, shift = columns_of(0)
        layer_norm(nc, ln, "ln_b", y, eps, ident, cols_out=by_batch, scale=scale, shift=shift)
        if probe and probe(nc, 1, h_cols[:]): return
        attention(nc, "self", h_cols, y, a["wqkv1"], a["wo1"], ident, out_bias=c["bo1_rows"], q_scale=HD ** -0.5)
        if probe and probe(nc, 2, y[:].rearrange("p t d -> p (t d)")): return
        scale, shift = columns_of(1)
        layer_norm(nc, ln, "ln_c", y, eps, ident, cols_out=by_batch, scale=scale, shift=shift)
        attention(nc, "cross", h_cols, y, a["wqkv2"], a["wo2"], ident, ctx_cols=c["ctx_t"], out_bias=c["bo2_rows"],
                  q_scale=HD ** -0.5)
        if probe and probe(nc, 3, y[:].rearrange("p t d -> p (t d)")): return
        scale, shift = columns_of(2)
        layer_norm(nc, ln, "ln_d", y, eps, ident, cols_out=by_batch, scale=scale, shift=shift)
        feed_forward(nc, h_cols, y, a["ff_w1"], a["ff_b1"], a["ff_w2"], c["ffb2_rows"])
        with nc.Block() as block:
            @block.vector
            def _(dve):
                dve.tensor_tensor(x[:], x[:], y[:], ALU.add)
        if probe and probe(nc, 4, x[:].rearrange("p t d -> p (t d)")): return

        layer_norm(nc, ln, "ln_e", x, eps, ident, rows_out=y)
        layer_norm(nc, ln, "ln_f", y, eps, ident, cols_out=by_batch, scale=gain, shift=bias)
        attention(nc, "causal", h_cols, y, a["wqkv3"], a["wo3"], ident, causal=True, masks=masks,
                  norm=(c["ones_half"], (c["qk_gain"][:, 0:NP], c["qk_gain"][:, NP:2 * NP]), c["eps"][:, 1:2]),
                  q_scale=10.0, accumulate=False)
        if probe and probe(nc, 5, y[:].rearrange("p t d -> p (t d)")): return
        layer_norm(nc, ln, "ln_g", y, eps, ident, cols_out=by_batch, scale=gain, shift=bias)
        gating(nc, "moe_gate", h_cols, gates[:], c["gate_w"], c["gate_b_rows"], ident, acc=y, b2=c["b2"])
        experts(nc, "moe", h_cols, y, gates[:], a["moe_w1"], a["moe_b1"], a["moe_w2"], ACT.Gelu_apprx_tanh)
        layer_norm(nc, ln, "ln_h", y, eps, ident, rows_out=x, add_to=x, gain_rows=g_rows, bias_rows=b_rows)
        if probe and probe(nc, 6, x[:].rearrange("p t d -> p (t d)")): return

        with ExitStack() as own:
            x_t = own.enter_context(nc.sbuf_tensor("x_t", [P, (S + 1) * B], F32))
            score_w = own.enter_context(nc.sbuf_tensor("score_w", [P, B, CPAD], F32))
            gate_w = own.enter_context(nc.sbuf_tensor("ctx_gate_w", [P, 3, 3 * P], F32))
            with nc.Block() as block:
                @block.vector
                def _(dve):
                    dve.memset(x_t[:, S * B:(S + 1) * B], 0.0)
            x_by_batch = x_t[:, 0:S * B].rearrange("p (t b) -> p b t", b=B)
            layer_norm(nc, ln, "ln_i", x, eps, ident, scale=one, shift=zero,
                       cols_out=lambda b: x_by_batch[:, bass.ds(b, 1), :].rearrange("p a t -> p (a t)"))
            recurrence_tables(nc, "tables", c["ctx_t"], c["ctx_k"], c["w_t"], c["k_ctx"],
                              score_w[:].rearrange("p b s -> p (b s)"), gate_w)
            recurrence(nc, x_t, score_w, gate_w, c["r_w"].rearrange("p (c g) -> p c g", c=4),
                       c["x_w"].rearrange("p (c g) -> p c g", c=4), c["bias_row"].rearrange("p (c g) -> p c g", c=4),
                       c["mask_l"], c["mask_r"], c["ones_s"].rearrange("p (k g) -> p k g", k=3), a["cond_t"], a["h0_c"],
                       h_cols)
        add_history(nc, x, h_cols[:], ident)
        if probe and probe(nc, 7, x[:].rearrange("p t d -> p (t d)")): return

        layer_norm(nc, ln, "ln_j", x, eps, ident, cols_out=by_batch, scale=one, shift=zero)
        gating(nc, "pick", h_cols, gates[:], c["gw2"], None, ident)
        if probe and probe(nc, 8, gates[:]): return
        experts(nc, "picked", h_cols, x, gates[:], a["ec_w1"], None, a["ec_w2"], ACT.Gelu)
        with nc.Block() as block:
            @block.sync
            def _(sp):
                sp.dma_start(out.rearrange("(n p) d -> p n d", p=P), x[:]).then_inc(s_out, 16)
                sp.wait_ge(s_out, 16)


def laid_out(np, i):
    f = {k: np.ascontiguousarray(v) for k, v in i.items()}
    x0 = "L0_xcond_"

    def pairs(q, k, v):
        return np.stack([w.reshape(P, NP, P).transpose(1, 0, 2) for w in (q, k, v)], 2)

    def chunks(w, order):
        w = w.reshape(w.shape[:-1] + (3, 4, 32))[..., order, :, :]
        return np.moveaxis(w, -3, -2).reshape(w.shape[:-3] + (4, 96))

    a = {"x": f["x"].reshape(B * S, P), "cond_t": f["cond_1024"].T}
    a["norm_w"] = np.concatenate([f[f"{x0}norm{n}_w"] for n in (1, 2, 3)], 1)
    a["norm_b"] = np.concatenate([f[f"{x0}norm{n}_b"].reshape(2, P).T for n in (1, 2, 3)], 1)
    for n, w in ((1, "attn1"), (2, "attn2")):
        a[f"wqkv{n}"] = pairs(f[f"{x0}{w}_wq"], f[f"{x0}{w}_wk"], f[f"{x0}{w}_wv"])
        a[f"wo{n}"] = f[f"{x0}{w}_wo"].reshape(NP, P, P)
        a[f"bo{n}_rows"] = np.broadcast_to(f[f"{x0}{w}_bo"], (P, P))
    a["wqkv3"] = pairs(f["L0_ffn_Wq"], f["L0_ffn_Wk"], f["L0_ffn_Wv"])
    a["wo3"] = f["L0_ffn_Wo"].reshape(NP, P, P)
    a["ff_w1"], a["ff_b1"] = f[x0 + "ff_w1"], f[x0 + "ff_b1"].reshape(2 * FC, P).T
    a["ff_w2"] = f[x0 + "ff_w2"].reshape(FC, P, P).transpose(1, 0, 2)
    a["ffb2_rows"] = np.broadcast_to(f[x0 + "ff_b2"], (P, P))
    a["ln_cols"] = np.stack([f["L0_ffn_ln_g"], f["L0_ffn_ln_b"]], 1)
    a["g_rows"] = np.broadcast_to(f["L0_ffn_ln_g"], (P, P))
    a["b_rows"] = np.broadcast_to(f["L0_ffn_ln_b"], (P, P))
    a["qk_gain"] = np.concatenate([f[f"L0_ffn_{n}_scale"].reshape(NP, P).T for n in "qk"], 1)
    a["gate_w"], a["gate_b_rows"] = f["L0_ffn_gate_w"], np.broadcast_to(f["L0_ffn_gate_b"], (P, E))
    a["moe_w1"], a["moe_b1"] = f["L0_ffn_w1"], f["L0_ffn_b1"].reshape(E, FC, P).transpose(0, 2, 1)
    a["moe_w2"], a["b2"] = f["L0_ffn_w2"].reshape(E, FC, P, P).transpose(0, 2, 1, 3), f["L0_ffn_b2"]
    ctx_t = np.zeros((P, B, CPAD), np.float32)
    ctx_t[:, :, :CTX] = f["ctx_1024"].transpose(2, 0, 1)
    a["ctx_t"] = ctx_t.reshape(P, B * CPAD)
    a["ctx_k"] = ctx_t.reshape(P, B, 3, 32).transpose(0, 2, 1, 3).reshape(P, 3 * P)
    a["w_t"] = f["L1_xcond_W"].T
    a["k_ctx"] = chunks(f["L1_xcond_kernel"][P:], [1, 0, 2]).reshape(P, 3 * P)
    a["x_w"] = chunks(f["L1_xcond_kernel"][:P], [1, 0, 2]).reshape(P, 3 * P)
    a["r_w"] = chunks(f["L1_xcond_recurrent_kernel"], [2, 1, 0]).reshape(P, 3 * P)
    bias = np.zeros((1, 4, P), np.float32)
    bias[0, :, 32:] = chunks(f["L1_xcond_bias"], [1, 0, 2])
    a["bias_row"] = bias.reshape(1, 4 * P)
    h0 = np.zeros((4, 32, 32), np.float32)
    h0[:, :B] = f["cond_1024"].reshape(B, 4, 32).transpose(1, 0, 2)
    a["h0_c"] = h0.reshape(P, 32)
    a["gw2"] = f["L1_ffn_gate_w"].T
    a["ec_w1"], a["ec_w2"] = f["L1_ffn_w1"], f["L1_ffn_w2"].reshape(E, FC, P, P).transpose(0, 2, 1, 3)
    a["ident"] = np.eye(P, dtype=np.float32)
    a["eps"] = np.broadcast_to(np.array([EPS, 1e-12, 1.0, 0.0], np.float32), (P, 4))
    a["ones_half"] = np.kron(np.eye(2, dtype=np.float32), np.ones((HD, HD), np.float32))
    a["masks"] = np.concatenate([np.eye(P), np.triu(np.full((P, P), -1e30), 1)], 1).astype(np.float32)
    group, row = np.arange(P) // 32, np.arange(P) % 32
    used = row == group
    a["mask_l"] = np.stack([~used, used]).astype(np.float32)
    mask_r = np.zeros((2, CPAD))
    mask_r[0, :CTX], mask_r[0, CTX + 1:], mask_r[1, CTX:] = -1e30, -1e30, -1e30
    a["mask_r"] = mask_r.astype(np.float32)
    ones = (32 * np.arange(3)[None, :] + row[:, None] < CTX).astype(np.float32)
    a["ones_s"] = np.repeat(ones, 2, 1)
    return {k: np.ascontiguousarray(v) for k, v in a.items()}


def kernel(**inputs):
    import numpy as np
    from concourse import bacc
    from concourse.bass_utils import run_bass_kernel_spmd

    arrays = laid_out(np, inputs)
    nc = bacc.Bacc("TRN2", target_bir_lowering=False, num_devices=1)
    a = {n: nc.dram_tensor(f"in_{n}", v.shape, mybir.dt.from_np(v.dtype), kind="ExternalInput").ap()
         for n, v in arrays.items()}
    out = nc.dram_tensor("out", (B * S, P), F32, kind="ExternalOutput").ap()
    program(nc, a, out)
    r = run_bass_kernel_spmd(nc, [{f"in_{n}": v for n, v in arrays.items()}], core_ids=[0])
    return r.results[0]["out"].reshape(B, S, P)
```

```python
from contextlib import ExitStack

import concourse.bass as bass
from concourse import mybir

F32 = mybir.dt.float32
BF16 = mybir.dt.bfloat16
ALU = mybir.AluOpType
ACT = mybir.ActivationFunctionType
AX = mybir.AxisListType


P = 128
B = 4
S = 512
NT = S // P
CTX = 77
CPAD = 96
NP = 8
HD = 64
E = 8
FC = 4
TOPK = 2 * S // E
EPS, EPS_L2 = 1e-5, 1e-12
QK_SCALE = 10.0
BANK = 512
STEPS_PER_TURN = 8


class Counted:

    def __init__(self, sem):
        self.sem, self.base = sem, 0


def layer_norm(nc, ln, name, src, eps_sb, ident, rows_out=None, cols_out=None, scale=None, shift=None,
               add_to=None, gain_rows=None, bias_rows=None):
    with ExitStack() as ctx:
        def sb(n, shape):
            return ctx.enter_context(nc.sbuf_tensor(f"{name}_{n}", shape, F32))

        stats, mv, std, rstd = sb("stats", [P, NT, 6]), sb("mv", [P, NT, 2]), sb("std", [P, NT]), sb("rstd", [P, NT])
        landed = sb("landed", [P, 1])
        xn, xg, xb = sb("xn", [P, NT, P]), sb("xg", [P, NT, P]), sb("xb", [P, NT, P])
        tp = ctx.enter_context(nc.psum_tensor(f"{name}_tp", [P, S], F32))
        block = ctx.enter_context(nc.Block())

        def wait(eng, what, n):
            eng.wait_ge(ln[what].sem, n + ln[what].base)

        @block.vector
        def _(dve):
            with dve.Fori(0, B) as b:
                for j in range(NT):
                    last = dve.bn_stats(stats[:, j, :], src[:, bass.ds(b * NT + j, 1), :])
                last.then_inc(ln["stats"].sem, 1)
                wait(dve, "stats", b + 1)
                dve.tensor_copy(landed[:], stats[:, NT - 1, 0:1])
                for j in range(NT):
                    last = dve.bn_aggr(mv[:, j, :], stats[:, j, :])
                last.then_inc(ln["aggr"].sem, 1)
                wait(dve, "sqrt", b + 1)
                dve.reciprocal(rstd[:], std[:]).then_inc(ln["rstd"].sem, 1)
                wait(dve, "rstd", b + 1)
                if cols_out is not None:
                    wait(dve, "turned", b + 1)
                for j in range(NT):
                    dst = xn[:, j, :] if gain_rows is not None or cols_out is not None else \
                        rows_out[:, bass.ds(b * NT + j, 1), :]
                    last = dve.tensor_scalar(dst, src[:, bass.ds(b * NT + j, 1), :], mv[:, j, 0:1],
                                             rstd[:, j:j + 1], ALU.subtract, ALU.mult)
                last.then_inc(ln["xn"].sem, 1)
                if gain_rows is not None:
                    wait(dve, "xn", b + 1)
                    dve.tensor_tensor(xg[:], xn[:], gain_rows, ALU.mult).then_inc(ln["gained"].sem, 1)
                    wait(dve, "gained", b + 1)
                    dve.tensor_tensor(xb[:], xg[:], bias_rows, ALU.add).then_inc(ln["biased"].sem, 1)
                    wait(dve, "biased", b + 1)
                    dve.tensor_tensor(rows_out[:, bass.ds(b * NT, NT), :], xb[:], add_to[:, bass.ds(b * NT, NT), :],
                                      ALU.add)

        @block.scalar
        def _(act):
            with act.Fori(0, B) as b:
                wait(act, "aggr", b + 1)
                act.activation(std[:], mv[:, :, 1], ACT.Sqrt, bias=eps_sb).then_inc(ln["sqrt"].sem, 1)
                if cols_out is not None:
                    wait(act, "turned", b + 2)
                    act.activation(cols_out(b), tp[:], ACT.Identity, bias=shift(b), scale=scale(b))\
                       .then_inc(ln["cols"].sem, 1)

        if cols_out is not None:
            @block.tensor
            def _(pe):
                with pe.Fori(0, B) as b:
                    wait(pe, "xn", b + 1)
                    wait(pe, "cols", b + 1)
                    for j in range(NT):
                        last = pe.transpose(tp[:, j * P:(j + 1) * P], xn[:, j, :], ident)
                    last.then_inc(ln["turned"].sem, 1)

    for what in ["stats", "aggr", "sqrt", "rstd", "xn"] + ["turned", "cols"] * (cols_out is not None) \
            + ["gained", "biased"] * (gain_rows is not None):
        ln[what].base += B


def attention(nc, name, h_cols, y, wqkv, wo, ident, ctx_cols=None, out_bias=None, masks=None, norm=None, q_scale=1.0,
              accumulate=True):
    causal = masks is not None
    NK = S if ctx_cols is None else CTX
    KT = NT if ctx_cols is None else 1
    kw = min(NK, P)
    U = 2 * NT

    def keys(qt):
        return (qt + 1) * P if causal else NK

    def ktiles(qt):
        return qt + 1 if causal else KT

    def queries(b):
        return h_cols[:, b * S:(b + 1) * S]

    def context(b):
        return queries(b) if ctx_cols is None else ctx_cols[:, b * CPAD:b * CPAD + CTX]

    def wait(eng, sem, n):
        if not isinstance(n, int) or n > 0:
            eng.wait_ge(sem, n)

    def turns(eng, turn):
        turn(0)
        with eng.Fori(1, NP - 1) as pair:
            turn(pair)
        turn(NP - 1)

    with ExitStack() as ctx:
        def sb(n, shape, dt=F32):
            return ctx.enter_context(nc.sbuf_tensor(f"{name}_{n}", shape, dt))

        def pb(n):
            return ctx.enter_context(nc.psum_tensor(f"{name}_{n}", [P, S], F32))

        def sem(n):
            return ctx.enter_context(nc.semaphore(f"{name}_{n}"))

        w_sb, wo_sb = sb("w_sb", [P, 3, P]), sb("wo_sb", [P, P])
        q_sb, k_sb, v_sb = sb("q_sb", [P, S]), sb("k_sb", [P, NK]), sb("v_sb", [P, KT, P])
        probs, probs_t = sb("probs", [P, 4, NK]), sb("probs_t", [P, 4, KT, P])
        o_sb = sb("o_sb", [P, S])
        negmax, total, rtotal = sb("negmax", [P, U]), sb("total", [P, U]), sb("rtotal", [P, U])
        sc = [pb(f"sc{i}") for i in range(4)]
        pt = [pb(f"pt{i}") for i in range(2)]
        ot, vb = pb("ot"), pb("vb")
        s_w, s_wo = sem("w"), sem("wo")
        s_pq, s_pk, s_pv = sem("pq"), sem("pk"), sem("pv")
        s_qe, s_ke, s_ve = sem("qe"), sem("ke"), sem("ve")
        s_sc, s_max, s_exp, s_rt, s_pn = sem("sc"), sem("max"), sem("exp"), sem("rt"), sem("pn")
        s_pt, s_pte, s_ot, s_oe, s_wd, s_y = sem("pt"), sem("pte"), sem("ot"), sem("oe"), sem("wd"), sem("y")
        s_y0 = sem("y0")
        if norm is not None:
            ones_half, qk_gain, eps_l2 = norm
            sq, rnorm = sb("sq", [P, 2, S]), sb("rnorm", [P, 2, S])
            s_sq, s_ss, s_ln, s_rn = sem("sq"), sem("ss"), sem("ln"), sem("rn")
        block = ctx.enter_context(nc.Block())

        @block.sync
        def _(sp):
            def turn(pair):
                wait(sp, s_pv, pair * B)
                sp.dma_start(w_sb[:], wqkv[bass.ds(pair, 1), :, :, :].rearrange("a p t n -> (a p) t n")).then_inc(s_w, 16)
                wait(sp, s_wd, pair * B)
                sp.dma_start(wo_sb[:], wo[bass.ds(pair, 1), :, :].rearrange("a p n -> (a p) n")).then_inc(s_wo, 16)

            turns(sp, turn)

        @block.tensor
        def _(pe):
            def project_qk(it, pair, b):
                wait(pe, s_w, pair * 16 + 16)
                wait(pe, s_exp, it * U - 2)
                pe.matmul(sc[0][:], w_sb[:, 0, :], queries(b), start=True, stop=True).then_inc(s_pq, 1)
                pe.matmul(sc[1][:, 0:NK], w_sb[:, 1, :], context(b), start=True, stop=True).then_inc(s_pk, 1)

            def project_v(it, b):
                wait(pe, s_ve, it)
                for kt in range(KT):
                    last = pe.matmul(vb[0:kw, kt * P:(kt + 1) * P], context(b)[:, kt * P:kt * P + kw], w_sb[:, 2, :],
                                     start=True, stop=True)
                last.then_inc(s_pv, 1)

            def square_sums(it):
                wait(pe, s_exp, it * U)
                for i in range(2):
                    wait(pe, s_sq, it * 2 + i + 1)
                    pe.matmul(sc[2 + i][:], ones_half, sq[:, i, :], start=True, stop=True).then_inc(s_ss, 1)

            def project_out(it, pair):
                wait(pe, s_oe, it + 1)
                wait(pe, s_wo, pair * 16 + 16)
                for j in range(NT):
                    last = pe.matmul(ot[:, j * P:(j + 1) * P], o_sb[:, j * P:(j + 1) * P], wo_sb[:], start=True, stop=True)
                last.then_inc(s_wd, 1)

            def scores(it, qt):
                for j in range(2):
                    u = 2 * qt + j
                    if u == 0:
                        wait(pe, s_qe, it + 1)
                        wait(pe, s_ke, it + 1)
                    else:
                        wait(pe, s_exp, it * U + u - 3)
                    bank = sc[u % 4]
                    last = pe.matmul(bank[:, 0:keys(qt)], q_sb[HD * j:HD * j + HD, qt * P:(qt + 1) * P],
                                     k_sb[HD * j:HD * j + HD, 0:keys(qt)], start=True, stop=not causal)
                    if causal:
                        last = pe.matmul(bank[:, qt * P:(qt + 1) * P], masks[0], masks[1], start=False, stop=True)
                    last.then_inc(s_sc, 1)

            def turn_probs(it, qt):
                for j in range(2):
                    u = 2 * qt + j
                    wait(pe, s_pn, it * U + u + 1)
                    wait(pe, s_pte, it * U + u - 1)
                    for kt in range(ktiles(qt)):
                        last = pe.transpose(pt[j][0:kw, kt * P:(kt + 1) * P], probs[:, u % 4, kt * P:kt * P + kw], ident)
                    last.then_inc(s_pt, 1)

            def values(it, qt):
                wait(pe, s_pte, it * U + 2 * qt + 2)
                if qt == 0:
                    wait(pe, s_ve, it + 1)
                    wait(pe, s_y, it)
                for kt in range(ktiles(qt)):
                    for j in range(2):
                        last = pe.matmul(ot[HD * j:HD * j + HD, qt * P:(qt + 1) * P], v_sb[0:kw, kt, HD * j:HD * j + HD],
                                         probs_t[0:kw, (2 * qt + j) % 4, kt, :], start=kt == 0,
                                         stop=kt == ktiles(qt) - 1, tile_position=(0, HD * j))
                if qt == NT - 1:
                    last.then_inc(s_ot, 1)

            def turn(pair):
                for b in range(B):
                    it = pair * B + b
                    first = isinstance(pair, int) and it == 0
                    final = isinstance(pair, int) and it == NP * B - 1
                    following = (it + 1, pair, b + 1) if b + 1 < B else (it + 1, pair + 1, 0)
                    before = pair if b else pair - 1
                    if first:
                        project_qk(0, 0, 0)
                        if norm is not None:
                            square_sums(0)
                    if norm is not None:
                        project_v(it, b)
                        if not first:
                            project_out(it - 1, before)
                    scores(it, 0)
                    scores(it, 1)
                    if norm is None:
                        project_v(it, b)
                        if not first:
                            project_out(it - 1, before)
                    turn_probs(it, 0)
                    scores(it, 2)
                    values(it, 0)
                    turn_probs(it, 1)
                    scores(it, 3)
                    values(it, 1)
                    turn_probs(it, 2)
                    if not final:
                        project_qk(*following)
                    values(it, 2)
                    turn_probs(it, 3)
                    if not final and norm is not None:
                        square_sums(it + 1)
                    values(it, 3)

            turns(pe, turn)
            project_out(NP * B - 1, NP - 1)

        @block.scalar
        def _(act):
            act.preload_act_table_set("natural_log_exp_and_others")

            def take_qk(it):
                if norm is None:
                    wait(act, s_pq, it + 1)
                    act.activation(q_sb[:], sc[0][:], ACT.Copy, scale=q_scale).then_inc(s_qe, 1)
                    wait(act, s_pk, it + 1)
                    act.activation(k_sb[:], sc[1][:, 0:NK], ACT.Copy).then_inc(s_ke, 1)
                else:
                    for i, projected in enumerate((s_pq, s_pk)):
                        wait(act, projected, it + 1)
                        act.activation(sq[:, i, :], sc[i][:], ACT.Square).then_inc(s_sq, 1)

            def norms(it):
                for i in range(2):
                    wait(act, s_ss, it * 2 + i + 1)
                    wait(act, (s_qe, s_ke)[i], it)
                    act.activation(rnorm[:, i, :], sc[2 + i][:], ACT.Ln, bias=eps_l2[i],
                                   scale=(q_scale ** -2, 1.0)[i]).then_inc(s_ln, 1)
                    wait(act, s_ln, it * 2 + i + 1)
                    act.activation(rnorm[:, i, :], rnorm[:, i, :], ACT.Exp, scale=-0.5).then_inc(s_rn, 1)

            def exps(it, qt):
                for j in range(2):
                    u = 2 * qt + j
                    wait(act, s_max, it * U + u + 1)
                    act.activation(probs[:, u % 4, 0:keys(qt)], sc[u % 4][:, 0:keys(qt)], ACT.Exp,
                                   bias=negmax[:, u:u + 1], accum_out=total[:, u:u + 1]).then_inc(s_exp, 1)

            def take_turned(it, qt):
                for j in range(2):
                    u = 2 * qt + j
                    wait(act, s_pt, it * U + u + 1)
                    act.activation(probs_t[0:kw, u % 4, 0:ktiles(qt), :],
                                   pt[j][0:kw, 0:ktiles(qt) * P].rearrange("p (t q) -> p t q", q=P),
                                   ACT.Copy).then_inc(s_pte, 1)

            def turn(pair):
                for b in range(B):
                    it = pair * B + b
                    final = isinstance(pair, int) and it == NP * B - 1
                    exps(it, 0)
                    exps(it, 1)
                    wait(act, s_pv, it + 1)
                    act.activation(v_sb[0:kw, :, :], vb[0:kw, 0:KT * P].rearrange("p (t d) -> p t d", d=P), ACT.Copy)\
                       .then_inc(s_ve, 1)
                    take_turned(it, 0)
                    exps(it, 2)
                    take_turned(it, 1)
                    exps(it, 3)
                    take_turned(it, 2)
                    if not final:
                        take_qk(it + 1)
                    take_turned(it, 3)
                    if not final and norm is not None:
                        norms(it + 1)

            take_qk(0)
            if norm is not None:
                norms(0)
            turns(act, turn)

        @block.vector
        def _(dve):
            def maxima(it, qt):
                for j in range(2):
                    u = 2 * qt + j
                    wait(dve, s_sc, it * U + u + 1)
                    dve.tensor_reduce(negmax[:, u:u + 1], sc[u % 4][:, 0:keys(qt)], axis=AX.X, op=ALU.max,
                                      negate=True).then_inc(s_max, 1)

            def normalise(it, qt):
                u = 2 * qt
                wait(dve, s_exp, it * U + u + 2)
                dve.reciprocal(rtotal[:, u:u + 2], total[:, u:u + 2]).then_inc(s_rt, 1)
                wait(dve, s_rt, it * NT + qt + 1)
                for j in range(2):
                    dve.tensor_scalar(probs[:, (u + j) % 4, 0:keys(qt)], probs[:, (u + j) % 4, 0:keys(qt)],
                                      rtotal[:, u + j:u + j + 1], None, ALU.mult).then_inc(s_pn, 1)

            def scale_qk(it, pair):
                for i, (to, done) in enumerate(((q_sb, s_qe), (k_sb, s_ke))):
                    wait(dve, s_rn, it * 2 + i + 1)
                    dve.scalar_tensor_tensor(out=to[:], in0=sc[i][:], scalar=qk_gain[i][:, bass.ds(pair, 1)],
                                             in1=rnorm[:, i, :], op0=ALU.mult, op1=ALU.mult).then_inc(done, 1)

            def add_out(it, b):
                wait(dve, s_wd, it + 1)
                wait(dve, s_y, it + 1 - B)
                out = y[:, b * NT:(b + 1) * NT, :]
                dve.tensor_tensor(out, out, ot[:].rearrange("p (t d) -> p t d", d=P), ALU.add).then_inc(s_y, 1)

            def turn(pair):
                for b in range(B):
                    it = pair * B + b
                    first = isinstance(pair, int) and it == 0
                    final = isinstance(pair, int) and it == NP * B - 1
                    maxima(it, 0)
                    maxima(it, 1)
                    normalise(it, 0)
                    if not first:
                        add_out(it - 1, (b - 1) % B)
                    maxima(it, 2)
                    normalise(it, 1)
                    maxima(it, 3)
                    normalise(it, 2)
                    normalise(it, 3)
                    wait(dve, s_ot, it + 1)
                    dve.tensor_copy(o_sb[:], ot[:]).then_inc(s_oe, 1)
                    if not final and norm is not None:
                        scale_qk(it + 1, pair if b + 1 < B else pair + 1)

            if not accumulate:
                dve.memset(y[:], 0.0).then_inc(s_y0, 1)
                dve.wait_ge(s_y0, 1)
            elif out_bias is not None:
                dve.tensor_tensor(y[:], y[:], out_bias.rearrange("p (a d) -> p a d", a=1).broadcast_to([P, B * NT, P]),
                                  ALU.add).then_inc(s_y0, 1)
                dve.wait_ge(s_y0, 1)
            if norm is not None:
                scale_qk(0, 0)
            turns(dve, turn)
            add_out(NP * B - 1, B - 1)


def feed_forward(nc, h_cols, y, w1, b1, w2, b2_rows):
    with ExitStack() as ctx:
        def sb(n, shape):
            return ctx.enter_context(nc.sbuf_tensor(f"ff_{n}", shape, F32))

        def pb(n):
            return ctx.enter_context(nc.psum_tensor(f"ff_{n}", [P, S], F32))

        def sem(n):
            return ctx.enter_context(nc.semaphore(f"ff_{n}"))

        w1_sb, b1_sb, w2_sb = sb("w1_sb", [P, 2 * FC * P]), sb("b1_sb", [P, 2 * FC]), sb("w2_sb", [P, FC, P])
        gate, hidden = sb("gate", [P, 2, S]), sb("hidden", [P, FC, S])
        up, gt, down = [pb("up0"), pb("up1")], [pb("gt0"), pb("gt1")], pb("down")
        s_w, s_up, s_gelu, s_hid, s_down, s_y, s_y0 = (sem(n) for n in ("w", "up", "gelu", "hid", "down", "y", "y0"))
        block = ctx.enter_context(nc.Block())

        @block.sync
        def _(sp):
            sp.dma_start(w1_sb[:], w1).then_inc(s_w, 16)
            sp.dma_start(b1_sb[:], b1).then_inc(s_w, 16)
            sp.dma_start(w2_sb[:], w2).then_inc(s_w, 16)

        @block.tensor
        def _(pe):
            pe.sem_inc(s_down, 1)
            pe.wait_ge(s_w, 48)
            with pe.Fori(0, B) as b:
                for f in range(FC):
                    pe.wait_ge(s_hid, b * FC + max(f - 1, 0) + 1)
                    pe.matmul(up[f % 2][:], w1_sb[:, f * P:(f + 1) * P], h_cols[:, bass.ds(b * S, S)],
                              start=True, stop=True)
                    pe.matmul(gt[f % 2][:], w1_sb[:, (FC + f) * P:(FC + f + 1) * P], h_cols[:, bass.ds(b * S, S)],
                              start=True, stop=True).then_inc(s_up, 1)
                pe.wait_ge(s_y, b + 1)
                for f in range(FC):
                    pe.wait_ge(s_hid, b * FC + f + 2)
                    for j in range(NT):
                        last = pe.matmul(down[:, j * P:(j + 1) * P], hidden[:, f, j * P:(j + 1) * P], w2_sb[:, f, :],
                                         start=f == 0 and j == 0, stop=f == FC - 1, skip_group_check=True)
                last.then_inc(s_down, 1)

        @block.scalar
        def _(act):
            act.wait_ge(s_w, 48)
            with act.Fori(0, B) as b:
                for f in range(FC):
                    act.wait_ge(s_up, b * FC + f + 1)
                    if f >= 2:
                        act.wait_ge(s_hid, b * FC + f)
                    act.activation(gate[:, f % 2, :], gt[f % 2][:], ACT.Gelu, bias=b1_sb[:, FC + f:FC + f + 1])\
                       .then_inc(s_gelu, 1)

        @block.vector
        def _(dve):
            dve.sem_inc(s_hid, 1)
            dve.sem_inc(s_y, 1)
            dve.tensor_tensor(y[:], y[:], b2_rows.rearrange("p (a d) -> p a d", a=1).broadcast_to([P, B * NT, P]), ALU.add)\
               .then_inc(s_y0, 1)
            dve.wait_ge(s_y0, 1)
            dve.wait_ge(s_w, 48)
            with dve.Fori(0, B) as b:
                for f in range(FC):
                    dve.wait_ge(s_gelu, b * FC + f + 1)
                    if f == 0:
                        dve.wait_ge(s_down, b + 1)
                    dve.scalar_tensor_tensor(out=hidden[:, f, :], in0=up[f % 2][:], scalar=b1_sb[:, f:f + 1],
                                             in1=gate[:, f % 2, :], op0=ALU.add, op1=ALU.mult).then_inc(s_hid, 1)
                dve.wait_ge(s_down, b + 2)
                out = y[:, bass.ds(b * NT, NT), :]
                dve.tensor_tensor(out, out, down[:].rearrange("p (t d) -> p t d", d=P), ALU.add).then_inc(s_y, 1)


def experts(nc, name, h_cols, acc, gates, w1, b1, w2, gelu):
    with ExitStack() as ctx:
        def sb(n, shape):
            return ctx.enter_context(nc.sbuf_tensor(f"{name}_{n}", shape, F32))

        def pb(n):
            return ctx.enter_context(nc.psum_tensor(f"{name}_{n}", [P, S], F32))

        def sem(n):
            return ctx.enter_context(nc.semaphore(f"{name}_{n}"))

        w1_sb, w2_sb, b1_sb = sb("w1_sb", [P, 2, FC * P]), sb("w2_sb", [P, 2, FC, P]), sb("b1_sb", [P, 2, FC])
        hidden = sb("hidden", [P, FC, S])
        up, down = [pb("up0"), pb("up1")], pb("down")
        s_w, s_down = [sem("w0"), sem("w1")], [sem("done0"), sem("done1")]
        s_up, s_gelu, s_acc = sem("up"), sem("gelu"), sem("acc")
        loads = 2 + (b1 is not None)
        block = ctx.enter_context(nc.Block())

        @block.sync
        def _(sp):
            with sp.Fori(0, E // 2) as turn:
                for k in range(2):
                    e = turn * 2 + k
                    sp.wait_ge(s_down[k], turn * B + 1)
                    sp.dma_start(w1_sb[:, k, :], w1[bass.ds(e, 1), :, :].rearrange("a p n -> (a p) n")).then_inc(s_w[k], 16)
                    sp.dma_start(w2_sb[:, k, :, :], w2[bass.ds(e, 1), :, :, :].rearrange("a p f n -> (a p) f n"))\
                      .then_inc(s_w[k], 16)
                    if b1 is not None:
                        sp.dma_start(b1_sb[:, k, :], b1[bass.ds(e, 1), :, :].rearrange("a p n -> (a p) n"))\
                          .then_inc(s_w[k], 16)

        @block.tensor
        def _(pe):
            pe.sem_inc(s_down[0], 1)
            pe.sem_inc(s_down[1], 1)
            with pe.Fori(0, E // 2) as turn:
                for k in range(2):
                    with pe.Fori(0, B) as b:
                        pe.wait_ge(s_w[k], 16 * loads * turn + 16 * loads)
                        n = (turn * 2 + k) * B + b
                        for f in range(FC):
                            pe.wait_ge(s_gelu, n * FC + max(f - 1, 0) + 1)
                            pe.matmul(up[f % 2][:], w1_sb[:, k, f * P:(f + 1) * P], h_cols[:, bass.ds(b * S, S)],
                                      start=True, stop=True).then_inc(s_up, 1)
                        pe.wait_ge(s_acc, n + 1)
                        for f in range(FC):
                            pe.wait_ge(s_gelu, n * FC + f + 2)
                            for j in range(NT):
                                last = pe.matmul(down[:, j * P:(j + 1) * P], hidden[:, f, j * P:(j + 1) * P],
                                                 w2_sb[:, k, f, :], start=f == 0 and j == 0, stop=f == FC - 1,
                                                 skip_group_check=True)
                        last.then_inc(s_down[k], 1)

        @block.scalar
        def _(act):
            act.sem_inc(s_gelu, 1)
            with act.Fori(0, E // 2) as turn:
                for k in range(2):
                    with act.Fori(0, B) as b:
                        act.wait_ge(s_w[k], 16 * loads * turn + 16 * loads)
                        n = (turn * 2 + k) * B + b
                        for f in range(FC):
                            act.wait_ge(s_up, n * FC + f + 1)
                            act.activation(hidden[:, f, :], up[f % 2][:], gelu,
                                           bias=b1_sb[:, k, f:f + 1] if b1 is not None else 0.0).then_inc(s_gelu, 1)

        @block.vector
        def _(dve):
            dve.sem_inc(s_acc, 1)
            with dve.Fori(0, E // 2) as turn:
                for k in range(2):
                    with dve.Fori(0, B) as b:
                        dve.wait_ge(s_down[k], turn * B + b + 2)
                        dve.wait_ge(s_acc, (turn * 2 + k) * B + b + 1)
                        for j in range(NT):
                            out = acc[:, bass.ds(b * NT + j, 1), :].rearrange("p a d -> p (a d)")
                            last = dve.scalar_tensor_tensor(out=out, in0=down[:, j * P:(j + 1) * P],
                                                            scalar=gates[:, bass.ds((b * NT + j) * E + turn * 2 + k, 1)],
                                                            in1=out, op0=ALU.mult, op1=ALU.add)
                        last.then_inc(s_acc, 1)


def gating(nc, name, h_cols, gates, gw, gb_rows, ident, acc=None, b2=None):
    NTT = B * NT
    with ExitStack() as ctx:
        def sb(n, shape):
            return ctx.enter_context(nc.sbuf_tensor(f"{name}_{n}", shape, F32))

        def pb(n):
            return ctx.enter_context(nc.psum_tensor(f"{name}_{n}", [P, S], F32))

        def sem(n):
            return ctx.enter_context(nc.semaphore(f"{name}_{n}"))

        logits, shifted = sb("logits", [P, NTT, E]), sb("shifted", [P, NTT, E])
        expd = sb("expd", [P, NTT, E])
        top, total, rtotal = sb("top", [P, NTT]), sb("total", [P, NTT]), sb("rtotal", [P, NTT])
        lg = pb("lg")
        tp = [pb(f"tp{i}") for i in range(4)]
        s_lg, s_step, s_exp, s_g, s_tp, s_ev, s_mm = (sem(n) for n in ("lg", "step", "exp", "g", "tp", "ev", "mm"))
        g3 = gates.rearrange("p (t e) -> p t e", e=E)
        if b2 is not None:
            gates_t = sb("gates_t", [E, NTT * P])
        else:
            ranked = [sb(f"ranked{i}", [B * E, S]) for i in range(2)]
            kept, top8 = sb("kept", [B * E, S]), sb("top8", [B * E, 8])
            probs = sb("probs", [P, NTT, E])
        block = ctx.enter_context(nc.Block())

        @block.tensor
        def _(pe):
            for i in range(NTT):
                last = pe.matmul(lg[:, i * E:(i + 1) * E], h_cols[:, i * P:(i + 1) * P], gw, start=True, stop=True)
            last.then_inc(s_lg, 1)
            pe.wait_ge(s_g, 1)
            if b2 is not None:
                for i in range(NTT):
                    last = pe.transpose(tp[i // NT][0:E, i % NT * P:(i % NT + 1) * P], gates[:, i * E:(i + 1) * E],
                                        ident)
                last.then_inc(s_tp, 1)
                pe.wait_ge(s_ev, 1)
                for i in range(NTT):
                    last = pe.matmul(tp[i // NT][:, i % NT * P:(i % NT + 1) * P], gates_t[:, i * P:(i + 1) * P], b2,
                                     start=True, stop=True)
                last.then_inc(s_mm, 1)
            else:
                for j in range(NT):
                    last = pe.transpose(tp[0][0:B * E, j * P:(j + 1) * P], shifted[:, j * B:(j + 1) * B, :]
                                        .rearrange("p t e -> p (t e)"), ident)
                last.then_inc(s_tp, 1)
                pe.wait_ge(s_ev, 1)
                for j in range(NT):
                    last = pe.transpose(tp[1][:, j * B * E:(j + 1) * B * E], kept[:, j * P:(j + 1) * P],
                                        ident[0:B * E, 0:B * E])
                last.then_inc(s_mm, 1)

        @block.scalar
        def _(act):
            act.wait_ge(s_step, 3)
            act.activation(expd[:], shifted[:], ACT.Exp).then_inc(s_exp, 1)

        @block.vector
        def _(dve):
            done = 0

            def mine(instruction):
                nonlocal done
                done += 1
                instruction.then_inc(s_step, 1)
                dve.wait_ge(s_step, done)

            dve.wait_ge(s_lg, 1)
            raw = lg[:, 0:NTT * E].rearrange("p (t e) -> p t e", e=E)
            if gb_rows is not None:
                bias = gb_rows.rearrange("p (a e) -> p a e", a=1).broadcast_to([P, NTT, E])
                mine(dve.tensor_tensor(logits[:], raw, bias, ALU.add))
            else:
                mine(dve.tensor_copy(logits[:], raw))
            mine(dve.tensor_reduce(top[:], logits[:], axis=AX.X, op=ALU.max))

            def spread(x):
                return x.rearrange("p (t a) -> p t a", a=1).broadcast_to([P, NTT, E])

            mine(dve.tensor_tensor(shifted[:], logits[:], spread(top[:]), ALU.subtract))
            dve.wait_ge(s_exp, 1)
            mine(dve.tensor_reduce(total[:], expd[:], axis=AX.X, op=ALU.add))
            mine(dve.reciprocal(rtotal[:], total[:]))
            if b2 is not None:
                dve.tensor_tensor(g3, expd[:], spread(rtotal[:]), ALU.mult).then_inc(s_g, 1)
                dve.wait_ge(s_tp, 1)
                for b in range(B):
                    last = dve.tensor_copy(gates_t[:, b * S:(b + 1) * S], tp[b][0:E, :])
                last.then_inc(s_ev, 1)
                dve.wait_ge(s_mm, 1)
                for b in range(B):
                    dve.tensor_copy(acc[:, b * NT:(b + 1) * NT, :], tp[b][:].rearrange("p (t d) -> p t d", d=P))
            else:
                mine(dve.tensor_tensor(probs[:], expd[:], spread(rtotal[:]), ALU.mult))
                dve.tensor_copy(shifted[:].rearrange("p (j b) e -> p b j e", b=B),
                                probs[:].rearrange("p (b j) e -> p b j e", b=B)).then_inc(s_g, 1)
                dve.wait_ge(s_tp, 1)
                mine(dve.tensor_copy(ranked[0][:], tp[0][0:B * E, :]))
                for r in range(TOPK // 8):
                    mine(dve.max(top8[:], ranked[r % 2][:]))
                    mine(dve.match_replace(ranked[(r + 1) % 2][:], top8[:], ranked[r % 2][:], -1.0))
                dve.tensor_scalar(kept[:], ranked[TOPK // 8 % 2][:], 0.0, None, ALU.is_lt).then_inc(s_ev, 1)
                dve.wait_ge(s_mm, 1)
                dve.tensor_tensor(g3.rearrange("p (b j) e -> p b j e", b=B), probs[:].rearrange("p (b j) e -> p b j e", b=B),
                                  tp[1][:, 0:NTT * E].rearrange("p (j b e) -> p b j e", b=B, e=E), ALU.mult)


def recurrence_tables(nc, name, ctx_t, ctx_k, w_t, k_ctx, bias_rows, is_key, score_w, gate_w):
    with ExitStack() as ctx:
        s_mm = ctx.enter_context(nc.semaphore(f"{name}_mm"))
        ps = [ctx.enter_context(nc.psum_tensor(f"{name}_ps{i}", [P, BANK], F32)) for i in range(4)]
        block = ctx.enter_context(nc.Block())

        @block.tensor
        def _(pe):
            pe.matmul(ps[0][:, 0:B * CPAD], w_t, ctx_t, start=True, stop=True).then_inc(s_mm, 1)
            for k in range(3):
                pe.matmul(ps[1 + k][:, 0:3 * P], ctx_k[:, k * P:(k + 1) * P], k_ctx, start=True, stop=True)\
                  .then_inc(s_mm, 1)

        @block.vector
        def _(dve):
            dve.wait_ge(s_mm, 1)
            dve.tensor_copy(score_w, ps[0][:, 0:B * CPAD])
            for k in range(3):
                dve.wait_ge(s_mm, 2 + k)
                dve.scalar_tensor_tensor(out=gate_w[:, k, :], in0=bias_rows, scalar=is_key[:, k:k + 1],
                                         in1=ps[1 + k][:, 0:3 * P], op0=ALU.mult, op1=ALU.add)


def recurrence(nc, x_t, score_w, gate_w, r_w, x_w, mask_l, mask_r, spread, h0_t, h0_c, history):
    with ExitStack() as ctx:
        def sb(n, w, rows=P):
            return ctx.enter_context(nc.sbuf_tensor(f"gru_{n}", [rows, w], F32))

        def pb(n):
            return ctx.enter_context(nc.psum_tensor(f"gru_{n}", [P, BANK], F32))

        def sem(n):
            return ctx.enter_context(nc.semaphore(f"gru_{n}"))

        h, h_t, xs = sb("h", 32), sb("h_t", 32), sb("xs", B)
        p, p_t = sb("p", CPAD), sb("p_t", CPAD)
        negmax, total, rtotal = sb("negmax", 1), sb("total", 2), sb("rtotal", 1)
        own = sb("own", 4 * 32)
        pre_r, pre_z, th_r, th_z = sb("pre_r", 32), sb("pre_z", 32), sb("th_r", 32), sb("th_z", 32)
        pre_c, r_hh, c_in, cand = sb("pre_c", 32), sb("r_hh", 32), sb("c_in", 32), sb("cand", 32)
        h_half, z_h, new = sb("h_half", 32), sb("z_h", 32), sb("new", 32)
        ps_s, ps_own, ps_r, ps_z, ps_c, ps_t = (pb(n) for n in ("ps_s", "ps_own", "ps_r", "ps_z", "ps_c", "ps_t"))
        (s_init, s_load, s_table, s_score, s_x, s_ownmm, s_total, s_rmm, s_cmm, s_zmm, s_max, s_exp, s_pt, s_rt, s_own,
         s_xs, s_prer, s_thr, s_prec, s_rhh, s_cin, s_cand, s_prez, s_thz, s_hhalf, s_zh, s_new, s_h, s_ht, s_hist) = (
            sem(n) for n in ("init", "load", "table", "score", "x", "ownmm", "total", "rmm", "cmm", "zmm", "max", "exp",
                             "pt", "rt", "own", "xs", "prer", "thr", "prec", "rhh", "cin", "cand", "prez", "thz", "hhalf",
                             "zh", "new", "h", "ht", "hist"))
        block = ctx.enter_context(nc.Block())
        U = STEPS_PER_TURN

        @block.sync
        def _(sp):
            sp.dma_start(h_t[:, 0:B], h0_t).then_inc(s_load, 16)
            sp.dma_start(h[:], h0_c).then_inc(s_load, 16)

        @block.gpsimd
        def _(pool):
            pool.sem_inc(s_hist, 1)
            pool.tensor_copy(xs[:], x_t[:, 0:B]).then_inc(s_xs, 1)
            with pool.Fori(0, S // U) as turn:
                for k in range(U):
                    t = turn * U + k
                    pool.wait_ge(s_x, t + 1)
                    pool.tensor_copy(xs[:], x_t[:, bass.ds((t + 1) * B, B)]).then_inc(s_xs, 1)
                    pool.wait_ge(s_ht, t + 2)
                    pool.tensor_copy(history[:, bass.ds(t * B, B)], h_t[:, 0:B]).then_inc(s_hist, 1)

        @block.tensor
        def _(pe):
            pe.wait_ge(s_init, 6)
            pe.wait_ge(s_load, 32)
            with pe.Fori(0, S // U) as turn:
                for k in range(U):
                    t = turn * U + k
                    pe.wait_ge(s_xs, t + 1)
                    pe.wait_ge(s_own, t + 1)
                    pe.matmul(ps_s[:, 0:CPAD], mask_l, mask_r, start=True, stop=False)
                    for c in range(4):
                        last = pe.matmul(ps_own[32 * c:32 * c + B, 0:P], xs[:], x_w[:, c, :], start=True, stop=False,
                                         tile_position=(0, 32 * c))
                    last.then_inc(s_x, 1)
                    pe.wait_ge(s_ht, t + 1)
                    for b in range(B):
                        last = pe.matmul(ps_s[32 * b:32 * b + B, 0:80], h_t[:, 0:B], score_w[:, b, 0:80], start=False,
                                         stop=True, tile_position=(0, 32 * b))
                    last.then_inc(s_score, 1)
                    for c in range(4):
                        last = pe.matmul(ps_own[32 * c:32 * c + B, 0:96], h_t[:, 0:B], r_w[:, c, :], start=False,
                                         stop=True, tile_position=(0, 32 * c))
                    last.then_inc(s_ownmm, 1)
                    pe.wait_ge(s_exp, t + 1)
                    for c in range(4):
                        last = pe.matmul(ps_t[32 * c:32 * c + B, 0:2], spread, total[:], start=True, stop=True,
                                         tile_position=(0, 32 * c))
                    last.then_inc(s_total, 1)
                    pe.wait_ge(s_pt, t + 1)
                    for lo, bank, done in ((0, ps_r, s_rmm), (64, ps_c, s_cmm), (32, ps_z, s_zmm)):
                        for k3 in range(3):
                            for c in range(4):
                                last = pe.matmul(bank[32 * c:32 * c + B, 0:32], p_t[:, 32 * k3:32 * k3 + B],
                                                 gate_w[:, k3, 96 * c + lo:96 * c + lo + 32], start=k3 == 0,
                                                 stop=k3 == 2, tile_position=(0, 32 * c))
                        last.then_inc(done, 1)

        @block.scalar
        def _(act):
            act.wait_ge(s_load, 32)
            act.activation(cand[:], h[:], ACT.Exp).then_inc(s_table, 1)
            act.wait_ge(s_table, 1)
            with act.Fori(0, S // U) as turn:
                for k in range(U):
                    t = turn * U + k
                    act.wait_ge(s_max, t + 1)
                    act.activation(p[:], ps_s[:, 0:CPAD], ACT.Exp, bias=negmax[:, 0:1], accum_out=total[:, 0:1])\
                       .then_inc(s_exp, 1)
                    act.wait_ge(s_prer, t + 1)
                    act.activation(th_r[:], pre_r[:], ACT.Tanh, scale=0.5).then_inc(s_thr, 1)
                    act.wait_ge(s_cin, t + 1)
                    act.activation(cand[:], c_in[:], ACT.Tanh).then_inc(s_cand, 1)
                    act.wait_ge(s_prez, t + 1)
                    act.activation(th_z[:], pre_z[:], ACT.Tanh, scale=0.5).then_inc(s_thz, 1)

        @block.vector
        def _(dve):
            dve.sem_inc(s_own, 1)
            dve.sem_inc(s_ht, 1)
            dve.memset(ps_r[:], 0.0).then_inc(s_init, 1)
            dve.memset(ps_c[:], 0.0).then_inc(s_init, 1)
            dve.memset(ps_z[:], 0.0).then_inc(s_init, 1)
            dve.memset(ps_own[:], 0.0).then_inc(s_init, 1)
            dve.memset(ps_t[:], 1.0).then_inc(s_init, 1)
            dve.memset(total[:], 1.0).then_inc(s_init, 1)
            dve.wait_ge(s_load, 32)
            dve.tensor_scalar(h_half[:], h[:], 0.5, None, ALU.mult).then_inc(s_hhalf, 1)
            with dve.Fori(0, S // U) as turn:
                for k in range(U):
                    t = turn * U + k
                    dve.wait_ge(s_score, t + 1)
                    dve.tensor_reduce(negmax[:], ps_s[:, 0:78], axis=AX.X, op=ALU.max, negate=True).then_inc(s_max, 1)
                    dve.wait_ge(s_exp, t + 1)
                    dve.transpose(p_t[:], p[:]).then_inc(s_pt, 1)
                    dve.wait_ge(s_ownmm, t + 1)
                    dve.tensor_copy(own[:], ps_own[:, 0:P]).then_inc(s_own, 1)
                    dve.wait_ge(s_total, t + 1)
                    dve.reciprocal(rtotal[:], ps_t[:, 0:1]).then_inc(s_rt, 1)
                    dve.wait_ge(s_rmm, t + 1)
                    dve.wait_ge(s_rt, t + 1)
                    dve.scalar_tensor_tensor(out=pre_r[:], in0=ps_r[:, 0:32], scalar=rtotal[:, 0:1], in1=own[:, 32:64],
                                             op0=ALU.mult, op1=ALU.add).then_inc(s_prer, 1)
                    dve.wait_ge(s_cmm, t + 1)
                    dve.scalar_tensor_tensor(out=pre_c[:], in0=ps_c[:, 0:32], scalar=rtotal[:, 0:1], in1=own[:, 96:P],
                                             op0=ALU.mult, op1=ALU.add).then_inc(s_prec, 1)
                    dve.wait_ge(s_thr, t + 1)
                    dve.scalar_tensor_tensor(out=r_hh[:], in0=th_r[:], scalar=1.0, in1=own[:, 0:32], op0=ALU.add,
                                             op1=ALU.mult).then_inc(s_rhh, 1)
                    dve.wait_ge(s_rhh, t + 1)
                    dve.scalar_tensor_tensor(out=c_in[:], in0=r_hh[:], scalar=0.5, in1=pre_c[:], op0=ALU.mult,
                                             op1=ALU.add).then_inc(s_cin, 1)
                    dve.wait_ge(s_zmm, t + 1)
                    dve.wait_ge(s_hist, t + 1)
                    dve.scalar_tensor_tensor(out=pre_z[:], in0=ps_z[:, 0:32], scalar=rtotal[:, 0:1], in1=own[:, 64:96],
                                             op0=ALU.mult, op1=ALU.add).then_inc(s_prez, 1)
                    dve.wait_ge(s_thz, t + 1)
                    dve.wait_ge(s_hhalf, t + 1)
                    dve.scalar_tensor_tensor(out=z_h[:], in0=th_z[:], scalar=1.0, in1=h_half[:], op0=ALU.add,
                                             op1=ALU.mult).then_inc(s_zh, 1)
                    dve.scalar_tensor_tensor(out=new[:], in0=th_z[:], scalar=1.0, in1=cand[:], op0=ALU.subtract,
                                             op1=ALU.mult).then_inc(s_new, 1)
                    dve.wait_ge(s_new, t + 1)
                    dve.scalar_tensor_tensor(out=h[:], in0=new[:], scalar=-0.5, in1=z_h[:], op0=ALU.mult,
                                             op1=ALU.add).then_inc(s_h, 1)
                    dve.wait_ge(s_h, t + 1)
                    dve.transpose(h_t[:], h[:]).then_inc(s_ht, 1)
                    dve.tensor_scalar(h_half[:], h[:], 0.5, None, ALU.mult).then_inc(s_hhalf, 1)


def add_history(nc, x, history, ident):
    with ExitStack() as ctx:
        s_tp = ctx.enter_context(nc.semaphore("hist_tp"))
        tp = [ctx.enter_context(nc.psum_tensor(f"hist_tp{b}", [P, S], F32)) for b in range(B)]
        block = ctx.enter_context(nc.Block())
        by_batch = history.rearrange("p (t b) -> p b t", b=B)

        @block.tensor
        def _(pe):
            for b in range(B):
                for j in range(NT):
                    last = pe.transpose(tp[b][:, j * P:(j + 1) * P], by_batch[:, b, j * P:(j + 1) * P], ident)
                last.then_inc(s_tp, 1)

        @block.vector
        def _(dve):
            for b in range(B):
                dve.wait_ge(s_tp, b + 1)
                rows = x[:, b * NT:(b + 1) * NT, :]
                dve.tensor_tensor(rows, rows, tp[b][:].rearrange("p (t d) -> p t d", d=P), ALU.add)


def condition_columns(nc, cond_t, norm_w, norm_b, columns):
    with ExitStack() as ctx:
        s_mm = ctx.enter_context(nc.semaphore("cond_mm"))
        ps = ctx.enter_context(nc.psum_tensor("cond_ps", [P, S], F32))
        block = ctx.enter_context(nc.Block())

        @block.tensor
        def _(pe):
            for i in range(6):
                last = pe.matmul(ps[:, i * B:(i + 1) * B], norm_w[:, i * P:(i + 1) * P], cond_t, start=True, stop=True)
            last.then_inc(s_mm, 1)

        @block.vector
        def _(dve):
            dve.wait_ge(s_mm, 1)
            for i in range(6):
                dve.tensor_scalar(columns[:, i * B:(i + 1) * B], ps[:, i * B:(i + 1) * B], norm_b[:, i:i + 1],
                                  1.0 if i % 2 == 0 else 0.0, ALU.add, ALU.add)


def program(nc, a, out, probe=None):
    with ExitStack() as ctx:
        def sb(n, shape, dt=F32):
            return ctx.enter_context(nc.sbuf_tensor(n, shape, dt))

        ln = {n: Counted(ctx.enter_context(nc.semaphore(f"ln_{n}")))
              for n in ("stats", "aggr", "sqrt", "rstd", "xn", "turned", "cols", "gained", "biased")}
        s_in = ctx.enter_context(nc.semaphore("in"))
        s_out = ctx.enter_context(nc.semaphore("out"))
        x, y = sb("x", [P, B * NT, P]), sb("y", [P, B * NT, P])
        h_cols = sb("h_cols", [P, B * S])
        columns = sb("columns", [P, 6 * B])
        gates = sb("gates", [P, B * NT * E])
        resident = {}
        for n in ("ident", "masks", "eps", "ones_half", "cond_t", "norm_w", "norm_b", "ctx_t", "ctx_k", "bo1_rows", "bo2_rows",
                  "ffb2_rows", "ln_cols", "g_rows", "b_rows", "qk_gain", "gate_w", "gate_b_rows", "b2", "gw2",
                  "w_t", "k_ctx", "r_w", "x_w", "bias_rows", "mask_l", "mask_r", "is_key", "spread"):
            resident[n] = sb(f"c_{n}", list(a[n].shape))
        c = {n: t[:] for n, t in resident.items()}
        narrow = {n: sb(f"b_{n}", list(a[n].shape), BF16) for n in ("masks", "mask_l", "mask_r")}
        x_dram = a["x"].rearrange("(n p) d -> p n d", p=P)
        with nc.Block() as block:
            @block.scalar
            def _(act):
                act.sem_inc(ln["cols"].sem, 1)

            @block.tensor
            def _(pe):
                pe.sem_inc(ln["turned"].sem, 1)

            @block.sync
            def _(sp):
                sp.dma_start(x[:], x_dram).then_inc(s_in, 16)
                for n in resident:
                    sp.dma_start(c[n], a[n]).then_inc(s_in, 16)
                sp.wait_ge(s_in, 16 * (1 + len(resident)))

            @block.vector
            def _(dve):
                dve.wait_ge(s_in, 16 * (1 + len(resident)))
                for n, t in narrow.items():
                    dve.tensor_copy(t[:], c[n])
        c.update({n: t[:] for n, t in narrow.items()})
        ident, eps = c["ident"], c["eps"][:, 0:1]
        g_rows = c["g_rows"].rearrange("p (a d) -> p a d", a=1).broadcast_to([P, NT, P])
        b_rows = c["b_rows"].rearrange("p (a d) -> p a d", a=1).broadcast_to([P, NT, P])
        masks = (c["masks"][:, 0:P], c["masks"][:, P:2 * P])

        def columns_of(layer):
            return (lambda b: columns[:, bass.ds(b + (2 * layer) * B, 1)],
                    lambda b: columns[:, bass.ds(b + (2 * layer + 1) * B, 1)])

        def by_batch(b):
            return h_cols[:, bass.ds(b * S, S)]

        gain, bias = (lambda b: c["ln_cols"][:, 0:1]), (lambda b: c["ln_cols"][:, 1:2])
        one, zero = (lambda b: c["eps"][:, 2:3]), (lambda b: c["eps"][:, 3:4])

        condition_columns(nc, c["cond_t"], c["norm_w"], c["norm_b"], columns)
        layer_norm(nc, ln, "ln_a", x, eps, ident, rows_out=y)
        scale, shift = columns_of(0)
        layer_norm(nc, ln, "ln_b", y, eps, ident, cols_out=by_batch, scale=scale, shift=shift)
        if probe and probe(nc, 1, h_cols[:]): return
        attention(nc, "self", h_cols, y, a["wqkv1"], a["wo1"], ident, out_bias=c["bo1_rows"], q_scale=HD ** -0.5)
        if probe and probe(nc, 2, y[:].rearrange("p t d -> p (t d)")): return
        scale, shift = columns_of(1)
        layer_norm(nc, ln, "ln_c", y, eps, ident, cols_out=by_batch, scale=scale, shift=shift)
        attention(nc, "cross", h_cols, y, a["wqkv2"], a["wo2"], ident, ctx_cols=c["ctx_t"], out_bias=c["bo2_rows"],
                  q_scale=HD ** -0.5)
        if probe and probe(nc, 3, y[:].rearrange("p t d -> p (t d)")): return
        scale, shift = columns_of(2)
        layer_norm(nc, ln, "ln_d", y, eps, ident, cols_out=by_batch, scale=scale, shift=shift)
        feed_forward(nc, h_cols, y, a["ff_w1"], a["ff_b1"], a["ff_w2"], c["ffb2_rows"])
        with nc.Block() as block:
            @block.vector
            def _(dve):
                dve.tensor_tensor(x[:], x[:], y[:], ALU.add)
        if probe and probe(nc, 4, x[:].rearrange("p t d -> p (t d)")): return

        layer_norm(nc, ln, "ln_e", x, eps, ident, rows_out=y)
        layer_norm(nc, ln, "ln_f", y, eps, ident, cols_out=by_batch, scale=gain, shift=bias)
        attention(nc, "causal", h_cols, y, a["wqkv3"], a["wo3"], ident, masks=masks,
                  norm=(c["ones_half"], (c["qk_gain"][:, 0:NP], c["qk_gain"][:, NP:2 * NP]),
                        (c["eps"][:, 4:5], c["eps"][:, 1:2])), q_scale=QK_SCALE, accumulate=False)
        if probe and probe(nc, 5, y[:].rearrange("p t d -> p (t d)")): return
        layer_norm(nc, ln, "ln_g", y, eps, ident, cols_out=by_batch, scale=gain, shift=bias)
        gating(nc, "moe_gate", h_cols, gates[:], c["gate_w"], c["gate_b_rows"], ident, acc=y, b2=c["b2"])
        experts(nc, "moe", h_cols, y, gates[:], a["moe_w1"], a["moe_b1"], a["moe_w2"], ACT.Gelu_apprx_tanh)
        layer_norm(nc, ln, "ln_h", y, eps, ident, rows_out=x, add_to=x, gain_rows=g_rows, bias_rows=b_rows)
        if probe and probe(nc, 6, x[:].rearrange("p t d -> p (t d)")): return

        with ExitStack() as own:
            x_t = own.enter_context(nc.sbuf_tensor("x_t", [P, (S + 1) * B], F32))
            score_w = own.enter_context(nc.sbuf_tensor("score_w", [P, B, CPAD], F32))
            gate_w = own.enter_context(nc.sbuf_tensor("ctx_gate_w", [P, 3, 3 * P], F32))
            with nc.Block() as block:
                @block.vector
                def _(dve):
                    dve.memset(x_t[:, S * B:(S + 1) * B], 0.0)
            x_by_batch = x_t[:, 0:S * B].rearrange("p (t b) -> p b t", b=B)
            layer_norm(nc, ln, "ln_i", x, eps, ident, scale=one, shift=zero,
                       cols_out=lambda b: x_by_batch[:, bass.ds(b, 1), :].rearrange("p a t -> p (a t)"))
            recurrence_tables(nc, "tables", c["ctx_t"], c["ctx_k"], c["w_t"], c["k_ctx"],
                              c["bias_rows"], c["is_key"], score_w[:].rearrange("p b s -> p (b s)"), gate_w)
            recurrence(nc, x_t, score_w, gate_w, c["r_w"].rearrange("p (c g) -> p c g", c=4),
                       c["x_w"].rearrange("p (c g) -> p c g", c=4), c["mask_l"], c["mask_r"], c["spread"], a["cond_t"],
                       a["h0_c"], h_cols)
        add_history(nc, x, h_cols[:], ident)
        if probe and probe(nc, 7, x[:].rearrange("p t d -> p (t d)")): return

        layer_norm(nc, ln, "ln_j", x, eps, ident, cols_out=by_batch, scale=one, shift=zero)
        gating(nc, "pick", h_cols, gates[:], c["gw2"], None, ident)
        if probe and probe(nc, 8, gates[:]): return
        experts(nc, "picked", h_cols, x, gates[:], a["ec_w1"], None, a["ec_w2"], ACT.Gelu)
        with nc.Block() as block:
            @block.sync
            def _(sp):
                sp.dma_start(out.rearrange("(n p) d -> p n d", p=P), x[:]).then_inc(s_out, 16)
                sp.wait_ge(s_out, 16)


def laid_out(np, i):
    f = {k: np.ascontiguousarray(v) for k, v in i.items()}
    x0 = "L0_xcond_"

    def pairs(q, k, v):
        return np.stack([w.reshape(P, NP, P).transpose(1, 0, 2) for w in (q, k, v)], 2)

    def chunks(w, order):
        w = w.reshape(w.shape[:-1] + (3, 4, 32))[..., order, :, :]
        return np.moveaxis(w, -3, -2).reshape(w.shape[:-3] + (4, 96))

    a = {"x": f["x"].reshape(B * S, P), "cond_t": f["cond_1024"].T}
    a["norm_w"] = np.concatenate([f[f"{x0}norm{n}_w"] for n in (1, 2, 3)], 1)
    a["norm_b"] = np.concatenate([f[f"{x0}norm{n}_b"].reshape(2, P).T for n in (1, 2, 3)], 1)
    for n, w in ((1, "attn1"), (2, "attn2")):
        a[f"wqkv{n}"] = pairs(f[f"{x0}{w}_wq"], f[f"{x0}{w}_wk"], f[f"{x0}{w}_wv"])
        a[f"wo{n}"] = f[f"{x0}{w}_wo"].reshape(NP, P, P)
        a[f"bo{n}_rows"] = np.broadcast_to(f[f"{x0}{w}_bo"], (P, P))
    a["wqkv3"] = pairs(f["L0_ffn_Wq"], f["L0_ffn_Wk"], f["L0_ffn_Wv"])
    a["wo3"] = f["L0_ffn_Wo"].reshape(NP, P, P)
    a["ff_w1"], a["ff_b1"] = f[x0 + "ff_w1"], f[x0 + "ff_b1"].reshape(2 * FC, P).T
    a["ff_w2"] = f[x0 + "ff_w2"].reshape(FC, P, P).transpose(1, 0, 2)
    a["ffb2_rows"] = np.broadcast_to(f[x0 + "ff_b2"], (P, P))
    a["ln_cols"] = np.stack([f["L0_ffn_ln_g"], f["L0_ffn_ln_b"]], 1)
    a["g_rows"] = np.broadcast_to(f["L0_ffn_ln_g"], (P, P))
    a["b_rows"] = np.broadcast_to(f["L0_ffn_ln_b"], (P, P))
    a["qk_gain"] = np.concatenate([f[f"L0_ffn_{n}_scale"].reshape(NP, P).T for n in "qk"], 1)
    a["gate_w"], a["gate_b_rows"] = f["L0_ffn_gate_w"], np.broadcast_to(f["L0_ffn_gate_b"], (P, E))
    a["moe_w1"], a["moe_b1"] = f["L0_ffn_w1"], f["L0_ffn_b1"].reshape(E, FC, P).transpose(0, 2, 1)
    a["moe_w2"], a["b2"] = f["L0_ffn_w2"].reshape(E, FC, P, P).transpose(0, 2, 1, 3), f["L0_ffn_b2"]
    ctx_t = np.zeros((P, B, CPAD), np.float32)
    ctx_t[:, :, :CTX] = f["ctx_1024"].transpose(2, 0, 1)
    a["ctx_t"] = ctx_t.reshape(P, B * CPAD)
    a["ctx_k"] = ctx_t.reshape(P, B, 3, 32).transpose(0, 2, 1, 3).reshape(P, 3 * P)
    a["w_t"] = f["L1_xcond_W"].T
    a["k_ctx"] = chunks(f["L1_xcond_kernel"][P:], [1, 0, 2]).reshape(P, 3 * P)
    x_w = np.zeros((P, 4, P), np.float32)
    x_w[:, :, 32:] = chunks(f["L1_xcond_kernel"][:P], [1, 0, 2])
    a["x_w"] = x_w.reshape(P, 4 * P)
    a["r_w"] = chunks(f["L1_xcond_recurrent_kernel"], [2, 1, 0]).reshape(P, 3 * P)
    a["bias_rows"] = np.broadcast_to(chunks(f["L1_xcond_bias"], [1, 0, 2]).reshape(3 * P), (P, 3 * P))
    h0 = np.zeros((4, 32, 32), np.float32)
    h0[:, :B] = f["cond_1024"].reshape(B, 4, 32).transpose(1, 0, 2)
    a["h0_c"] = h0.reshape(P, 32)
    a["gw2"] = f["L1_ffn_gate_w"].T
    a["ec_w1"], a["ec_w2"] = f["L1_ffn_w1"], f["L1_ffn_w2"].reshape(E, FC, P, P).transpose(0, 2, 1, 3)
    a["ident"] = np.eye(P, dtype=np.float32)
    a["eps"] = np.broadcast_to(np.array([EPS, EPS_L2, 1.0, 0.0, EPS_L2 / QK_SCALE ** 2], np.float32), (P, 5))
    a["ones_half"] = np.kron(np.eye(2, dtype=np.float32), np.ones((HD, HD), np.float32))
    a["masks"] = np.concatenate([np.eye(P), np.triu(np.full((P, P), -1e30), 1)], 1).astype(np.float32)
    group, row = np.arange(P) // 32, np.arange(P) % 32
    used = row == group
    a["mask_l"] = np.stack([~used, used]).astype(np.float32)
    mask_r = np.zeros((2, CPAD))
    mask_r[0, :CTX], mask_r[0, CTX + 1:], mask_r[1, CTX:] = -1e30, -1e30, -1e30
    a["mask_r"] = mask_r.astype(np.float32)
    a["is_key"] = (32 * np.arange(3)[None, :] + row[:, None] < CTX).astype(np.float32)
    a["spread"] = (np.arange(P)[:, None] == 33 * np.arange(B)[None, :]).astype(np.float32)
    return {k: np.ascontiguousarray(v) for k, v in a.items()}


def kernel(**inputs):
    import numpy as np
    from concourse import bacc
    from concourse.bass_utils import run_bass_kernel_spmd

    arrays = laid_out(np, inputs)
    nc = bacc.Bacc("TRN2", target_bir_lowering=False, num_devices=1)
    a = {n: nc.dram_tensor(f"in_{n}", v.shape, mybir.dt.from_np(v.dtype), kind="ExternalInput").ap()
         for n, v in arrays.items()}
    out = nc.dram_tensor("out", (B * S, P), F32, kind="ExternalOutput").ap()
    program(nc, a, out)
    r = run_bass_kernel_spmd(nc, [{f"in_{n}": v for n, v in arrays.items()}], core_ids=[0])
    return r.results[0]["out"].reshape(B, S, P)
```

```python
from contextlib import ExitStack

import concourse.bass as bass
from concourse import mybir

F32 = mybir.dt.float32
BF16 = mybir.dt.bfloat16
ALU = mybir.AluOpType
ACT = mybir.ActivationFunctionType
AX = mybir.AxisListType


P = 128
B = 4
S = 512
NT = S // P
CTX = 77
CPAD = 96
NP = 8
HD = 64
E = 8
FC = 4
TOPK = 2 * S // E
EPS, EPS_L2 = 1e-5, 1e-12
QK_SCALE = 10.0
BANK = 512
EARLY = {"ident": P, "eps": 5}
LATE = {"masks": 2 * P, "ones_half": P, "cond_t": B, "norm_w": 6 * P, "norm_b": 6, "ctx_t": B * CPAD, "ctx_k": 3 * P,
        "bo1_rows": P, "bo2_rows": P, "ffb2_rows": P, "ln_cols": 2, "g_rows": P, "b_rows": P, "qk_gain": 2 * NP,
        "gate_w": E, "gate_b_rows": E, "gw2": E, "w_t": P, "k_ctx": 3 * P, "r_w": 3 * P, "x_w": 4 * P,
        "bias_rows": 3 * P, "is_key": 3, "spread": B, "up_to": P, "ones": P, "numbers": TOPK}
STEPS_PER_TURN = 16


class Counted:

    def __init__(self, sem):
        self.sem, self.base = sem, 0


def layer_norm(nc, ln, name, src, eps_sb, ident, rows_out=None, cols_out=None, scale=None, shift=None,
               add_to=None, gain_rows=None, bias_rows=None):
    n_tiles = B * NT
    with ExitStack() as ctx:
        def sb(n, shape):
            return ctx.enter_context(nc.sbuf_tensor(f"{name}_{n}", shape, F32))

        stats, mv = sb("stats", [P, n_tiles, 6]), sb("mv", [P, n_tiles, 2])
        std, rstd = sb("std", [P, n_tiles]), sb("rstd", [P, n_tiles])
        xn = rows_out if gain_rows is None and rows_out is not None else sb("xn", [P, n_tiles, P])
        tp = [ctx.enter_context(nc.psum_tensor(f"{name}_tp{b}", [P, S], F32)) for b in range(B)] if cols_out else None
        block = ctx.enter_context(nc.Block())

        def wait(eng, what, n):
            eng.wait_ge(ln[what].sem, n + ln[what].base)

        @block.vector
        def _(dve):
            for i in range(n_tiles):
                last = dve.bn_stats(stats[:, i, :], src[:, i, :])
            last.then_inc(ln["stats"].sem, 1)
            wait(dve, "stats", 1)
            for i in range(n_tiles):
                last = dve.bn_aggr(mv[:, i, :], stats[:, i, :])
            last.then_inc(ln["aggr"].sem, 1)
            wait(dve, "sqrt", 1)
            dve.reciprocal(rstd[:], std[:]).then_inc(ln["rstd"].sem, 1)
            wait(dve, "rstd", 1)
            for b in range(B):
                for i in range(b * NT, (b + 1) * NT):
                    last = dve.tensor_scalar(xn[:, i, :], src[:, i, :], mv[:, i, 0:1], rstd[:, i:i + 1], ALU.subtract,
                                             ALU.mult)
                last.then_inc(ln["xn"].sem, 1)
            if gain_rows is not None:
                wait(dve, "xn", B)
                dve.tensor_tensor(xn[:], xn[:], gain_rows, ALU.mult).then_inc(ln["gained"].sem, 1)
                wait(dve, "gained", 1)
                dve.tensor_tensor(xn[:], xn[:], bias_rows, ALU.add).then_inc(ln["biased"].sem, 1)
                wait(dve, "biased", 1)
                dve.tensor_tensor(rows_out[:], xn[:], add_to[:], ALU.add)

        @block.scalar
        def _(act):
            wait(act, "aggr", 1)
            act.activation(std[:], mv[:, :, 1], ACT.Sqrt, bias=eps_sb).then_inc(ln["sqrt"].sem, 1)
            if cols_out is not None:
                for b in range(B):
                    wait(act, "turned", b + 1)
                    act.activation(cols_out(b), tp[b][:], ACT.Identity, bias=shift(b), scale=scale(b))

        if cols_out is not None:
            @block.tensor
            def _(pe):
                for b in range(B):
                    wait(pe, "xn", b + 1)
                    for j in range(NT):
                        last = pe.transpose(tp[b][:, j * P:(j + 1) * P], xn[:, b * NT + j, :], ident)
                    last.then_inc(ln["turned"].sem, 1)

    for what, n in (("stats", 1), ("aggr", 1), ("sqrt", 1), ("rstd", 1), ("xn", B), ("turned", B * (cols_out is not None)),
                    ("gained", gain_rows is not None), ("biased", gain_rows is not None)):
        ln[what].base += int(n)


def wait_positive(eng, sem, n):
    if not isinstance(n, int) or n > 0:
        eng.wait_ge(sem, n)


def turns(eng, turn):
    turn(0)
    with eng.Fori(1, NP - 1) as pair:
        turn(pair)
    turn(NP - 1)


def attention(nc, name, h_cols, y, wqkv, wo, ident, out_bias=None, masks=None, norm=None, q_scale=1.0):
    causal = masks is not None
    U = 2 * NT

    def tile(n):
        return NT - 1 - n

    def keys(n):
        return (tile(n) + 1) * P if causal else S

    def ktiles(n):
        return tile(n) + 1 if causal else NT

    def tokens(b):
        return h_cols[:, b * S:(b + 1) * S]

    with ExitStack() as ctx:
        def sb(n, shape, dt=F32):
            return ctx.enter_context(nc.sbuf_tensor(f"{name}_{n}", shape, dt))

        def pb(n):
            return ctx.enter_context(nc.psum_tensor(f"{name}_{n}", [P, S], F32))

        def sem(n):
            return ctx.enter_context(nc.semaphore(f"{name}_{n}"))

        w_sb, wo_sb = sb("w_sb", [P, 3, P]), sb("wo_sb", [P, P])
        q_sb, k_sb, v_sb = sb("q_sb", [P, S]), sb("k_sb", [P, S]), sb("v_sb", [P, NT, P])
        probs, probs_t = sb("probs", [P, 4, S]), sb("probs_t", [P, 4, NT, P])
        o_sb = sb("o_sb", [P, S])
        negmax, total, rtotal = sb("negmax", [P, U]), sb("total", [P, U]), sb("rtotal", [P, U])
        sc = [pb(f"sc{i}") for i in range(4)]
        pt = [pb(f"pt{i}") for i in range(2)]
        ot, vb = pb("ot"), pb("vb")
        s_w, s_wo = sem("w"), sem("wo")
        s_pq, s_pk, s_pv = sem("pq"), sem("pk"), sem("pv")
        s_qe, s_ke, s_ve = sem("qe"), sem("ke"), sem("ve")
        s_sc, s_max, s_exp, s_rt, s_pn = sem("sc"), sem("max"), sem("exp"), sem("rt"), sem("pn")
        s_pt, s_pte, s_ot, s_oe, s_wd, s_y = sem("pt"), sem("pte"), sem("ot"), sem("oe"), sem("wd"), sem("y")
        s_y0 = sem("y0")
        if norm is not None:
            ones_half, qk_gain, eps_l2 = norm
            sq, rnorm = sb("sq", [P, 2, S]), sb("rnorm", [P, 2, S])
            s_sq, s_ss, s_ln, s_rn = sem("sq"), sem("ss"), sem("ln"), sem("rn")
        block = ctx.enter_context(nc.Block())

        @block.sync
        def _(sp):
            def turn(pair):
                wait_positive(sp, s_pv, pair * B)
                sp.dma_start(w_sb[:], wqkv[bass.ds(pair, 1), :, :, :].rearrange("a p t n -> (a p) t n")).then_inc(s_w, 16)
                wait_positive(sp, s_wd, pair * B)
                sp.dma_start(wo_sb[:], wo[bass.ds(pair, 1), :, :].rearrange("a p n -> (a p) n")).then_inc(s_wo, 16)

            turns(sp, turn)

        @block.tensor
        def _(pe):
            def project_qk(it, pair, b):
                wait_positive(pe, s_w, pair * 16 + 16)
                wait_positive(pe, s_exp, it * U - 2)
                pe.matmul(sc[0][:], w_sb[:, 0, :], tokens(b), start=True, stop=True).then_inc(s_pq, 1)
                pe.matmul(sc[1][:], w_sb[:, 1, :], tokens(b), start=True, stop=True).then_inc(s_pk, 1)

            def project_v(it, b):
                wait_positive(pe, s_ve, it)
                for kt in range(NT):
                    last = pe.matmul(vb[:, kt * P:(kt + 1) * P], tokens(b)[:, kt * P:(kt + 1) * P], w_sb[:, 2, :],
                                     start=True, stop=True)
                last.then_inc(s_pv, 1)

            def square_sums(it):
                wait_positive(pe, s_exp, it * U)
                for i in range(2):
                    wait_positive(pe, s_sq, it * 2 + i + 1)
                    pe.matmul(sc[2 + i][:], ones_half, sq[:, i, :], start=True, stop=True).then_inc(s_ss, 1)

            def project_out(it, pair):
                wait_positive(pe, s_oe, it + 1)
                wait_positive(pe, s_wo, pair * 16 + 16)
                for j in range(NT):
                    last = pe.matmul(ot[:, j * P:(j + 1) * P], o_sb[:, j * P:(j + 1) * P], wo_sb[:], start=True, stop=True)
                last.then_inc(s_wd, 1)

            def scores(it, n):
                for j in range(2):
                    u = 2 * n + j
                    if u == 0:
                        wait_positive(pe, s_qe, it + 1)
                        wait_positive(pe, s_ke, it + 1)
                    else:
                        wait_positive(pe, s_exp, it * U + u - 3)
                    bank = sc[u % 4]
                    last = pe.matmul(bank[:, 0:keys(n)], q_sb[HD * j:HD * j + HD, tile(n) * P:(tile(n) + 1) * P],
                                     k_sb[HD * j:HD * j + HD, 0:keys(n)], start=True, stop=not causal)
                    if causal:
                        last = pe.matmul(bank[:, keys(n) - P:keys(n)], masks[0], masks[1], start=False, stop=True)
                    last.then_inc(s_sc, 1)

            def turn_probs(it, n):
                for j in range(2):
                    u = 2 * n + j
                    wait_positive(pe, s_pn, it * U + u + 1)
                    wait_positive(pe, s_pte, it * U + u - 1)
                    for kt in range(ktiles(n)):
                        last = pe.transpose(pt[j][:, kt * P:(kt + 1) * P], probs[:, u % 4, kt * P:(kt + 1) * P], ident)
                    last.then_inc(s_pt, 1)

            def values(it, n):
                wait_positive(pe, s_pte, it * U + 2 * n + 2)
                if n == 0:
                    wait_positive(pe, s_ve, it + 1)
                    wait_positive(pe, s_y, it)
                for kt in range(ktiles(n)):
                    for j in range(2):
                        last = pe.matmul(ot[HD * j:HD * j + HD, tile(n) * P:(tile(n) + 1) * P], v_sb[:, kt, HD * j:HD * j + HD],
                                         probs_t[:, (2 * n + j) % 4, kt, :], start=kt == 0,
                                         stop=kt == ktiles(n) - 1, tile_position=(0, HD * j))
                if n == NT - 1:
                    last.then_inc(s_ot, 1)

            def turn(pair):
                for b in range(B):
                    it = pair * B + b
                    first = isinstance(pair, int) and it == 0
                    final = isinstance(pair, int) and it == NP * B - 1
                    following = (it + 1, pair, b + 1) if b + 1 < B else (it + 1, pair + 1, 0)
                    before = pair if b else pair - 1
                    if first:
                        project_qk(0, 0, 0)
                        if norm is not None:
                            square_sums(0)
                    if norm is not None:
                        project_v(it, b)
                        if not first:
                            project_out(it - 1, before)
                    scores(it, 0)
                    scores(it, 1)
                    if norm is None:
                        project_v(it, b)
                        if not first:
                            project_out(it - 1, before)
                    turn_probs(it, 0)
                    scores(it, 2)
                    values(it, 0)
                    turn_probs(it, 1)
                    scores(it, 3)
                    values(it, 1)
                    turn_probs(it, 2)
                    if not final:
                        project_qk(*following)
                    turn_probs(it, 3)
                    if not final and norm is not None:
                        square_sums(it + 1)
                    values(it, 2)
                    values(it, 3)

            turns(pe, turn)
            project_out(NP * B - 1, NP - 1)

        @block.scalar
        def _(act):
            act.preload_act_table_set("natural_log_exp_and_others")

            def take_qk(it):
                if norm is None:
                    wait_positive(act, s_pq, it + 1)
                    act.activation(q_sb[:], sc[0][:], ACT.Copy, scale=q_scale).then_inc(s_qe, 1)
                    wait_positive(act, s_pk, it + 1)
                    act.activation(k_sb[:], sc[1][:], ACT.Copy).then_inc(s_ke, 1)
                else:
                    for i, projected in enumerate((s_pq, s_pk)):
                        wait_positive(act, projected, it + 1)
                        act.activation(sq[:, i, :], sc[i][:], ACT.Square).then_inc(s_sq, 1)

            def norms(it):
                for i in range(2):
                    wait_positive(act, s_ss, it * 2 + i + 1)
                    wait_positive(act, (s_qe, s_ke)[i], it)
                    act.activation(rnorm[:, i, :], sc[2 + i][:], ACT.Ln, bias=eps_l2[i],
                                   scale=(q_scale ** -2, 1.0)[i]).then_inc(s_ln, 1)
                    wait_positive(act, s_ln, it * 2 + i + 1)
                    act.activation(rnorm[:, i, :], rnorm[:, i, :], ACT.Exp, scale=-0.5).then_inc(s_rn, 1)

            def exponentials(it, u):
                wait_positive(act, s_max, it * U + u + 1)
                act.activation(probs[:, u % 4, 0:keys(u // 2)], sc[u % 4][:, 0:keys(u // 2)], ACT.Exp,
                               bias=negmax[:, u:u + 1], accum_out=total[:, u:u + 1]).then_inc(s_exp, 1)

            def take_turned(it, u):
                wait_positive(act, s_pt, it * U + u + 1)
                act.activation(probs_t[:, u % 4, 0:ktiles(u // 2), :],
                               pt[u % 2][:, 0:ktiles(u // 2) * P].rearrange("p (t q) -> p t q", q=P),
                               ACT.Copy).then_inc(s_pte, 1)

            def take_v(it):
                wait_positive(act, s_pv, it + 1)
                act.activation(v_sb[:], vb[:].rearrange("p (t d) -> p t d", d=P), ACT.Copy).then_inc(s_ve, 1)

            def turn(pair):
                for b in range(B):
                    it = pair * B + b
                    final = isinstance(pair, int) and it == NP * B - 1
                    if norm is not None:
                        take_v(it)
                    exponentials(it, 0)
                    exponentials(it, 1)
                    exponentials(it, 2)
                    if norm is None:
                        take_v(it)
                        exponentials(it, 3)
                        take_turned(it, 0)
                    else:
                        take_turned(it, 0)
                        exponentials(it, 3)
                    take_turned(it, 1)
                    exponentials(it, 4)
                    exponentials(it, 5)
                    take_turned(it, 2)
                    take_turned(it, 3)
                    exponentials(it, 6)
                    exponentials(it, 7)
                    take_turned(it, 4)
                    take_turned(it, 5)
                    if not final:
                        take_qk(it + 1)
                    take_turned(it, 6)
                    take_turned(it, 7)
                    if not final and norm is not None:
                        norms(it + 1)

            take_qk(0)
            if norm is not None:
                norms(0)
            turns(act, turn)

        @block.vector
        def _(dve):
            def maximum(it, u):
                wait_positive(dve, s_sc, it * U + u + 1)
                dve.tensor_reduce(negmax[:, u:u + 1], sc[u % 4][:, 0:keys(u // 2)], axis=AX.X, op=ALU.max,
                                  negate=True).then_inc(s_max, 1)

            def normalise(it, u):
                wait_positive(dve, s_exp, it * U + u + 1)
                dve.reciprocal(rtotal[:, u:u + 1], total[:, u:u + 1]).then_inc(s_rt, 1)
                wait_positive(dve, s_rt, it * U + u + 1)
                row = probs[:, u % 4, 0:keys(u // 2)]
                dve.tensor_scalar(row, row, rtotal[:, u:u + 1], None, ALU.mult).then_inc(s_pn, 1)

            def scale_qk(it, pair):
                for i, (to, done) in enumerate(((q_sb, s_qe), (k_sb, s_ke))):
                    wait_positive(dve, s_rn, it * 2 + i + 1)
                    dve.scalar_tensor_tensor(out=to[:], in0=sc[i][:], scalar=qk_gain[i][:, bass.ds(pair, 1)],
                                             in1=rnorm[:, i, :], op0=ALU.mult, op1=ALU.mult).then_inc(done, 1)

            def add_out(it, b):
                wait_positive(dve, s_wd, it + 1)
                wait_positive(dve, s_y, it + 1 - B)
                out = y[:, b * NT:(b + 1) * NT, :]
                dve.tensor_tensor(out, out, ot[:].rearrange("p (t d) -> p t d", d=P), ALU.add).then_inc(s_y, 1)

            def turn(pair):
                for b in range(B):
                    it = pair * B + b
                    first = isinstance(pair, int) and it == 0
                    final = isinstance(pair, int) and it == NP * B - 1
                    maximum(it, 0)
                    maximum(it, 1)
                    normalise(it, 0)
                    maximum(it, 2)
                    normalise(it, 1)
                    maximum(it, 3)
                    if not first:
                        add_out(it - 1, (b - 1) % B)
                    normalise(it, 2)
                    normalise(it, 3)
                    maximum(it, 4)
                    maximum(it, 5)
                    normalise(it, 4)
                    normalise(it, 5)
                    maximum(it, 6)
                    maximum(it, 7)
                    normalise(it, 6)
                    normalise(it, 7)
                    wait_positive(dve, s_ot, it + 1)
                    dve.tensor_copy(o_sb[:], ot[:]).then_inc(s_oe, 1)
                    if not final and norm is not None:
                        scale_qk(it + 1, pair if b + 1 < B else pair + 1)

            if out_bias is None:
                dve.memset(y[:], 0.0).then_inc(s_y0, 1)
                dve.wait_ge(s_y0, 1)
            else:
                dve.tensor_tensor(y[:], y[:], out_bias.rearrange("p (a d) -> p a d", a=1).broadcast_to([P, B * NT, P]),
                                  ALU.add).then_inc(s_y0, 1)
                dve.wait_ge(s_y0, 1)
            if norm is not None:
                scale_qk(0, 0)
            turns(dve, turn)
            add_out(NP * B - 1, B - 1)


def context_attention(nc, name, h_cols, y, wqkv, wo, ident, ctx_cols, out_bias, q_scale):
    with ExitStack() as ctx:
        def sb(n, shape):
            return ctx.enter_context(nc.sbuf_tensor(f"{name}_{n}", shape, F32))

        def pb(n):
            return ctx.enter_context(nc.psum_tensor(f"{name}_{n}", [P, S], F32))

        def sem(n):
            return ctx.enter_context(nc.semaphore(f"{name}_{n}"))

        w_sb, wo_sb = sb("w_sb", [P, 3, P]), sb("wo_sb", [P, P])
        q_sb, k_sb, v_sb = sb("q_sb", [P, S]), sb("k_sb", [P, CTX]), sb("v_sb", [CTX, B, P])
        top, shifted = sb("top", [P, 2, NT]), sb("shifted", [P, 2, NT, CTX])
        probs, total, rtotal = sb("probs", [P, 2, NT, CTX]), sb("total", [P, 2, NT]), sb("rtotal", [P, 2, NT])
        probs_t, o_sb = sb("probs_t", [CTX, 2, S]), sb("o_sb", [P, S])
        sc, pt = [pb("sc0"), pb("sc1")], [pb("pt0"), pb("pt1")]
        pq, pkv, ot, projected = pb("pq"), pb("pkv"), pb("ot"), pb("projected")
        (s_w, s_wo, s_qkv, s_taken, s_sc, s_top, s_shift, s_exp, s_total, s_rt, s_pn, s_pt, s_pte, s_ot, s_oe, s_wd, s_y,
         s_y0) = (sem(n) for n in ("w", "wo", "qkv", "taken", "sc", "top", "shift", "exp", "total", "rt", "pn", "pt",
                                   "pte", "ot", "oe", "wd", "y", "y0"))
        block = ctx.enter_context(nc.Block())

        def by_tile(bank):
            return bank[:, 0:NT * CTX].rearrange("p (t k) -> p t k", k=CTX)

        def spread(column):
            return column.rearrange("p (t a) -> p t a", a=1).broadcast_to([P, NT, CTX])

        @block.sync
        def _(sp):
            def turn(pair):
                wait_positive(sp, s_qkv, pair * B)
                sp.dma_start(w_sb[:], wqkv[bass.ds(pair, 1), :, :, :].rearrange("a p t n -> (a p) t n")).then_inc(s_w, 16)
                wait_positive(sp, s_wd, pair * B)
                sp.dma_start(wo_sb[:], wo[bass.ds(pair, 1), :, :].rearrange("a p n -> (a p) n")).then_inc(s_wo, 16)

            turns(sp, turn)

        @block.tensor
        def _(pe):
            def project(it, pair, b):
                context = ctx_cols[:, b * CPAD:b * CPAD + CTX]
                wait_positive(pe, s_w, pair * 16 + 16)
                wait_positive(pe, s_taken, it)
                pe.matmul(pq[:], w_sb[:, 0, :], h_cols[:, b * S:(b + 1) * S], start=True, stop=True)
                pe.matmul(pkv[:, 0:CTX], w_sb[:, 1, :], context, start=True, stop=True)
                pe.matmul(pkv[0:CTX, P:2 * P], context, w_sb[:, 2, :], start=True, stop=True).then_inc(s_qkv, 1)

            def scores(it):
                wait_positive(pe, s_taken, it + 1)
                for j in range(2):
                    wait_positive(pe, s_shift, it * 2 + j - 1)
                    for n in range(NT):
                        last = pe.matmul(sc[j][:, n * CTX:(n + 1) * CTX], q_sb[HD * j:HD * j + HD, n * P:(n + 1) * P],
                                         k_sb[HD * j:HD * j + HD, :], start=True, stop=True)
                    last.then_inc(s_sc, 1)

            def turn_probs(it):
                for j in range(2):
                    wait_positive(pe, s_pn, it * 2 + j + 1)
                    wait_positive(pe, s_pte, it * 2 + j - 1)
                    for n in range(NT):
                        last = pe.transpose(pt[j][0:CTX, n * P:(n + 1) * P], probs[:, j, n, :], ident)
                    last.then_inc(s_pt, 1)

            def values(it, b):
                wait_positive(pe, s_pte, it * 2 + 2)
                wait_positive(pe, s_oe, it)
                for j in range(2):
                    last = pe.matmul(ot[HD * j:HD * j + HD, :], v_sb[:, b, HD * j:HD * j + HD], probs_t[:, j, :],
                                     start=True, stop=True, tile_position=(0, HD * j))
                last.then_inc(s_ot, 1)

            def project_out(it, pair):
                wait_positive(pe, s_oe, it + 1)
                wait_positive(pe, s_wo, pair * 16 + 16)
                wait_positive(pe, s_y, it)
                for n in range(NT):
                    last = pe.matmul(projected[:, n * P:(n + 1) * P], o_sb[:, n * P:(n + 1) * P], wo_sb[:], start=True,
                                     stop=True)
                last.then_inc(s_wd, 1)

            def turn(pair):
                for b in range(B):
                    it = pair * B + b
                    first, second = (isinstance(pair, int) and it == n for n in (0, 1))
                    final = isinstance(pair, int) and it == NP * B - 1
                    scores(it)
                    if not (first or second):
                        project_out(it - 2, pair if b > 1 else pair - 1)
                    if not first:
                        turn_probs(it - 1)
                    if not final:
                        project(it + 1, pair if b + 1 < B else pair + 1, (b + 1) % B)
                    if not first:
                        values(it - 1, (b - 1) % B)

            project(0, 0, 0)
            turns(pe, turn)
            project_out(NP * B - 2, NP - 1)
            turn_probs(NP * B - 1)
            values(NP * B - 1, B - 1)
            project_out(NP * B - 1, NP - 1)

        @block.scalar
        def _(act):
            act.preload_act_table_set("natural_log_exp_and_others")

            def take(it, b):
                wait_positive(act, s_qkv, it + 1)
                act.activation(q_sb[:], pq[:], ACT.Copy, scale=q_scale)
                act.activation(k_sb[:], pkv[:, 0:CTX], ACT.Copy)
                act.activation(v_sb[:, b, :], pkv[0:CTX, P:2 * P], ACT.Copy).then_inc(s_taken, 1)

            def take_turned(it):
                for j in range(2):
                    wait_positive(act, s_pt, it * 2 + j + 1)
                    act.activation(probs_t[:, j, :], pt[j][0:CTX, :], ACT.Copy).then_inc(s_pte, 1)

            def take_out(it):
                wait_positive(act, s_ot, it + 1)
                act.activation(o_sb[:], ot[:], ACT.Copy).then_inc(s_oe, 1)

            def turn(pair):
                for b in range(B):
                    it = pair * B + b
                    first = isinstance(pair, int) and it == 0
                    final = isinstance(pair, int) and it == NP * B - 1
                    if not first:
                        take_turned(it - 1)
                    for j in range(2):
                        wait_positive(act, s_shift, it * 2 + j + 1)
                        act.activation(probs[:, j, :, :], shifted[:, j, :, :], ACT.Exp).then_inc(s_exp, 1)
                    if not final:
                        take(it + 1, (b + 1) % B)
                    if not first:
                        take_out(it - 1)

            take(0, 0)
            turns(act, turn)
            take_turned(NP * B - 1)
            take_out(NP * B - 1)

        @block.vector
        def _(dve):
            def add_out(it, b):
                wait_positive(dve, s_wd, it + 1)
                out = y[:, b * NT:(b + 1) * NT, :]
                dve.tensor_tensor(out, out, projected[:].rearrange("p (t d) -> p t d", d=P), ALU.add).then_inc(s_y, 1)

            def turn(pair):
                for b in range(B):
                    it = pair * B + b
                    first, second = (isinstance(pair, int) and it == n for n in (0, 1))
                    for j in range(2):
                        wait_positive(dve, s_sc, it * 2 + j + 1)
                        dve.tensor_reduce(top[:, j, :], by_tile(sc[j]), axis=AX.X, op=ALU.max).then_inc(s_top, 1)
                    for j in range(2):
                        wait_positive(dve, s_top, it * 2 + j + 1)
                        dve.tensor_tensor(shifted[:, j, :, :], by_tile(sc[j]), spread(top[:, j, :]), ALU.subtract)\
                           .then_inc(s_shift, 1)
                    if not (first or second):
                        add_out(it - 2, (b - 2) % B)
                    for j in range(2):
                        wait_positive(dve, s_exp, it * 2 + j + 1)
                        dve.tensor_reduce(total[:, j, :], probs[:, j, :, :], axis=AX.X, op=ALU.add).then_inc(s_total, 1)
                        wait_positive(dve, s_total, it * 2 + j + 1)
                        dve.reciprocal(rtotal[:, j, :], total[:, j, :]).then_inc(s_rt, 1)
                        wait_positive(dve, s_rt, it * 2 + j + 1)
                        dve.tensor_tensor(probs[:, j, :, :], probs[:, j, :, :], spread(rtotal[:, j, :]), ALU.mult)\
                           .then_inc(s_pn, 1)

            dve.tensor_tensor(y[:], y[:], out_bias.rearrange("p (a d) -> p a d", a=1).broadcast_to([P, B * NT, P]),
                              ALU.add).then_inc(s_y0, 1)
            dve.wait_ge(s_y0, 1)
            turns(dve, turn)
            add_out(NP * B - 2, B - 2)
            add_out(NP * B - 1, B - 1)


def feed_forward(nc, h_cols, x, y, w1, b1, w2, b2_rows):
    with ExitStack() as ctx:
        def sb(n, shape):
            return ctx.enter_context(nc.sbuf_tensor(f"ff_{n}", shape, F32))

        def pb(n):
            return ctx.enter_context(nc.psum_tensor(f"ff_{n}", [P, S], F32))

        def sem(n):
            return ctx.enter_context(nc.semaphore(f"ff_{n}"))

        w1_sb, b1_sb, w2_sb = sb("w1_sb", [P, 2 * FC * P]), sb("b1_sb", [P, 2 * FC]), sb("w2_sb", [P, FC, P])
        gate, hidden = sb("gate", [P, 2, S]), sb("hidden", [P, FC, S])
        up, gt, down = [pb("up0"), pb("up1")], [pb("gt0"), pb("gt1")], pb("down")
        s_w, s_up, s_gelu, s_hid, s_down, s_y, s_y0 = (sem(n) for n in ("w", "up", "gelu", "hid", "down", "y", "y0"))
        block = ctx.enter_context(nc.Block())

        @block.sync
        def _(sp):
            sp.dma_start(w1_sb[:], w1).then_inc(s_w, 16)
            sp.dma_start(b1_sb[:], b1).then_inc(s_w, 16)
            sp.dma_start(w2_sb[:], w2).then_inc(s_w, 16)

        @block.tensor
        def _(pe):
            pe.sem_inc(s_down, 1)
            pe.wait_ge(s_w, 48)
            with pe.Fori(0, B) as b:
                for f in range(FC):
                    pe.wait_ge(s_hid, b * FC + max(f - 1, 0) + 1)
                    pe.matmul(up[f % 2][:], w1_sb[:, f * P:(f + 1) * P], h_cols[:, bass.ds(b * S, S)],
                              start=True, stop=True)
                    pe.matmul(gt[f % 2][:], w1_sb[:, (FC + f) * P:(FC + f + 1) * P], h_cols[:, bass.ds(b * S, S)],
                              start=True, stop=True).then_inc(s_up, 1)
                pe.wait_ge(s_y, b + 1)
                for f in range(FC):
                    pe.wait_ge(s_hid, b * FC + f + 2)
                    for j in range(NT):
                        last = pe.matmul(down[:, j * P:(j + 1) * P], hidden[:, f, j * P:(j + 1) * P], w2_sb[:, f, :],
                                         start=f == 0 and j == 0, stop=f == FC - 1, skip_group_check=True)
                last.then_inc(s_down, 1)

        @block.scalar
        def _(act):
            act.wait_ge(s_w, 48)
            with act.Fori(0, B) as b:
                for f in range(FC):
                    act.wait_ge(s_up, b * FC + f + 1)
                    if f >= 2:
                        act.wait_ge(s_hid, b * FC + f)
                    act.activation(gate[:, f % 2, :], gt[f % 2][:], ACT.Gelu, bias=b1_sb[:, FC + f:FC + f + 1])\
                       .then_inc(s_gelu, 1)

        @block.vector
        def _(dve):
            dve.sem_inc(s_hid, 1)
            dve.sem_inc(s_y, 1)
            dve.tensor_tensor(y[:], y[:], b2_rows.rearrange("p (a d) -> p a d", a=1).broadcast_to([P, B * NT, P]), ALU.add)\
               .then_inc(s_y0, 1)
            dve.wait_ge(s_y0, 1)
            dve.tensor_tensor(x[:], x[:], y[:], ALU.add).then_inc(s_y0, 1)
            dve.wait_ge(s_y0, 2)
            dve.wait_ge(s_w, 48)
            with dve.Fori(0, B) as b:
                for f in range(FC):
                    dve.wait_ge(s_gelu, b * FC + f + 1)
                    if f == 0:
                        dve.wait_ge(s_down, b + 1)
                    dve.scalar_tensor_tensor(out=hidden[:, f, :], in0=up[f % 2][:], scalar=b1_sb[:, f:f + 1],
                                             in1=gate[:, f % 2, :], op0=ALU.add, op1=ALU.mult).then_inc(s_hid, 1)
                dve.wait_ge(s_down, b + 2)
                out = x[:, bass.ds(b * NT, NT), :]
                dve.tensor_tensor(out, out, down[:].rearrange("p (t d) -> p t d", d=P), ALU.add).then_inc(s_y, 1)


def experts(nc, name, h_cols, acc, gates, w1, b1, w2, gelu):
    with ExitStack() as ctx:
        def sb(n, shape):
            return ctx.enter_context(nc.sbuf_tensor(f"{name}_{n}", shape, F32))

        def pb(n):
            return ctx.enter_context(nc.psum_tensor(f"{name}_{n}", [P, S], F32))

        def sem(n):
            return ctx.enter_context(nc.semaphore(f"{name}_{n}"))

        w1_sb, w2_sb, b1_sb = sb("w1_sb", [P, 2, FC * P]), sb("w2_sb", [P, 2, FC, P]), sb("b1_sb", [P, 2, FC])
        hidden = sb("hidden", [P, FC, S])
        up, down = [pb("up0"), pb("up1")], pb("down")
        s_w, s_down = [sem("w0"), sem("w1")], [sem("done0"), sem("done1")]
        s_up, s_gelu, s_acc = sem("up"), sem("gelu"), sem("acc")
        loads = 2 + (b1 is not None)
        block = ctx.enter_context(nc.Block())

        @block.sync
        def _(sp):
            with sp.Fori(0, E // 2) as turn:
                for k in range(2):
                    e = turn * 2 + k
                    sp.wait_ge(s_down[k], turn * B + 1)
                    sp.dma_start(w1_sb[:, k, :], w1[bass.ds(e, 1), :, :].rearrange("a p n -> (a p) n")).then_inc(s_w[k], 16)
                    sp.dma_start(w2_sb[:, k, :, :], w2[bass.ds(e, 1), :, :, :].rearrange("a p f n -> (a p) f n"))\
                      .then_inc(s_w[k], 16)
                    if b1 is not None:
                        sp.dma_start(b1_sb[:, k, :], b1[bass.ds(e, 1), :, :].rearrange("a p n -> (a p) n"))\
                          .then_inc(s_w[k], 16)

        @block.tensor
        def _(pe):
            pe.sem_inc(s_down[0], 1)
            pe.sem_inc(s_down[1], 1)
            with pe.Fori(0, E // 2) as turn:
                for k in range(2):
                    with pe.Fori(0, B) as b:
                        pe.wait_ge(s_w[k], 16 * loads * turn + 16 * loads)
                        n = (turn * 2 + k) * B + b
                        for f in range(FC):
                            pe.wait_ge(s_gelu, n * FC + max(f - 1, 0) + 1)
                            pe.matmul(up[f % 2][:], w1_sb[:, k, f * P:(f + 1) * P], h_cols[:, bass.ds(b * S, S)],
                                      start=True, stop=True).then_inc(s_up, 1)
                        pe.wait_ge(s_acc, n + 1)
                        for f in range(FC):
                            pe.wait_ge(s_gelu, n * FC + f + 2)
                            for j in range(NT):
                                last = pe.matmul(down[:, j * P:(j + 1) * P], hidden[:, f, j * P:(j + 1) * P],
                                                 w2_sb[:, k, f, :], start=f == 0 and j == 0, stop=f == FC - 1,
                                                 skip_group_check=True)
                        last.then_inc(s_down[k], 1)

        @block.scalar
        def _(act):
            act.sem_inc(s_gelu, 1)
            with act.Fori(0, E // 2) as turn:
                for k in range(2):
                    with act.Fori(0, B) as b:
                        act.wait_ge(s_w[k], 16 * loads * turn + 16 * loads)
                        n = (turn * 2 + k) * B + b
                        for f in range(FC):
                            act.wait_ge(s_up, n * FC + f + 1)
                            act.activation(hidden[:, f, :], up[f % 2][:], gelu,
                                           bias=b1_sb[:, k, f:f + 1] if b1 is not None else 0.0).then_inc(s_gelu, 1)

        @block.vector
        def _(dve):
            dve.sem_inc(s_acc, 1)
            with dve.Fori(0, E // 2) as turn:
                for k in range(2):
                    with dve.Fori(0, B) as b:
                        dve.wait_ge(s_down[k], turn * B + b + 2)
                        dve.wait_ge(s_acc, (turn * 2 + k) * B + b + 1)
                        for j in range(NT):
                            out = acc[:, bass.ds(b * NT + j, 1), :].rearrange("p a d -> p (a d)")
                            last = dve.scalar_tensor_tensor(out=out, in0=down[:, j * P:(j + 1) * P],
                                                            scalar=gates[:, bass.ds((b * NT + j) * E + turn * 2 + k, 1)],
                                                            in1=out, op0=ALU.mult, op1=ALU.add)
                        last.then_inc(s_acc, 1)


def picked_experts(nc, name, h_rows, acc, gates, rank, numbers, ident, w1, w2):
    with ExitStack() as ctx:
        def sb(n, shape):
            return ctx.enter_context(nc.sbuf_tensor(f"{name}_{n}", shape, F32))

        def pb(n):
            return ctx.enter_context(nc.psum_tensor(f"{name}_{n}", [P, S], F32))

        def sem(n):
            return ctx.enter_context(nc.semaphore(f"{name}_{n}"))

        w1_sb, w2_sb = sb("w1_sb", [P, 2, FC * P]), sb("w2_sb", [P, 2, FC, P])
        gather, spread, spread_t = (sb(n, [P, 2, NT, TOPK]) for n in ("gather", "spread", "spread_t"))
        tokens, hidden, result = sb("tokens", [P, TOPK]), sb("hidden", [P, FC, TOPK]), sb("result", [TOPK, P])
        gathered, turned, up, down = pb("gathered"), pb("turned"), pb("up"), pb("down")
        sums = [pb(f"sums{b}") for b in range(B)]
        s_w = [sem("w0"), sem("w1")]
        (s_gather, s_spread, s_gathered, s_tokens, s_turned, s_taken, s_up, s_gelu, s_down, s_result, s_sums) = (
            sem(n) for n in ("gather", "spread", "gathered", "tokens", "turned", "taken", "up", "gelu", "down", "result",
                             "sums"))
        block = ctx.enter_context(nc.Block())

        def expert_pairs(eng, turn):
            turn(0)
            with eng.Fori(1, E // 2 - 1) as pair:
                turn(pair)
            turn(E // 2 - 1)

        def units(pair):
            return [((pair * 2 + k) * B + b, pair * 2 + k, k, b) for k in range(2) for b in range(B)]

        def is_unit(i, n):
            return isinstance(i, int) and i == n

        last_unit = E * B - 1

        @block.sync
        def _(sp):
            def turn(pair):
                for k in range(2):
                    e = pair * 2 + k
                    wait_positive(sp, s_down, (e - 1) * B)
                    sp.dma_start(w1_sb[:, k, :], w1[bass.ds(e, 1), :, :].rearrange("a p n -> (a p) n")).then_inc(s_w[k], 16)
                    sp.dma_start(w2_sb[:, k, :, :], w2[bass.ds(e, 1), :, :, :].rearrange("a p f n -> (a p) f n"))\
                      .then_inc(s_w[k], 16)

            expert_pairs(sp, turn)

        @block.tensor
        def _(pe):
            def second_product(i, k):
                wait_positive(pe, s_gelu, i + 1)
                wait_positive(pe, s_result, i)
                for f in range(FC):
                    last = pe.matmul(down[:, 0:P], hidden[:, f, :], w2_sb[:, k, f, :], start=f == 0, stop=f == FC - 1)
                last.then_inc(s_down, 1)

            def spread_result(i, b, first, final):
                wait_positive(pe, s_taken, i + 1)
                wait_positive(pe, s_result, i + 1)
                for j in range(NT):
                    last = pe.matmul(sums[b][:, j * P:(j + 1) * P], spread_t[:, b % 2, j, :], result[:],
                                     start=first and j == 0, stop=final, skip_group_check=True)
                last.then_inc(s_sums, 1)

            def turn(pair):
                for i, e, k, b in units(pair):
                    before = i - 1, (k if b else 1 - k), (b - 1) % B
                    wait_positive(pe, s_gather, i + 1)
                    wait_positive(pe, s_tokens, i)
                    for j in range(NT):
                        last = pe.matmul(gathered[:, 0:TOPK], h_rows[:, b * NT + j, :], gather[:, b % 2, j, :],
                                         start=j == 0, stop=j == NT - 1)
                    last.then_inc(s_gathered, 1)
                    wait_positive(pe, s_spread, i + 1)
                    wait_positive(pe, s_taken, i)
                    for j in range(NT):
                        last = pe.transpose(turned[:, j * P:(j + 1) * P], spread[:, b % 2, j, :], ident)
                    last.then_inc(s_turned, 1)
                    if not is_unit(i, 0):
                        second_product(before[0], before[1])
                    wait_positive(pe, s_w[k], pair * 32 + 32)
                    wait_positive(pe, s_tokens, i + 1)
                    for f in range(FC):
                        last = pe.matmul(up[:, f * P:(f + 1) * P], w1_sb[:, k, f * P:(f + 1) * P], tokens[:], start=True,
                                         stop=True)
                    last.then_inc(s_up, 1)
                    if not is_unit(i, 0):
                        spread_result(before[0], before[2], isinstance(i, int) and i <= B,
                                      isinstance(i, int) and i > last_unit + 1 - B)

            expert_pairs(pe, turn)
            second_product(last_unit, 1)
            spread_result(last_unit, B - 1, False, True)

        @block.scalar
        def _(act):
            def turn(pair):
                for i, e, k, b in units(pair):
                    wait_positive(act, s_turned, i + 1)
                    act.activation(spread_t[:, b % 2, :, :], turned[:].rearrange("p (t k) -> p t k", k=P), ACT.Copy)\
                       .then_inc(s_taken, 1)
                    wait_positive(act, s_up, i + 1)
                    act.activation(hidden[:], up[:].rearrange("p (f k) -> p f k", k=P), ACT.Gelu).then_inc(s_gelu, 1)

            expert_pairs(act, turn)

        @block.vector
        def _(dve):
            def make_gather(i, e, b):
                wait_positive(dve, s_gathered, i - 1)
                for j in range(NT):
                    last = dve.tensor_scalar(gather[:, b % 2, j, :], numbers, rank[:, bass.ds((j * B + b) * E + e, 1)],
                                             None, ALU.is_equal)
                last.then_inc(s_gather, 1)

            def make_spread(i, e, b):
                wait_positive(dve, s_turned, i - 1)
                for j in range(NT):
                    last = dve.tensor_scalar(spread[:, b % 2, j, :], numbers, rank[:, bass.ds((j * B + b) * E + e, 1)],
                                             gates[:, bass.ds((b * NT + j) * E + e, 1)], ALU.is_equal, ALU.mult)
                last.then_inc(s_spread, 1)

            def take_result(i):
                wait_positive(dve, s_down, i + 1)
                dve.tensor_copy(result[:], down[:, 0:P]).then_inc(s_result, 1)

            def turn(pair):
                for i, e, k, b in units(pair):
                    following = i + 1, (e if b + 1 < B else e + 1), (b + 1) % B
                    wait_positive(dve, s_gathered, i + 1)
                    dve.tensor_copy(tokens[:], gathered[:, 0:TOPK]).then_inc(s_tokens, 1)
                    if not is_unit(i, last_unit):
                        make_gather(*following)
                    if not is_unit(i, 0):
                        take_result(i - 1)
                    if not is_unit(i, last_unit):
                        make_spread(*following)

            make_gather(0, 0, 0)
            make_spread(0, 0, 0)
            expert_pairs(dve, turn)
            take_result(last_unit)
            wait_positive(dve, s_sums, E * B)
            for b in range(B):
                rows = acc[:, b * NT:(b + 1) * NT, :]
                dve.tensor_tensor(rows, rows, sums[b][:].rearrange("p (t d) -> p t d", d=P), ALU.add)


def gating(nc, name, h_cols, gates, gw, gb_rows, ident, acc=None, b2=None, rank=None, up_to=None,
           ones=None):
    NTT = B * NT
    with ExitStack() as ctx:
        def sb(n, shape):
            return ctx.enter_context(nc.sbuf_tensor(f"{name}_{n}", shape, F32))

        def pb(n):
            return ctx.enter_context(nc.psum_tensor(f"{name}_{n}", [P, S], F32))

        def sem(n):
            return ctx.enter_context(nc.semaphore(f"{name}_{n}"))

        logits, shifted = sb("logits", [P, NTT, E]), sb("shifted", [P, NTT, E])
        expd = sb("expd", [P, NTT, E])
        top, total, rtotal = sb("top", [P, NTT]), sb("total", [P, NTT]), sb("rtotal", [P, NTT])
        lg = pb("lg")
        tp = [pb(f"tp{i}") for i in range(4)]
        s_lg, s_step, s_exp, s_g, s_tp, s_ev, s_mm = (sem(n) for n in ("lg", "step", "exp", "g", "tp", "ev", "mm"))
        g3 = gates.rearrange("p (t e) -> p t e", e=E)
        if b2 is not None:
            gates_t = sb("gates_t", [E, NTT * P])
        else:
            ranked = [sb(f"ranked{i}", [B * E, S]) for i in range(2)]
            s_kept, s_rank = sem("kept"), sem("rank")
            kept_rows = sb("kept_rows", [P, NTT * E])
            kept, top8 = sb("kept", [B * E, S]), sb("top8", [B * E, 8])
        block = ctx.enter_context(nc.Block())

        @block.tensor
        def _(pe):
            for i in range(NTT):
                last = pe.matmul(lg[:, i * E:(i + 1) * E], h_cols[:, i * P:(i + 1) * P], gw, start=True, stop=True)
            last.then_inc(s_lg, 1)
            pe.wait_ge(s_g, 1)
            if b2 is not None:
                for i in range(NTT):
                    last = pe.transpose(tp[i // NT][0:E, i % NT * P:(i % NT + 1) * P], gates[:, i * E:(i + 1) * E],
                                        ident)
                last.then_inc(s_tp, 1)
                pe.wait_ge(s_ev, 1)
                for i in range(NTT):
                    last = pe.matmul(tp[i // NT][:, i % NT * P:(i % NT + 1) * P], gates_t[:, i * P:(i + 1) * P], b2,
                                     start=True, stop=True)
                last.then_inc(s_mm, 1)
            else:
                for j in range(NT):
                    last = pe.transpose(tp[0][0:B * E, j * P:(j + 1) * P], shifted[:, j * B:(j + 1) * B, :]
                                        .rearrange("p t e -> p (t e)"), ident)
                last.then_inc(s_tp, 1)
                pe.wait_ge(s_ev, 1)
                for j in range(NT):
                    last = pe.transpose(tp[1][:, j * B * E:(j + 1) * B * E], kept[:, j * P:(j + 1) * P],
                                        ident[0:B * E, 0:B * E])
                last.then_inc(s_mm, 1)
                pe.wait_ge(s_kept, 1)
                w = B * E
                for j in range(NT):
                    for i in range(j + 1):
                        last = pe.matmul(tp[2][:, j * w:(j + 1) * w], up_to if i == j else ones,
                                         kept_rows[:, i * w:(i + 1) * w], start=i == 0, stop=i == j)
                last.then_inc(s_rank, 1)

        @block.scalar
        def _(act):
            act.wait_ge(s_step, 3)
            act.activation(expd[:], shifted[:], ACT.Exp).then_inc(s_exp, 1)

        @block.vector
        def _(dve):
            done = 0

            def mine(instruction):
                nonlocal done
                done += 1
                instruction.then_inc(s_step, 1)
                dve.wait_ge(s_step, done)

            dve.wait_ge(s_lg, 1)
            raw = lg[:, 0:NTT * E].rearrange("p (t e) -> p t e", e=E)
            if gb_rows is not None:
                bias = gb_rows.rearrange("p (a e) -> p a e", a=1).broadcast_to([P, NTT, E])
                mine(dve.tensor_tensor(logits[:], raw, bias, ALU.add))
            else:
                mine(dve.tensor_copy(logits[:], raw))
            mine(dve.tensor_reduce(top[:], logits[:], axis=AX.X, op=ALU.max))

            def spread(x):
                return x.rearrange("p (t a) -> p t a", a=1).broadcast_to([P, NTT, E])

            mine(dve.tensor_tensor(shifted[:], logits[:], spread(top[:]), ALU.subtract))
            dve.wait_ge(s_exp, 1)
            mine(dve.tensor_reduce(total[:], expd[:], axis=AX.X, op=ALU.add))
            mine(dve.reciprocal(rtotal[:], total[:]))
            if b2 is not None:
                dve.tensor_tensor(g3, expd[:], spread(rtotal[:]), ALU.mult).then_inc(s_g, 1)
                dve.wait_ge(s_tp, 1)
                for b in range(B):
                    last = dve.tensor_copy(gates_t[:, b * S:(b + 1) * S], tp[b][0:E, :])
                last.then_inc(s_ev, 1)
                dve.wait_ge(s_mm, 1)
                for b in range(B):
                    dve.tensor_copy(acc[:, b * NT:(b + 1) * NT, :], tp[b][:].rearrange("p (t d) -> p t d", d=P))
            else:
                mine(dve.tensor_tensor(g3, expd[:], spread(rtotal[:]), ALU.mult))
                dve.tensor_copy(shifted[:].rearrange("p (j b) e -> p b j e", b=B),
                                g3.rearrange("p (b j) e -> p b j e", b=B)).then_inc(s_g, 1)
                dve.wait_ge(s_tp, 1)
                mine(dve.tensor_copy(ranked[0][:], tp[0][0:B * E, :]))
                for r in range(TOPK // 8):
                    mine(dve.max(top8[:], ranked[r % 2][:]))
                    mine(dve.match_replace(ranked[(r + 1) % 2][:], top8[:], ranked[r % 2][:], -1.0))
                dve.tensor_scalar(kept[:], ranked[TOPK // 8 % 2][:], 0.0, None, ALU.is_lt).then_inc(s_ev, 1)
                dve.wait_ge(s_mm, 1)
                dve.tensor_copy(kept_rows[:], tp[1][:, 0:NTT * E]).then_inc(s_kept, 1)
                dve.wait_ge(s_rank, 1)
                dve.tensor_tensor(rank, tp[2][:, 0:NTT * E], kept_rows[:], ALU.mult)


def recurrence_tables(nc, name, ctx_t, ctx_k, w_t, k_ctx, bias_rows, is_key, score_w, gate_w):
    with ExitStack() as ctx:
        s_mm = ctx.enter_context(nc.semaphore(f"{name}_mm"))
        ps = [ctx.enter_context(nc.psum_tensor(f"{name}_ps{i}", [P, BANK], F32)) for i in range(4)]
        block = ctx.enter_context(nc.Block())

        @block.tensor
        def _(pe):
            pe.matmul(ps[0][:, 0:B * CPAD], w_t, ctx_t, start=True, stop=True).then_inc(s_mm, 1)
            for k in range(3):
                pe.matmul(ps[1 + k][:, 0:3 * P], ctx_k[:, k * P:(k + 1) * P], k_ctx, start=True, stop=True)\
                  .then_inc(s_mm, 1)

        @block.vector
        def _(dve):
            dve.wait_ge(s_mm, 1)
            dve.tensor_copy(score_w, ps[0][:, 0:B * CPAD])
            for k in range(3):
                dve.wait_ge(s_mm, 2 + k)
                dve.scalar_tensor_tensor(out=gate_w[:, k, :], in0=bias_rows, scalar=is_key[:, k:k + 1],
                                         in1=ps[1 + k][:, 0:3 * P], op0=ALU.mult, op1=ALU.add)


def recurrence(nc, x_t, score_w, gate_w, r_w, x_w, mask_l, mask_r, spread, h0_t, h0_c, history):
    with ExitStack() as ctx:
        def sb(n, w, rows=P):
            return ctx.enter_context(nc.sbuf_tensor(f"gru_{n}", [rows, w], F32))

        def pb(n):
            return ctx.enter_context(nc.psum_tensor(f"gru_{n}", [P, BANK], F32))

        def sem(n):
            return ctx.enter_context(nc.semaphore(f"gru_{n}"))

        new_t, old_t = sb("new_t", 32), sb("old_t", 32)
        h, xs = sb("h", 32), sb("xs", B)
        p, p_t = sb("p", CPAD), sb("p_t", CPAD)
        negmax, total, rtotal = sb("negmax", 1), sb("total", 2), sb("rtotal", 1)
        own = sb("own", 4 * 32)
        pre_r, pre_z, th_r, th_z, one_z = (sb(n, 32) for n in ("pre_r", "pre_z", "th_r", "th_z", "one_z"))
        pre_c, r_hh, c_in, cand = sb("pre_c", 32), sb("r_hh", 32), sb("c_in", 32), sb("cand", 32)
        h_half, z_h, new = sb("h_half", 32), sb("z_h", 32), sb("new", 32)
        ps_s, ps_own, ps_g, ps_c, ps_t = (pb(n) for n in ("ps_s", "ps_own", "ps_g", "ps_c", "ps_t"))
        (s_init, s_load, s_table, s_score, s_x, s_ownmm, s_total, s_rzmm, s_cmm, s_max, s_exp, s_pt, s_rt, s_own,
         s_xs, s_prer, s_thr, s_prec, s_rhh, s_cin, s_cand, s_prez, s_thz, s_hhalf, s_zh, s_onez, s_new, s_h, s_old, s_newt,
         s_hist) = (
            sem(n) for n in ("init", "load", "table", "score", "x", "ownmm", "total", "rzmm", "cmm", "max", "exp",
                             "pt", "rt", "own", "xs", "prer", "thr", "prec", "rhh", "cin", "cand", "prez", "thz", "hhalf",
                             "zh", "onez", "new", "h", "old", "newt", "hist"))
        block = ctx.enter_context(nc.Block())
        U = STEPS_PER_TURN

        @block.sync
        def _(sp):
            sp.dma_start(new_t[:, 0:B], h0_t).then_inc(s_load, 16)
            sp.dma_start(h[:], h0_c).then_inc(s_load, 16)

        @block.gpsimd
        def _(pool):
            pool.sem_inc(s_hist, 1)
            pool.tensor_copy(xs[:], x_t[:, 0:B]).then_inc(s_xs, 1)
            with pool.Fori(0, S // U) as turn:
                for k in range(U):
                    t = turn * U + k
                    pool.wait_ge(s_x, t + 1)
                    pool.tensor_copy(xs[:], x_t[:, bass.ds((t + 1) * B, B)]).then_inc(s_xs, 1)
                    pool.wait_ge(s_newt, t + 2)
                    pool.tensor_tensor(history[:, bass.ds(t * B, B)], new_t[:, 0:B], old_t[:, 0:B], ALU.add)\
                        .then_inc(s_hist, 1)

        @block.tensor
        def _(pe):
            def state_scores(half, final):
                for b in range(B):
                    last = pe.matmul(ps_s[32 * b:32 * b + B, 0:CTX + 1], half[:, 0:B], score_w[:, b, 0:CTX + 1],
                                     start=False, stop=final, tile_position=(0, 32 * b))
                return last

            def state_gates(half, final):
                for c in range(4):
                    last = pe.matmul(ps_own[32 * c:32 * c + B, 0:96], half[:, 0:B], r_w[:, c, :], start=False,
                                     stop=final, tile_position=(0, 32 * c))
                return last

            pe.wait_ge(s_init, 7)
            pe.wait_ge(s_load, 32)
            with pe.Fori(0, S // U) as turn:
                for k in range(U):
                    t = turn * U + k
                    pe.wait_ge(s_xs, t + 1)
                    pe.wait_ge(s_own, t + 1)
                    pe.matmul(ps_s[:, 0:CTX + 1], mask_l, mask_r[:, 0:CTX + 1], start=True, stop=False)
                    for c in range(4):
                        last = pe.matmul(ps_own[32 * c:32 * c + B, 0:P], xs[:], x_w[:, c, :], start=True, stop=False,
                                         tile_position=(0, 32 * c))
                    last.then_inc(s_x, 1)
                    pe.wait_ge(s_old, t + 1)
                    state_scores(old_t, False)
                    pe.wait_ge(s_newt, t + 1)
                    state_scores(new_t, True).then_inc(s_score, 1)
                    state_gates(old_t, False)
                    state_gates(new_t, True).then_inc(s_ownmm, 1)
                    pe.wait_ge(s_exp, t + 1)
                    for c in range(4):
                        last = pe.matmul(ps_t[32 * c:32 * c + B, 0:2], spread, total[:], start=True, stop=True,
                                         tile_position=(0, 32 * c))
                    last.then_inc(s_total, 1)
                    pe.wait_ge(s_pt, t + 1)
                    for lo, hi, bank, done in ((0, 64, ps_g, s_rzmm), (64, 96, ps_c, s_cmm)):
                        for k3 in range(3):
                            for c in range(4):
                                last = pe.matmul(bank[32 * c:32 * c + B, 0:hi - lo], p_t[:, 32 * k3:32 * k3 + B],
                                                 gate_w[:, k3, 96 * c + lo:96 * c + hi], start=k3 == 0, stop=k3 == 2,
                                                 tile_position=(0, 32 * c))
                        last.then_inc(done, 1)

        @block.scalar
        def _(act):
            act.wait_ge(s_load, 32)
            act.wait_ge(s_init, 7)
            act.activation(cand[:], h[:], ACT.Exp).then_inc(s_table, 1)
            act.wait_ge(s_table, 1)
            with act.Fori(0, S // U) as turn:
                for k in range(U):
                    t = turn * U + k
                    act.wait_ge(s_max, t + 1)
                    act.activation(p[:, 0:CTX + 1], ps_s[:, 0:CTX + 1], ACT.Exp, bias=negmax[:, 0:1], accum_out=total[:, 0:1])\
                       .then_inc(s_exp, 1)
                    act.wait_ge(s_prer, t + 1)
                    act.activation(th_r[:], pre_r[:], ACT.Tanh, scale=0.5).then_inc(s_thr, 1)
                    act.wait_ge(s_prez, t + 1)
                    act.activation(th_z[:], pre_z[:], ACT.Tanh, scale=0.5).then_inc(s_thz, 1)
                    act.wait_ge(s_cin, t + 1)
                    act.activation(cand[:], c_in[:], ACT.Tanh).then_inc(s_cand, 1)

        @block.vector
        def _(dve):
            dve.sem_inc(s_own, 1)
            dve.sem_inc(s_old, 1)
            dve.sem_inc(s_newt, 1)
            dve.memset(old_t[:], 0.0).then_inc(s_init, 1)
            dve.memset(ps_g[:], 0.0).then_inc(s_init, 1)
            dve.memset(ps_c[:], 0.0).then_inc(s_init, 1)
            dve.memset(ps_own[:], 0.0).then_inc(s_init, 1)
            dve.memset(ps_t[:], 1.0).then_inc(s_init, 1)
            dve.memset(total[:], 1.0).then_inc(s_init, 1)
            dve.memset(p[:], 0.0).then_inc(s_init, 1)
            dve.wait_ge(s_load, 32)
            dve.tensor_scalar(h_half[:], h[:], 0.5, None, ALU.mult).then_inc(s_hhalf, 1)
            with dve.Fori(0, S // U) as turn:
                for k in range(U):
                    t = turn * U + k
                    dve.wait_ge(s_score, t + 1)
                    dve.tensor_reduce(negmax[:], ps_s[:, 0:CTX + 1], axis=AX.X, op=ALU.max, negate=True).then_inc(s_max, 1)
                    dve.wait_ge(s_exp, t + 1)
                    dve.transpose(p_t[:], p[:]).then_inc(s_pt, 1)
                    dve.wait_ge(s_ownmm, t + 1)
                    dve.tensor_copy(own[:], ps_own[:, 0:P]).then_inc(s_own, 1)
                    dve.wait_ge(s_total, t + 1)
                    dve.reciprocal(rtotal[:], ps_t[:, 0:1]).then_inc(s_rt, 1)
                    dve.wait_ge(s_rzmm, t + 1)
                    dve.wait_ge(s_rt, t + 1)
                    dve.scalar_tensor_tensor(out=pre_r[:], in0=ps_g[:, 0:32], scalar=rtotal[:, 0:1], in1=own[:, 32:64],
                                             op0=ALU.mult, op1=ALU.add).then_inc(s_prer, 1)
                    dve.scalar_tensor_tensor(out=pre_z[:], in0=ps_g[:, 32:64], scalar=rtotal[:, 0:1], in1=own[:, 64:96],
                                             op0=ALU.mult, op1=ALU.add).then_inc(s_prez, 1)
                    dve.wait_ge(s_cmm, t + 1)
                    dve.scalar_tensor_tensor(out=pre_c[:], in0=ps_c[:, 0:32], scalar=rtotal[:, 0:1], in1=own[:, 96:P],
                                             op0=ALU.mult, op1=ALU.add).then_inc(s_prec, 1)
                    dve.wait_ge(s_thr, t + 1)
                    dve.scalar_tensor_tensor(out=r_hh[:], in0=th_r[:], scalar=1.0, in1=own[:, 0:32], op0=ALU.add,
                                             op1=ALU.mult).then_inc(s_rhh, 1)
                    dve.wait_ge(s_thz, t + 1)
                    dve.wait_ge(s_hhalf, t + 1)
                    dve.scalar_tensor_tensor(out=z_h[:], in0=th_z[:], scalar=1.0, in1=h_half[:], op0=ALU.add,
                                             op1=ALU.mult).then_inc(s_zh, 1)
                    dve.wait_ge(s_rhh, t + 1)
                    dve.scalar_tensor_tensor(out=c_in[:], in0=r_hh[:], scalar=0.5, in1=pre_c[:], op0=ALU.mult,
                                             op1=ALU.add).then_inc(s_cin, 1)
                    dve.tensor_scalar(one_z[:], th_z[:], -0.5, 0.5, ALU.mult, ALU.add).then_inc(s_onez, 1)
                    dve.wait_ge(s_hist, t + 1)
                    dve.wait_ge(s_zh, t + 1)
                    dve.transpose(old_t[:], z_h[:]).then_inc(s_old, 1)
                    dve.wait_ge(s_cand, t + 1)
                    dve.wait_ge(s_onez, t + 1)
                    dve.tensor_tensor(new[:], cand[:], one_z[:], ALU.mult).then_inc(s_new, 1)
                    dve.wait_ge(s_new, t + 1)
                    dve.transpose(new_t[:], new[:]).then_inc(s_newt, 1)
                    dve.tensor_tensor(h[:], new[:], z_h[:], ALU.add).then_inc(s_h, 1)
                    dve.wait_ge(s_h, t + 1)
                    dve.tensor_scalar(h_half[:], h[:], 0.5, None, ALU.mult).then_inc(s_hhalf, 1)


def add_history(nc, x, history, ident):
    with ExitStack() as ctx:
        s_tp = ctx.enter_context(nc.semaphore("hist_tp"))
        tp = [ctx.enter_context(nc.psum_tensor(f"hist_tp{b}", [P, S], F32)) for b in range(B)]
        block = ctx.enter_context(nc.Block())
        by_batch = history.rearrange("p (t b) -> p b t", b=B)

        @block.tensor
        def _(pe):
            for b in range(B):
                for j in range(NT):
                    last = pe.transpose(tp[b][:, j * P:(j + 1) * P], by_batch[:, b, j * P:(j + 1) * P], ident)
                last.then_inc(s_tp, 1)

        @block.vector
        def _(dve):
            for b in range(B):
                dve.wait_ge(s_tp, b + 1)
                rows = x[:, b * NT:(b + 1) * NT, :]
                dve.tensor_tensor(rows, rows, tp[b][:].rearrange("p (t d) -> p t d", d=P), ALU.add)


def condition_columns(nc, cond_t, norm_w, norm_b, columns):
    with ExitStack() as ctx:
        s_mm = ctx.enter_context(nc.semaphore("cond_mm"))
        ps = ctx.enter_context(nc.psum_tensor("cond_ps", [P, S], F32))
        block = ctx.enter_context(nc.Block())

        @block.tensor
        def _(pe):
            for i in range(6):
                last = pe.matmul(ps[:, i * B:(i + 1) * B], norm_w[:, i * P:(i + 1) * P], cond_t, start=True, stop=True)
            last.then_inc(s_mm, 1)

        @block.vector
        def _(dve):
            dve.wait_ge(s_mm, 1)
            for i in range(6):
                dve.tensor_scalar(columns[:, i * B:(i + 1) * B], ps[:, i * B:(i + 1) * B], norm_b[:, i:i + 1],
                                  1.0 if i % 2 == 0 else 0.0, ALU.add, ALU.add)


def program(nc, a, out):
    with ExitStack() as ctx:
        def sb(n, shape, dt=F32):
            return ctx.enter_context(nc.sbuf_tensor(n, shape, dt))

        ln = {n: Counted(ctx.enter_context(nc.semaphore(f"ln_{n}")))
              for n in ("stats", "aggr", "sqrt", "rstd", "xn", "turned", "gained", "biased")}
        s_in, s_late = ctx.enter_context(nc.semaphore("in")), ctx.enter_context(nc.semaphore("late"))
        s_out = ctx.enter_context(nc.semaphore("out"))
        x, y = sb("x", [P, B * NT, P]), sb("y", [P, B * NT, P])
        h_cols = sb("h_cols", [P, B * S])
        columns = sb("columns", [P, 6 * B])
        gates, rank = sb("gates", [P, B * NT * E]), sb("rank", [P, B * NT * E])
        early, late = sb("early", [P, sum(EARLY.values())]), sb("late", [P, sum(LATE.values())])
        c = {}
        for widths, t in ((EARLY, early), (LATE, late)):
            at = 0
            for n, w in widths.items():
                c[n] = t[:, at:at + w]
                at += w
        short = {n: sb(f"c_{n}", list(a[n].shape)) for n in ("b2", "mask_l", "mask_r")}
        c.update({n: t[:] for n, t in short.items()})
        narrow = {n: sb(f"b_{n}", [c[n].shape[0], c[n].shape[1]], BF16) for n in ("masks", "mask_l", "mask_r")}
        x_dram = a["x"].rearrange("(n p) d -> p n d", p=P)
        with nc.Block() as block:
            @block.sync
            def _(sp):
                sp.dma_start(x[:], x_dram).then_inc(s_in, 16)
                sp.dma_start(early[:], a["early"]).then_inc(s_in, 16)
                sp.dma_start(late[:], a["late"]).then_inc(s_late, 16)
                for n in short:
                    sp.dma_start(c[n], a[n]).then_inc(s_late, 16)
                sp.wait_ge(s_in, 32)
        ident, eps = c["ident"], c["eps"][:, 0:1]
        g_rows = c["g_rows"].rearrange("p (a d) -> p a d", a=1).broadcast_to([P, B * NT, P])
        b_rows = c["b_rows"].rearrange("p (a d) -> p a d", a=1).broadcast_to([P, B * NT, P])

        def columns_of(layer):
            return (lambda b: columns[:, bass.ds(b + (2 * layer) * B, 1)],
                    lambda b: columns[:, bass.ds(b + (2 * layer + 1) * B, 1)])

        def by_batch(b):
            return h_cols[:, bass.ds(b * S, S)]

        gain, bias = (lambda b: c["ln_cols"][:, 0:1]), (lambda b: c["ln_cols"][:, 1:2])
        one, zero = (lambda b: c["eps"][:, 2:3]), (lambda b: c["eps"][:, 3:4])

        layer_norm(nc, ln, "ln_a", x, eps, ident, rows_out=y)
        with nc.Block() as block:
            @block.vector
            def _(dve):
                dve.wait_ge(s_late, 16 * (1 + len(short)))
                for n, t in narrow.items():
                    dve.tensor_copy(t[:], c[n])
        c.update({n: t[:] for n, t in narrow.items()})
        masks = (c["masks"][:, 0:P], c["masks"][:, P:2 * P])
        condition_columns(nc, c["cond_t"], c["norm_w"], c["norm_b"], columns)
        scale, shift = columns_of(0)
        layer_norm(nc, ln, "ln_b", y, eps, ident, cols_out=by_batch, scale=scale, shift=shift)
        attention(nc, "self", h_cols, y, a["wqkv1"], a["wo1"], ident, out_bias=c["bo1_rows"], q_scale=HD ** -0.5)
        scale, shift = columns_of(1)
        layer_norm(nc, ln, "ln_c", y, eps, ident, cols_out=by_batch, scale=scale, shift=shift)
        context_attention(nc, "cross", h_cols, y, a["wqkv2"], a["wo2"], ident, c["ctx_t"], c["bo2_rows"], HD ** -0.5)
        scale, shift = columns_of(2)
        layer_norm(nc, ln, "ln_d", y, eps, ident, cols_out=by_batch, scale=scale, shift=shift)
        feed_forward(nc, h_cols, x, y, a["ff_w1"], a["ff_b1"], a["ff_w2"], c["ffb2_rows"])

        layer_norm(nc, ln, "ln_e", x, eps, ident, rows_out=y)
        layer_norm(nc, ln, "ln_f", y, eps, ident, cols_out=by_batch, scale=gain, shift=bias)
        attention(nc, "causal", h_cols, y, a["wqkv3"], a["wo3"], ident, masks=masks,
                  norm=(c["ones_half"], (c["qk_gain"][:, 0:NP], c["qk_gain"][:, NP:2 * NP]),
                        (c["eps"][:, 4:5], c["eps"][:, 1:2])), q_scale=QK_SCALE)
        layer_norm(nc, ln, "ln_g", y, eps, ident, cols_out=by_batch, scale=gain, shift=bias)
        gating(nc, "moe_gate", h_cols, gates[:], c["gate_w"], c["gate_b_rows"], ident, acc=y, b2=c["b2"])
        experts(nc, "moe", h_cols, y, gates[:], a["moe_w1"], a["moe_b1"], a["moe_w2"], ACT.Gelu_apprx_tanh)
        layer_norm(nc, ln, "ln_h", y, eps, ident, rows_out=x, add_to=x, gain_rows=g_rows, bias_rows=b_rows)

        with ExitStack() as own:
            x_t = own.enter_context(nc.sbuf_tensor("x_t", [P, (S + 1) * B], F32))
            score_w = own.enter_context(nc.sbuf_tensor("score_w", [P, B, CPAD], F32))
            gate_w = own.enter_context(nc.sbuf_tensor("ctx_gate_w", [P, 3, 3 * P], F32))
            with nc.Block() as block:
                @block.vector
                def _(dve):
                    dve.memset(x_t[:, S * B:(S + 1) * B], 0.0)
            x_by_batch = x_t[:, 0:S * B].rearrange("p (t b) -> p b t", b=B)
            layer_norm(nc, ln, "ln_i", x, eps, ident, scale=one, shift=zero,
                       cols_out=lambda b: x_by_batch[:, bass.ds(b, 1), :].rearrange("p a t -> p (a t)"))
            recurrence_tables(nc, "tables", c["ctx_t"], c["ctx_k"], c["w_t"], c["k_ctx"],
                              c["bias_rows"], c["is_key"], score_w[:].rearrange("p b s -> p (b s)"), gate_w)
            recurrence(nc, x_t, score_w, gate_w, c["r_w"].rearrange("p (c g) -> p c g", c=4),
                       c["x_w"].rearrange("p (c g) -> p c g", c=4), c["mask_l"], c["mask_r"], c["spread"], a["cond_t"],
                       a["h0_c"], h_cols)
        add_history(nc, x, h_cols[:], ident)

        layer_norm(nc, ln, "ln_j", x, eps, ident, rows_out=y, cols_out=by_batch, scale=one, shift=zero)
        gating(nc, "pick", h_cols, gates[:], c["gw2"], None, ident, rank=rank[:], up_to=c["up_to"], ones=c["ones"])
        picked_experts(nc, "picked", y, x, gates[:], rank[:], c["numbers"], ident, a["ec_w1"], a["ec_w2"])
        with nc.Block() as block:
            @block.sync
            def _(sp):
                sp.dma_start(out.rearrange("(n p) d -> p n d", p=P), x[:]).then_inc(s_out, 16)
                sp.wait_ge(s_out, 16)


def laid_out(np, i):
    f = {k: np.ascontiguousarray(v) for k, v in i.items()}
    x0 = "L0_xcond_"

    def pairs(q, k, v):
        return np.stack([w.reshape(P, NP, P).transpose(1, 0, 2) for w in (q, k, v)], 2)

    def chunks(w, order):
        w = w.reshape(w.shape[:-1] + (3, 4, 32))[..., order, :, :]
        return np.moveaxis(w, -3, -2).reshape(w.shape[:-3] + (4, 96))

    a = {"x": f["x"].reshape(B * S, P), "cond_t": f["cond_1024"].T}
    a["norm_w"] = np.concatenate([f[f"{x0}norm{n}_w"] for n in (1, 2, 3)], 1)
    a["norm_b"] = np.concatenate([f[f"{x0}norm{n}_b"].reshape(2, P).T for n in (1, 2, 3)], 1)
    for n, w in ((1, "attn1"), (2, "attn2")):
        a[f"wqkv{n}"] = pairs(f[f"{x0}{w}_wq"], f[f"{x0}{w}_wk"], f[f"{x0}{w}_wv"])
        a[f"wo{n}"] = f[f"{x0}{w}_wo"].reshape(NP, P, P)
        a[f"bo{n}_rows"] = np.broadcast_to(f[f"{x0}{w}_bo"], (P, P))
    a["wqkv3"] = pairs(f["L0_ffn_Wq"], f["L0_ffn_Wk"], f["L0_ffn_Wv"])
    a["wo3"] = f["L0_ffn_Wo"].reshape(NP, P, P)
    a["ff_w1"], a["ff_b1"] = f[x0 + "ff_w1"], f[x0 + "ff_b1"].reshape(2 * FC, P).T
    a["ff_w2"] = f[x0 + "ff_w2"].reshape(FC, P, P).transpose(1, 0, 2)
    a["ffb2_rows"] = np.broadcast_to(f[x0 + "ff_b2"], (P, P))
    a["ln_cols"] = np.stack([f["L0_ffn_ln_g"], f["L0_ffn_ln_b"]], 1)
    a["g_rows"] = np.broadcast_to(f["L0_ffn_ln_g"], (P, P))
    a["b_rows"] = np.broadcast_to(f["L0_ffn_ln_b"], (P, P))
    a["qk_gain"] = np.concatenate([f[f"L0_ffn_{n}_scale"].reshape(NP, P).T for n in "qk"], 1)
    a["gate_w"], a["gate_b_rows"] = f["L0_ffn_gate_w"], np.broadcast_to(f["L0_ffn_gate_b"], (P, E))
    a["moe_w1"], a["moe_b1"] = f["L0_ffn_w1"], f["L0_ffn_b1"].reshape(E, FC, P).transpose(0, 2, 1)
    a["moe_w2"], a["b2"] = f["L0_ffn_w2"].reshape(E, FC, P, P).transpose(0, 2, 1, 3), f["L0_ffn_b2"]
    ctx_t = np.zeros((P, B, CPAD), np.float32)
    ctx_t[:, :, :CTX] = f["ctx_1024"].transpose(2, 0, 1)
    a["ctx_t"] = ctx_t.reshape(P, B * CPAD)
    a["ctx_k"] = ctx_t.reshape(P, B, 3, 32).transpose(0, 2, 1, 3).reshape(P, 3 * P)
    a["w_t"] = f["L1_xcond_W"].T
    a["k_ctx"] = chunks(f["L1_xcond_kernel"][P:], [1, 0, 2]).reshape(P, 3 * P)
    x_w = np.zeros((P, 4, P), np.float32)
    x_w[:, :, 32:] = chunks(f["L1_xcond_kernel"][:P], [1, 0, 2])
    a["x_w"] = x_w.reshape(P, 4 * P)
    a["r_w"] = chunks(f["L1_xcond_recurrent_kernel"], [2, 1, 0]).reshape(P, 3 * P)
    a["bias_rows"] = np.broadcast_to(chunks(f["L1_xcond_bias"], [1, 0, 2]).reshape(3 * P), (P, 3 * P))
    h0 = np.zeros((4, 32, 32), np.float32)
    h0[:, :B] = f["cond_1024"].reshape(B, 4, 32).transpose(1, 0, 2)
    a["h0_c"] = h0.reshape(P, 32)
    a["gw2"] = f["L1_ffn_gate_w"].T
    a["ec_w1"], a["ec_w2"] = f["L1_ffn_w1"], f["L1_ffn_w2"].reshape(E, FC, P, P).transpose(0, 2, 1, 3)
    a["ident"] = np.eye(P, dtype=np.float32)
    a["up_to"], a["ones"] = np.triu(np.ones((P, P), np.float32)), np.ones((P, P), np.float32)
    a["numbers"] = np.broadcast_to(np.arange(1, TOPK + 1).astype(np.float32), (P, TOPK))
    a["eps"] = np.broadcast_to(np.array([EPS, EPS_L2, 1.0, 0.0, EPS_L2 / QK_SCALE ** 2], np.float32), (P, 5))
    a["ones_half"] = np.kron(np.eye(2, dtype=np.float32), np.ones((HD, HD), np.float32))
    a["masks"] = np.concatenate([np.eye(P), np.triu(np.full((P, P), -1e30), 1)], 1).astype(np.float32)
    group, row = np.arange(P) // 32, np.arange(P) % 32
    used = row == group
    a["mask_l"] = np.stack([~used, used]).astype(np.float32)
    mask_r = np.zeros((2, CPAD))
    mask_r[0, :CTX], mask_r[0, CTX + 1:], mask_r[1, CTX:] = -1e30, -1e30, -1e30
    a["mask_r"] = mask_r.astype(np.float32)
    a["is_key"] = (32 * np.arange(3)[None, :] + row[:, None] < CTX).astype(np.float32)
    a["spread"] = (np.arange(P)[:, None] == 33 * np.arange(B)[None, :]).astype(np.float32)
    cond = a["cond_t"]
    for name, widths in (("early", EARLY), ("late", LATE)):
        a[name] = np.concatenate([a.pop(n) for n in widths], 1)
    a["cond_t"] = cond
    return {k: np.ascontiguousarray(v) for k, v in a.items()}


def kernel(**inputs):
    import numpy as np
    from concourse import bacc
    from concourse.bass_utils import run_bass_kernel_spmd

    arrays = laid_out(np, inputs)
    nc = bacc.Bacc("TRN2", target_bir_lowering=False, num_devices=1)
    a = {n: nc.dram_tensor(f"in_{n}", v.shape, mybir.dt.from_np(v.dtype), kind="ExternalInput").ap()
         for n, v in arrays.items()}
    out = nc.dram_tensor("out", (B * S, P), F32, kind="ExternalOutput").ap()
    program(nc, a, out)
    r = run_bass_kernel_spmd(nc, [{f"in_{n}": v for n, v in arrays.items()}], core_ids=[0])
    return r.results[0]["out"].reshape(B, S, P)
```
